# Optimizing a Trainium2 kernel written in Bass

```python
import numpy as np
import jax
import jax.numpy as jnp

def _softmax(x, axis=-1):
    return jax.nn.softmax(x, axis=axis)

def _gelu(x):
    return jax.nn.gelu(x, approximate=True)

def _silu(x):
    return jax.nn.silu(x)

def _sigmoid(x):
    return jax.nn.sigmoid(x)

def _layernorm(x, axis=-1, eps=1e-05):
    m = jnp.mean(x, axis=axis, keepdims=True)
    v = jnp.var(x, axis=axis, keepdims=True)
    return (x - m) / jnp.sqrt(v + eps)

def _scatter_add(tgt, idx, src, axis=0):
    return tgt.at[idx].add(src)

def _segment_sum(src, seg, n):
    return jax.ops.segment_sum(src, seg, n)
kernel_name = 'mk_gnn_resnorm_d4_gnn_r64_561b9c'

def setup_inputs(seed: int=0):
    np.random.seed(seed)
    _w = jnp.asarray

    def _rec_inputs():
        import jax
        import jax.numpy as jnp
        _gk = jax.random.key(seed)
        x = -0.0009044 + 1 * jax.random.normal(jax.random.fold_in(_gk, 1), (100000, 160), jnp.float32)
        src = jax.random.randint(jax.random.fold_in(_gk, 2), (25000,), 0, 100000, jnp.int32)
        dst = jax.random.randint(jax.random.fold_in(_gk, 3), (25000,), 0, 100000, jnp.int32)
        _o = jnp.argsort(dst, stable=True)
        src = src[_o]
        dst = dst[_o]
        edge_attr_10 = jax.random.uniform(jax.random.fold_in(_gk, 12), (25000, 10), jnp.float32, 0.0, 1)
        edge_attr_16 = -0.000191324 + 0.999809 * jax.random.normal(jax.random.fold_in(_gk, 13), (25000, 16), jnp.float32)
        edge_attr_3 = 0.00262751 + 0.999568 * jax.random.normal(jax.random.fold_in(_gk, 14), (25000, 3), jnp.float32)
        edge_attr_4 = -0.000149047 + 1.00006 * jax.random.normal(jax.random.fold_in(_gk, 15), (25000, 4), jnp.float32)
        edge_attr_64 = jax.random.uniform(jax.random.fold_in(_gk, 16), (25000, 64), jnp.float32, 0.0, 1)
        edge_attr_8 = 0.000735704 + 1.0001 * jax.random.normal(jax.random.fold_in(_gk, 17), (25000, 8), jnp.float32)
        node_vec1 = jax.random.uniform(jax.random.fold_in(_gk, 18), (100000, 1), jnp.float32, 0.0, 1)
        return (x, src, dst, edge_attr_10, edge_attr_16, edge_attr_3, edge_attr_4, edge_attr_64, edge_attr_8, node_vec1)
    x, src, dst, edge_attr_10, edge_attr_16, edge_attr_3, edge_attr_4, edge_attr_64, edge_attr_8, node_vec1 = _rec_inputs()

    def _L0_gnn_setup():
        import jax, jax.numpy as jnp
        import numpy as np
        N_NODES = 10000
        N_EDGES = 5000
        NUM_NEIGHBORS = 32.0
        INV_SQRT3 = 1.0 / np.sqrt(3.0)

        def _fctp_scalar_attr(xs, xv, Ws, Wv, a):
            out_s = xs @ Ws * (a / np.sqrt(xs.shape[1]))[:, None]
            out_v = jnp.einsum('nuc,uw->nwc', xv, Wv) * (a / np.sqrt(xv.shape[1]))[:, None, None]
            return (out_s, out_v)
        key = jax.random.key(seed)
        ks = jax.random.split(key, 16)
        f32 = jnp.float32
        return {'node_input': jax.random.normal(ks[0], (N_NODES, 160), f32), 'node_attr': jnp.ones((N_NODES, 1), f32), 'edge_attr': jax.random.normal(ks[1], (N_EDGES, 4), f32), 'edge_scalar_attr': jax.random.normal(ks[2], (N_EDGES, 8), f32), 'Wsc0': jax.random.normal(ks[3], (64, 64), f32), 'Wsc1': jax.random.normal(ks[4], (32, 32), f32), 'Wl1_0': jax.random.normal(ks[5], (64, 64), f32), 'Wl1_1': jax.random.normal(ks[6], (32, 32), f32), 'Wfc1': jax.random.normal(ks[7], (8, 64), f32), 'Wfc2': jax.random.normal(ks[8], (64, 64), f32), 'Wfc3': jax.random.normal(ks[9], (64, 192), f32), 'Wl2_s': jax.random.normal(ks[10], (96, 64), f32), 'Wl2_v': jax.random.normal(ks[11], (96, 32), f32), 'Wa': jax.random.normal(ks[12], (96, 1), f32), 'edge_src': jax.random.randint(ks[13], (N_EDGES,), 0, N_NODES), 'edge_dst': jax.random.randint(ks[14], (N_EDGES,), 0, N_NODES)}
    _L0_gnn_all = _L0_gnn_setup()
    _L0_gnn_in = {k: v for k, v in _L0_gnn_all.items() if k in ('Wsc0', 'Wsc1', 'Wl1_0', 'Wl1_1', 'Wfc1', 'Wfc2', 'Wfc3', 'Wl2_s', 'Wl2_v', 'Wa')}
    del _L0_gnn_all

    def _L1_gnn_setup():
        import jax, jax.numpy as jnp
        import numpy as np
        N = 20000
        E = 5000
        MUL0 = 64
        MUL1 = 32
        FC_IN = 16
        FC_H = 64
        WNUM = 192
        key = jax.random.key(seed)
        ks = jax.random.split(key, 16)
        return {'x': jax.random.normal(ks[0], (N, MUL0 + 3 * MUL1), jnp.float32), 'node_attr': jnp.ones((N, 1), jnp.float32), 'edge_scalars': jax.random.normal(ks[1], (E, FC_IN), jnp.float32), 'edge_attr_sh': jax.random.normal(ks[2], (E, 4), jnp.float32), 'edge_src': jax.random.randint(ks[3], (E,), 0, N), 'edge_dst': jax.random.randint(ks[4], (E,), 0, N), 'Wfc1': jax.random.normal(ks[5], (FC_IN, FC_H), jnp.float32), 'Wfc2': jax.random.normal(ks[6], (FC_H, WNUM), jnp.float32), 'Wsc0': jax.random.normal(ks[7], (MUL0, MUL0), jnp.float32), 'Wsc1': jax.random.normal(ks[8], (MUL1, MUL1), jnp.float32), 'Wl1_0': jax.random.normal(ks[9], (MUL0, MUL0), jnp.float32), 'Wl1_1': jax.random.normal(ks[10], (MUL1, MUL1), jnp.float32), 'Wl2_s': jax.random.normal(ks[11], (MUL0 + MUL1, MUL0), jnp.float32), 'Wl2_v': jax.random.normal(ks[12], (MUL0 + MUL1, MUL1), jnp.float32), 'Wa': 0.1 * jax.random.normal(ks[13], (MUL0 + MUL1, 1), jnp.float32)}
    _L1_gnn_all = _L1_gnn_setup()
    _L1_gnn_in = {k: v for k, v in _L1_gnn_all.items() if k in ('Wfc1', 'Wfc2', 'Wsc0', 'Wsc1', 'Wl1_0', 'Wl1_1', 'Wl2_s', 'Wl2_v', 'Wa')}
    del _L1_gnn_all

    def _L2_gnn_setup():
        import jax, jax.numpy as jnp
        import numpy as np
        N_NODES = 50000
        N_EDGES = 12500
        MUL0, MUL1 = (64, 32)
        N_BASIS, N_RADIAL = (10, 100)
        W_NUMEL = 192
        NUM_NEIGHBORS = 16.0
        INV_SQRT3 = np.float32(1.0 / np.sqrt(3.0))
        RELU_GAIN = np.float32(np.sqrt(2.0))
        FAN_L2 = np.float32(np.sqrt(MUL0 + MUL1))

        def _fctp_scalar_attr(x0, x1, a, W0, W1):
            o0 = x0 @ W0 * a * (1.0 / np.sqrt(W0.shape[0]))
            o1 = jnp.einsum('nud,uw->nwd', x1, W1) * a[..., None] * (1.0 / np.sqrt(W1.shape[0]))
            return (o0, o1)
        key = jax.random.key(seed)
        ks = jax.random.split(key, 16)
        return {'node_input': jax.random.normal(ks[0], (N_NODES, MUL0 + 3 * MUL1), jnp.float32), 'node_attr': jnp.ones((N_NODES, 1), jnp.float32), 'edge_attr': jax.random.normal(ks[1], (N_EDGES, 4), jnp.float32), 'edge_length_embedded': jax.random.uniform(ks[2], (N_EDGES, N_BASIS), dtype=jnp.float32), 'W_si0': jax.random.normal(ks[3], (MUL0, MUL0), jnp.float32), 'W_si1': jax.random.normal(ks[4], (MUL1, MUL1), jnp.float32), 'W_l1_0': jax.random.normal(ks[5], (MUL0, MUL0), jnp.float32), 'W_l1_1': jax.random.normal(ks[6], (MUL1, MUL1), jnp.float32), 'W_l2_00': jax.random.normal(ks[7], (MUL0, MUL0), jnp.float32), 'W_l2_10': jax.random.normal(ks[8], (MUL1, MUL0), jnp.float32), 'W_l2_01': jax.random.normal(ks[9], (MUL0, MUL1), jnp.float32), 'W_l2_11': jax.random.normal(ks[10], (MUL1, MUL1), jnp.float32), 'W_fc1': jax.random.normal(ks[11], (N_BASIS, N_RADIAL), jnp.float32), 'W_fc2': jax.random.normal(ks[12], (N_RADIAL, W_NUMEL), jnp.float32), 'edge_src': jax.random.randint(ks[13], (N_EDGES,), 0, N_NODES), 'edge_dst': jax.random.randint(ks[14], (N_EDGES,), 0, N_NODES)}
    _L2_gnn_all = _L2_gnn_setup()
    _L2_gnn_in = {k: v for k, v in _L2_gnn_all.items() if k in ('W_si0', 'W_si1', 'W_l1_0', 'W_l1_1', 'W_l2_00', 'W_l2_10', 'W_l2_01', 'W_l2_11', 'W_fc1', 'W_fc2')}
    del _L2_gnn_all

    def _L3_gnn_setup():
        import jax, jax.numpy as jnp
        import numpy as np
        N, E = (10000, 2500)
        C0, C1 = (64, 32)
        H, A = (8, 8)
        H0, H1 = (8, 4)
        M0, M1 = (128, 64)
        NG, RH = (64, 64)
        WN = C0 + C0 + C1 + C1 + C1
        DS, DV = (C0 + C1, C0 + 2 * C1)
        EPS = 1e-05
        SQ3 = np.float32(np.sqrt(3.0))
        SQ2 = np.float32(np.sqrt(2.0))

        def _split(x):
            return (x[:, :C0], x[:, C0:].reshape(x.shape[0], C1, 3))

        def _merge(s, v):
            return jnp.concatenate([s, v.reshape(v.shape[0], -1)], axis=1)

        def _eq_ln(x, w0, b0, w1):
            s, v = _split(x)
            s = s - s.mean(axis=1, keepdims=True)
            s = s * jax.lax.rsqrt(jnp.square(s).mean(axis=1, keepdims=True) + EPS) * w0 + b0
            v = v * jax.lax.rsqrt(jnp.square(v).mean(axis=(1, 2), keepdims=True) + EPS) * w1[None, :, None]
            return (s, v)

        def _eq_lin(s, v, ws, bs, wv):
            return (s @ ws + bs, jnp.einsum('nud,uk->nkd', v, wv))

        def _ln(x, g, b):
            xc = x - x.mean(-1, keepdims=True)
            return xc * jax.lax.rsqrt(jnp.square(xc).mean(-1, keepdims=True) + EPS) * g + b

        def _smooth_leaky(x, alpha=0.2):
            return 0.5 * (1 + alpha) * x + 0.5 * (1 - alpha) * x * (2.0 * jax.nn.sigmoid(x) - 1.0)

        def _forward(node_input, node_attr, edge_vec, edge_scalars, edge_src, edge_dst, ln1_w0, ln1_b0, ln1_w1, ln2_w0, ln2_b0, ln2_w1, msrc_ws, msrc_wv, mdst_ws, mdst_bs, mdst_wv, rw1, rb1, rg1, rbe1, rw2, rb2, rg2, rbe2, rw3, roff, lin_ws, lin_bs, lin_wv, alpha_dot, proj_ws, proj_bs, proj_wv, f1_ws, f1_bs, f1_wv, f2_ws, f2_bs, f2_wv):
            n = node_input.shape[0]
            s, v = _eq_ln(node_input, ln1_w0, ln1_b0, ln1_w1)
            src_s = s @ msrc_ws
            src_v = jnp.einsum('nud,uk->nkd', v, msrc_wv)
            dst_s = s @ mdst_ws + mdst_bs
            dst_v = jnp.einsum('nud,uk->nkd', v, mdst_wv)
            ms = src_s[edge_src] + dst_s[edge_dst]
            mv = src_v[edge_src] + dst_v[edge_dst]
            h = jax.nn.silu(_ln(edge_scalars @ rw1 + rb1, rg1, rbe1))
            h = jax.nn.silu(_ln(h @ rw2 + rb2, rg2, rbe2))
            w = h @ rw3 + roff
            rhat = edge_vec * jax.lax.rsqrt(jnp.sum(jnp.square(edge_vec), -1, keepdims=True) + 1e-12)
            Y1 = SQ3 * rhat
            w1, w2, w3, w4, w5 = jnp.split(w, [C0, 2 * C0, 2 * C0 + C1, 2 * C0 + 2 * C1], axis=1)
            o0a = w1 * ms
            o0b = w4 * (jnp.einsum('eud,ed->eu', mv, Y1) / SQ3)
            o1a = (w2 * ms)[:, :, None] * Y1[:, None, :]
            o1b = w3[:, :, None] * mv
            o1c = w5[:, :, None] * (jnp.cross(mv, Y1[:, None, :]) / SQ2)
            ds = jnp.concatenate([o0a, o0b], axis=1)
            dv = jnp.concatenate([o1a, o1b, o1c], axis=1)
            ls, lv = _eq_lin(ds, dv, lin_ws, lin_bs, lin_wv)
            e = ls.shape[0]
            alpha = ls[:, :H * A].reshape(e, H, A)
            vs = ls[:, H * A:].reshape(e, H, H0)
            vv = lv.reshape(e, H, H1, 3)
            a = jnp.einsum('ehk,hk->eh', _smooth_leaky(alpha), alpha_dot)
            amax = jax.lax.stop_gradient(jax.ops.segment_max(a, edge_dst, num_segments=n))
            a = jnp.exp(a - amax[edge_dst])
            a = a / (jax.ops.segment_sum(a, edge_dst, num_segments=n)[edge_dst] + 1e-12)
            ns = jax.ops.segment_sum(vs * a[..., None], edge_dst, num_segments=n).reshape(n, H * H0)
            nv = jax.ops.segment_sum(vv * a[..., None, None], edge_dst, num_segments=n).reshape(n, H * H1, 3)
            ps, pv = _eq_lin(ns, nv, proj_ws, proj_bs, proj_wv)
            x = node_input + _merge(ps, pv)
            s2, v2 = _eq_ln(x, ln2_w0, ln2_b0, ln2_w1)
            a0 = node_attr[:, :1]
            fs, fv = _eq_lin(s2, v2, f1_ws, f1_bs, f1_wv)
            fs = fs * a0
            fv = fv * a0[:, :, None]
            sc = jax.nn.silu(fs[:, :M0])
            fv = fv * jax.nn.sigmoid(fs[:, M0:])[:, :, None]
            os_, ov = _eq_lin(sc, fv, f2_ws, f2_bs, f2_wv)
            os_ = os_ * a0
            ov = ov * a0[:, :, None]
            return x + _merge(os_, ov)
        key = jax.random.key(seed)
        ks = iter(jax.random.split(key, 24))

        def nrm(shape, fan):
            return jax.random.normal(next(ks), shape, jnp.float32) / np.float32(np.sqrt(fan))
        inp = {}
        inp['node_input'] = jax.random.normal(next(ks), (N, C0 + 3 * C1), jnp.float32)
        inp['node_attr'] = jnp.ones((N, 1), jnp.float32)
        inp['edge_vec'] = jax.random.normal(next(ks), (E, 3), jnp.float32)
        inp['edge_scalars'] = jax.random.uniform(next(ks), (E, NG), dtype=jnp.float32)
        inp['edge_src'] = jax.random.randint(next(ks), (E,), 0, N)
        inp['edge_dst'] = jax.random.randint(next(ks), (E,), 0, N)
        inp['ln1_w0'] = jnp.ones((C0,), jnp.float32)
        inp['ln1_b0'] = jnp.zeros((C0,), jnp.float32)
        inp['ln1_w1'] = jnp.ones((C1,), jnp.float32)
        inp['ln2_w0'] = jnp.ones((C0,), jnp.float32)
        inp['ln2_b0'] = jnp.zeros((C0,), jnp.float32)
        inp['ln2_w1'] = jnp.ones((C1,), jnp.float32)
        inp['msrc_ws'] = nrm((C0, C0), C0)
        inp['msrc_wv'] = nrm((C1, C1), C1)
        inp['mdst_ws'] = nrm((C0, C0), C0)
        inp['mdst_bs'] = jnp.zeros((C0,), jnp.float32)
        inp['mdst_wv'] = nrm((C1, C1), C1)
        inp['rw1'] = nrm((NG, RH), NG)
        inp['rb1'] = jnp.zeros((RH,), jnp.float32)
        inp['rg1'] = jnp.ones((RH,), jnp.float32)
        inp['rbe1'] = jnp.zeros((RH,), jnp.float32)
        inp['rw2'] = nrm((RH, RH), RH)
        inp['rb2'] = jnp.zeros((RH,), jnp.float32)
        inp['rg2'] = jnp.ones((RH,), jnp.float32)
        inp['rbe2'] = jnp.zeros((RH,), jnp.float32)
        inp['rw3'] = nrm((RH, WN), RH)
        inp['roff'] = 0.1 * jax.random.normal(next(ks), (WN,), jnp.float32)
        inp['lin_ws'] = nrm((DS, H * A + H * H0), DS)
        inp['lin_bs'] = jnp.zeros((H * A + H * H0,), jnp.float32)
        inp['lin_wv'] = nrm((DV, H * H1), DV)
        inp['alpha_dot'] = nrm((H, A), A)
        inp['proj_ws'] = nrm((H * H0, C0), H * H0)
        inp['proj_bs'] = jnp.zeros((C0,), jnp.float32)
        inp['proj_wv'] = nrm((H * H1, C1), H * H1)
        inp['f1_ws'] = nrm((C0, M0 + M1), C0)
        inp['f1_bs'] = jnp.zeros((M0 + M1,), jnp.float32)
        inp['f1_wv'] = nrm((C1, M1), C1)
        inp['f2_ws'] = nrm((M0, C0), M0)
        inp['f2_bs'] = jnp.zeros((C0,), jnp.float32)
        inp['f2_wv'] = nrm((M1, C1), M1)
        return inp
    _L3_gnn_all = _L3_gnn_setup()
    _L3_gnn_in = {k: v for k, v in _L3_gnn_all.items() if k in ('ln1_w0', 'ln1_b0', 'ln1_w1', 'ln2_w0', 'ln2_b0', 'ln2_w1', 'msrc_ws', 'msrc_wv', 'mdst_ws', 'mdst_bs', 'mdst_wv', 'rw1', 'rb1', 'rg1', 'rbe1', 'rw2', 'rb2', 'rg2', 'rbe2', 'rw3', 'roff', 'lin_ws', 'lin_bs', 'lin_wv', 'alpha_dot', 'proj_ws', 'proj_bs', 'proj_wv', 'f1_ws', 'f1_bs', 'f1_wv', 'f2_ws', 'f2_bs', 'f2_wv')}
    del _L3_gnn_all
    return {'x': x, 'src': src, 'dst': dst, 'edge_attr_10': edge_attr_10, 'edge_attr_16': edge_attr_16, 'edge_attr_3': edge_attr_3, 'edge_attr_4': edge_attr_4, 'edge_attr_64': edge_attr_64, 'edge_attr_8': edge_attr_8, 'node_vec1': node_vec1, 'L0_gnn_Wsc0': _L0_gnn_in['Wsc0'], 'L0_gnn_Wsc1': _L0_gnn_in['Wsc1'], 'L0_gnn_Wl1_0': _L0_gnn_in['Wl1_0'], 'L0_gnn_Wl1_1': _L0_gnn_in['Wl1_1'], 'L0_gnn_Wfc1': _L0_gnn_in['Wfc1'], 'L0_gnn_Wfc2': _L0_gnn_in['Wfc2'], 'L0_gnn_Wfc3': _L0_gnn_in['Wfc3'], 'L0_gnn_Wl2_s': _L0_gnn_in['Wl2_s'], 'L0_gnn_Wl2_v': _L0_gnn_in['Wl2_v'], 'L0_gnn_Wa': _L0_gnn_in['Wa'], 'L1_gnn_Wfc1': _L1_gnn_in['Wfc1'], 'L1_gnn_Wfc2': _L1_gnn_in['Wfc2'], 'L1_gnn_Wsc0': _L1_gnn_in['Wsc0'], 'L1_gnn_Wsc1': _L1_gnn_in['Wsc1'], 'L1_gnn_Wl1_0': _L1_gnn_in['Wl1_0'], 'L1_gnn_Wl1_1': _L1_gnn_in['Wl1_1'], 'L1_gnn_Wl2_s': _L1_gnn_in['Wl2_s'], 'L1_gnn_Wl2_v': _L1_gnn_in['Wl2_v'], 'L1_gnn_Wa': _L1_gnn_in['Wa'], 'L2_gnn_W_si0': _L2_gnn_in['W_si0'], 'L2_gnn_W_si1': _L2_gnn_in['W_si1'], 'L2_gnn_W_l1_0': _L2_gnn_in['W_l1_0'], 'L2_gnn_W_l1_1': _L2_gnn_in['W_l1_1'], 'L2_gnn_W_l2_00': _L2_gnn_in['W_l2_00'], 'L2_gnn_W_l2_10': _L2_gnn_in['W_l2_10'], 'L2_gnn_W_l2_01': _L2_gnn_in['W_l2_01'], 'L2_gnn_W_l2_11': _L2_gnn_in['W_l2_11'], 'L2_gnn_W_fc1': _L2_gnn_in['W_fc1'], 'L2_gnn_W_fc2': _L2_gnn_in['W_fc2'], 'L3_gnn_ln1_w0': _L3_gnn_in['ln1_w0'], 'L3_gnn_ln1_b0': _L3_gnn_in['ln1_b0'], 'L3_gnn_ln1_w1': _L3_gnn_in['ln1_w1'], 'L3_gnn_ln2_w0': _L3_gnn_in['ln2_w0'], 'L3_gnn_ln2_b0': _L3_gnn_in['ln2_b0'], 'L3_gnn_ln2_w1': _L3_gnn_in['ln2_w1'], 'L3_gnn_msrc_ws': _L3_gnn_in['msrc_ws'], 'L3_gnn_msrc_wv': _L3_gnn_in['msrc_wv'], 'L3_gnn_mdst_ws': _L3_gnn_in['mdst_ws'], 'L3_gnn_mdst_bs': _L3_gnn_in['mdst_bs'], 'L3_gnn_mdst_wv': _L3_gnn_in['mdst_wv'], 'L3_gnn_rw1': _L3_gnn_in['rw1'], 'L3_gnn_rb1': _L3_gnn_in['rb1'], 'L3_gnn_rg1': _L3_gnn_in['rg1'], 'L3_gnn_rbe1': _L3_gnn_in['rbe1'], 'L3_gnn_rw2': _L3_gnn_in['rw2'], 'L3_gnn_rb2': _L3_gnn_in['rb2'], 'L3_gnn_rg2': _L3_gnn_in['rg2'], 'L3_gnn_rbe2': _L3_gnn_in['rbe2'], 'L3_gnn_rw3': _L3_gnn_in['rw3'], 'L3_gnn_roff': _L3_gnn_in['roff'], 'L3_gnn_lin_ws': _L3_gnn_in['lin_ws'], 'L3_gnn_lin_bs': _L3_gnn_in['lin_bs'], 'L3_gnn_lin_wv': _L3_gnn_in['lin_wv'], 'L3_gnn_alpha_dot': _L3_gnn_in['alpha_dot'], 'L3_gnn_proj_ws': _L3_gnn_in['proj_ws'], 'L3_gnn_proj_bs': _L3_gnn_in['proj_bs'], 'L3_gnn_proj_wv': _L3_gnn_in['proj_wv'], 'L3_gnn_f1_ws': _L3_gnn_in['f1_ws'], 'L3_gnn_f1_bs': _L3_gnn_in['f1_bs'], 'L3_gnn_f1_wv': _L3_gnn_in['f1_wv'], 'L3_gnn_f2_ws': _L3_gnn_in['f2_ws'], 'L3_gnn_f2_bs': _L3_gnn_in['f2_bs'], 'L3_gnn_f2_wv': _L3_gnn_in['f2_wv']}

def reference(x, src, dst, edge_attr_10, edge_attr_16, edge_attr_3, edge_attr_4, edge_attr_64, edge_attr_8, node_vec1, L0_gnn_Wsc0, L0_gnn_Wsc1, L0_gnn_Wl1_0, L0_gnn_Wl1_1, L0_gnn_Wfc1, L0_gnn_Wfc2, L0_gnn_Wfc3, L0_gnn_Wl2_s, L0_gnn_Wl2_v, L0_gnn_Wa, L1_gnn_Wfc1, L1_gnn_Wfc2, L1_gnn_Wsc0, L1_gnn_Wsc1, L1_gnn_Wl1_0, L1_gnn_Wl1_1, L1_gnn_Wl2_s, L1_gnn_Wl2_v, L1_gnn_Wa, L2_gnn_W_si0, L2_gnn_W_si1, L2_gnn_W_l1_0, L2_gnn_W_l1_1, L2_gnn_W_l2_00, L2_gnn_W_l2_10, L2_gnn_W_l2_01, L2_gnn_W_l2_11, L2_gnn_W_fc1, L2_gnn_W_fc2, L3_gnn_ln1_w0, L3_gnn_ln1_b0, L3_gnn_ln1_w1, L3_gnn_ln2_w0, L3_gnn_ln2_b0, L3_gnn_ln2_w1, L3_gnn_msrc_ws, L3_gnn_msrc_wv, L3_gnn_mdst_ws, L3_gnn_mdst_bs, L3_gnn_mdst_wv, L3_gnn_rw1, L3_gnn_rb1, L3_gnn_rg1, L3_gnn_rbe1, L3_gnn_rw2, L3_gnn_rb2, L3_gnn_rg2, L3_gnn_rbe2, L3_gnn_rw3, L3_gnn_roff, L3_gnn_lin_ws, L3_gnn_lin_bs, L3_gnn_lin_wv, L3_gnn_alpha_dot, L3_gnn_proj_ws, L3_gnn_proj_bs, L3_gnn_proj_wv, L3_gnn_f1_ws, L3_gnn_f1_bs, L3_gnn_f1_wv, L3_gnn_f2_ws, L3_gnn_f2_bs, L3_gnn_f2_wv):
    import jax
    import jax.numpy as jnp

    def _L0_gnn_ref(node_input, node_attr, edge_attr, edge_scalar_attr, Wsc0, Wsc1, Wl1_0, Wl1_1, Wfc1, Wfc2, Wfc3, Wl2_s, Wl2_v, Wa, edge_src, edge_dst):
        import jax, jax.numpy as jnp
        import numpy as np
        N_NODES = 10000
        N_EDGES = 5000
        NUM_NEIGHBORS = 32.0
        INV_SQRT3 = 1.0 / np.sqrt(3.0)

        def _fctp_scalar_attr(xs, xv, Ws, Wv, a):
            out_s = xs @ Ws * (a / np.sqrt(xs.shape[1]))[:, None]
            out_v = jnp.einsum('nuc,uw->nwc', xv, Wv) * (a / np.sqrt(xv.shape[1]))[:, None, None]
            return (out_s, out_v)
        N = node_input.shape[0]
        a = node_attr[:, 0]
        xs = node_input[:, :64]
        xv = node_input[:, 64:].reshape(N, 32, 3)
        sc_s, sc_v = _fctp_scalar_attr(xs, xv, Wsc0, Wsc1, a)
        f_s, f_v = _fctp_scalar_attr(xs, xv, Wl1_0, Wl1_1, a)
        h = jax.nn.gelu(edge_scalar_attr @ Wfc1 / np.sqrt(8.0))
        h = jax.nn.gelu(h @ Wfc2 / np.sqrt(64.0))
        w = h @ Wfc3 / np.sqrt(64.0)
        w0, w1, w2, w3 = (w[:, :64], w[:, 64:128], w[:, 128:160], w[:, 160:192])
        gs = f_s[edge_src]
        gv = f_v[edge_src]
        y0 = edge_attr[:, 0]
        y1 = edge_attr[:, 1:4]
        mid0 = w0 * gs * y0[:, None]
        mid1 = w3 * jnp.einsum('euc,ec->eu', gv, y1) * INV_SQRT3
        mid2 = (w1 * gs)[:, :, None] * y1[:, None, :]
        mid3 = w2[:, :, None] * gv * y0[:, None, None]
        inv = 1.0 / np.sqrt(NUM_NEIGHBORS)
        seg = lambda x: jax.ops.segment_sum(x, edge_dst, num_segments=N) * inv
        ns0, ns1, nv2, nv3 = (seg(mid0), seg(mid1), seg(mid2), seg(mid3))
        mid_s = jnp.concatenate([ns0, ns1], axis=1)
        mid_v = jnp.concatenate([nv2, nv3], axis=1)
        out_s = mid_s @ Wl2_s * (a / np.sqrt(96.0))[:, None]
        out_v = jnp.einsum('nuc,uw->nwc', mid_v, Wl2_v) * (a / np.sqrt(96.0))[:, None, None]
        alpha = mid_s @ Wa * (a / np.sqrt(96.0))[:, None]
        res_s = sc_s + alpha * out_s
        res_v = sc_v + alpha[:, :, None] * out_v
        return jnp.concatenate([res_s, res_v.reshape(N, 96)], axis=1)

    def _L1_gnn_ref(x, node_attr, edge_scalars, edge_attr_sh, edge_src, edge_dst, Wfc1, Wfc2, Wsc0, Wsc1, Wl1_0, Wl1_1, Wl2_s, Wl2_v, Wa):
        import jax, jax.numpy as jnp
        import numpy as np
        N = 20000
        E = 5000
        MUL0 = 64
        MUL1 = 32
        FC_IN = 16
        FC_H = 64
        WNUM = 192
        n = x.shape[0]
        x0 = x[:, :MUL0]
        x1 = x[:, MUL0:].reshape(n, MUL1, 3)
        a = node_attr
        h = jax.nn.silu(edge_scalars @ (Wfc1 / jnp.sqrt(jnp.float32(FC_IN))))
        w = h @ (Wfc2 / jnp.sqrt(jnp.float32(FC_H)))
        w0 = w[:, :64]
        w1 = w[:, 64:128]
        w2 = w[:, 128:160]
        w3 = w[:, 160:192]
        inv8 = 1.0 / jnp.sqrt(jnp.float32(MUL0))
        inv32 = 1.0 / jnp.sqrt(jnp.float32(MUL1))
        sc = jnp.concatenate([x0 @ Wsc0 * a * inv8, (jnp.einsum('num,uv->nvm', x1, Wsc1) * a[..., None] * inv32).reshape(n, 3 * MUL1)], axis=1)
        f0 = x0 @ Wl1_0 * a * inv8
        f1 = jnp.einsum('num,uv->nvm', x1, Wl1_1) * a[..., None] * inv32
        e0 = f0[edge_src]
        e1 = f1[edge_src]
        sh0 = edge_attr_sh[:, :1]
        sh1 = edge_attr_sh[:, 1:4]
        mid0 = w0 * e0 * sh0
        mid1 = w3 * jnp.einsum('eum,em->eu', e1, sh1) / jnp.sqrt(3.0)
        mid2 = w1[:, :, None] * e0[:, :, None] * sh1[:, None, :]
        mid3 = w2[:, :, None] * e1 * sh0[:, :, None]
        cnt = jnp.clip(jax.ops.segment_sum(jnp.ones(edge_dst.shape, x.dtype), edge_dst, num_segments=n), 1.0)

        def smean(v):
            s = jax.ops.segment_sum(v, edge_dst, num_segments=n)
            return s / cnt.reshape((n,) + (1,) * (v.ndim - 1))
        n0, n1 = (smean(mid0), smean(mid1))
        n2, n3 = (smean(mid2), smean(mid3))
        scal = jnp.concatenate([n0, n1], axis=1)
        vec = jnp.concatenate([n2, n3], axis=1)
        inv96 = 1.0 / jnp.sqrt(jnp.float32(MUL0 + MUL1))
        alpha = scal @ Wa * a * inv96
        out_s = scal @ Wl2_s * a * inv96
        out_v = jnp.einsum('num,uv->nvm', vec, Wl2_v) * a[..., None] * inv96
        conv = jnp.concatenate([out_s, out_v.reshape(n, 3 * MUL1)], axis=1)
        return sc + alpha * conv

    def _L2_gnn_ref(node_input, node_attr, edge_src, edge_dst, edge_attr, edge_length_embedded, W_si0, W_si1, W_l1_0, W_l1_1, W_l2_00, W_l2_10, W_l2_01, W_l2_11, W_fc1, W_fc2):
        import jax, jax.numpy as jnp
        import numpy as np
        N_NODES = 50000
        N_EDGES = 12500
        MUL0, MUL1 = (64, 32)
        N_BASIS, N_RADIAL = (10, 100)
        W_NUMEL = 192
        NUM_NEIGHBORS = 16.0
        INV_SQRT3 = np.float32(1.0 / np.sqrt(3.0))
        RELU_GAIN = np.float32(np.sqrt(2.0))
        FAN_L2 = np.float32(np.sqrt(MUL0 + MUL1))

        def _fctp_scalar_attr(x0, x1, a, W0, W1):
            o0 = x0 @ W0 * a * (1.0 / np.sqrt(W0.shape[0]))
            o1 = jnp.einsum('nud,uw->nwd', x1, W1) * a[..., None] * (1.0 / np.sqrt(W1.shape[0]))
            return (o0, o1)
        N = node_input.shape[0]
        x0 = node_input[:, :MUL0]
        x1 = node_input[:, MUL0:].reshape(N, MUL1, 3)
        a = node_attr
        h = jax.nn.relu(edge_length_embedded @ W_fc1 * (1.0 / np.sqrt(N_BASIS))) * RELU_GAIN
        w = h @ W_fc2 * (1.0 / np.sqrt(N_RADIAL))
        w0, w1, w2, w3 = (w[:, :64], w[:, 64:128], w[:, 128:160], w[:, 160:192])
        si0, si1 = _fctp_scalar_attr(x0, x1, a, W_si0, W_si1)
        l0, l1 = _fctp_scalar_attr(x0, x1, a, W_l1_0, W_l1_1)
        y0 = l0[edge_src]
        y1 = l1[edge_src]
        e0 = edge_attr[:, :1]
        e1 = edge_attr[:, 1:4]
        m0 = w0 * y0 * e0
        m1 = (w1 * y0)[:, :, None] * e1[:, None, :]
        m2 = (w2 * e0)[:, :, None] * y1
        m3 = w3 * jnp.einsum('eud,ed->eu', y1, e1) * INV_SQRT3
        inv = np.float32(1.0 / np.sqrt(NUM_NEIGHBORS))
        s0 = jax.ops.segment_sum(m0, edge_dst, num_segments=N) * inv
        s1 = jax.ops.segment_sum(m1, edge_dst, num_segments=N) * inv
        s2 = jax.ops.segment_sum(m2, edge_dst, num_segments=N) * inv
        s3 = jax.ops.segment_sum(m3, edge_dst, num_segments=N) * inv
        o0 = (s0 @ W_l2_00 + s3 @ W_l2_10) * a / FAN_L2
        o1 = (jnp.einsum('nud,uw->nwd', s1, W_l2_01) + jnp.einsum('nud,uw->nwd', s2, W_l2_11)) * a[..., None] / FAN_L2
        out0 = si0 + 0.5 * o0
        out1 = si1 + 0.5 * o1
        return jnp.concatenate([out0, out1.reshape(N, 3 * MUL1)], axis=1)

    def _L3_gnn_ref(node_input, node_attr, edge_vec, edge_scalars, edge_src, edge_dst, ln1_w0, ln1_b0, ln1_w1, ln2_w0, ln2_b0, ln2_w1, msrc_ws, msrc_wv, mdst_ws, mdst_bs, mdst_wv, rw1, rb1, rg1, rbe1, rw2, rb2, rg2, rbe2, rw3, roff, lin_ws, lin_bs, lin_wv, alpha_dot, proj_ws, proj_bs, proj_wv, f1_ws, f1_bs, f1_wv, f2_ws, f2_bs, f2_wv):
        import jax, jax.numpy as jnp
        import numpy as np
        N, E = (10000, 2500)
        C0, C1 = (64, 32)
        H, A = (8, 8)
        H0, H1 = (8, 4)
        M0, M1 = (128, 64)
        NG, RH = (64, 64)
        WN = C0 + C0 + C1 + C1 + C1
        DS, DV = (C0 + C1, C0 + 2 * C1)
        EPS = 1e-05
        SQ3 = np.float32(np.sqrt(3.0))
        SQ2 = np.float32(np.sqrt(2.0))

        def _split(x):
            return (x[:, :C0], x[:, C0:].reshape(x.shape[0], C1, 3))

        def _merge(s, v):
            return jnp.concatenate([s, v.reshape(v.shape[0], -1)], axis=1)

        def _eq_ln(x, w0, b0, w1):
            s, v = _split(x)
            s = s - s.mean(axis=1, keepdims=True)
            s = s * jax.lax.rsqrt(jnp.square(s).mean(axis=1, keepdims=True) + EPS) * w0 + b0
            v = v * jax.lax.rsqrt(jnp.square(v).mean(axis=(1, 2), keepdims=True) + EPS) * w1[None, :, None]
            return (s, v)

        def _eq_lin(s, v, ws, bs, wv):
            return (s @ ws + bs, jnp.einsum('nud,uk->nkd', v, wv))

        def _ln(x, g, b):
            xc = x - x.mean(-1, keepdims=True)
            return xc * jax.lax.rsqrt(jnp.square(xc).mean(-1, keepdims=True) + EPS) * g + b

        def _smooth_leaky(x, alpha=0.2):
            return 0.5 * (1 + alpha) * x + 0.5 * (1 - alpha) * x * (2.0 * jax.nn.sigmoid(x) - 1.0)

        def _forward(node_input, node_attr, edge_vec, edge_scalars, edge_src, edge_dst, ln1_w0, ln1_b0, ln1_w1, ln2_w0, ln2_b0, ln2_w1, msrc_ws, msrc_wv, mdst_ws, mdst_bs, mdst_wv, rw1, rb1, rg1, rbe1, rw2, rb2, rg2, rbe2, rw3, roff, lin_ws, lin_bs, lin_wv, alpha_dot, proj_ws, proj_bs, proj_wv, f1_ws, f1_bs, f1_wv, f2_ws, f2_bs, f2_wv):
            n = node_input.shape[0]
            s, v = _eq_ln(node_input, ln1_w0, ln1_b0, ln1_w1)
            src_s = s @ msrc_ws
            src_v = jnp.einsum('nud,uk->nkd', v, msrc_wv)
            dst_s = s @ mdst_ws + mdst_bs
            dst_v = jnp.einsum('nud,uk->nkd', v, mdst_wv)
            ms = src_s[edge_src] + dst_s[edge_dst]
            mv = src_v[edge_src] + dst_v[edge_dst]
            h = jax.nn.silu(_ln(edge_scalars @ rw1 + rb1, rg1, rbe1))
            h = jax.nn.silu(_ln(h @ rw2 + rb2, rg2, rbe2))
            w = h @ rw3 + roff
            rhat = edge_vec * jax.lax.rsqrt(jnp.sum(jnp.square(edge_vec), -1, keepdims=True) + 1e-12)
            Y1 = SQ3 * rhat
            w1, w2, w3, w4, w5 = jnp.split(w, [C0, 2 * C0, 2 * C0 + C1, 2 * C0 + 2 * C1], axis=1)
            o0a = w1 * ms
            o0b = w4 * (jnp.einsum('eud,ed->eu', mv, Y1) / SQ3)
            o1a = (w2 * ms)[:, :, None] * Y1[:, None, :]
            o1b = w3[:, :, None] * mv
            o1c = w5[:, :, None] * (jnp.cross(mv, Y1[:, None, :]) / SQ2)
            ds = jnp.concatenate([o0a, o0b], axis=1)
            dv = jnp.concatenate([o1a, o1b, o1c], axis=1)
            ls, lv = _eq_lin(ds, dv, lin_ws, lin_bs, lin_wv)
            e = ls.shape[0]
            alpha = ls[:, :H * A].reshape(e, H, A)
            vs = ls[:, H * A:].reshape(e, H, H0)
            vv = lv.reshape(e, H, H1, 3)
            a = jnp.einsum('ehk,hk->eh', _smooth_leaky(alpha), alpha_dot)
            amax = jax.lax.stop_gradient(jax.ops.segment_max(a, edge_dst, num_segments=n))
            a = jnp.exp(a - amax[edge_dst])
            a = a / (jax.ops.segment_sum(a, edge_dst, num_segments=n)[edge_dst] + 1e-12)
            ns = jax.ops.segment_sum(vs * a[..., None], edge_dst, num_segments=n).reshape(n, H * H0)
            nv = jax.ops.segment_sum(vv * a[..., None, None], edge_dst, num_segments=n).reshape(n, H * H1, 3)
            ps, pv = _eq_lin(ns, nv, proj_ws, proj_bs, proj_wv)
            x = node_input + _merge(ps, pv)
            s2, v2 = _eq_ln(x, ln2_w0, ln2_b0, ln2_w1)
            a0 = node_attr[:, :1]
            fs, fv = _eq_lin(s2, v2, f1_ws, f1_bs, f1_wv)
            fs = fs * a0
            fv = fv * a0[:, :, None]
            sc = jax.nn.silu(fs[:, :M0])
            fv = fv * jax.nn.sigmoid(fs[:, M0:])[:, :, None]
            os_, ov = _eq_lin(sc, fv, f2_ws, f2_bs, f2_wv)
            os_ = os_ * a0
            ov = ov * a0[:, :, None]
            return x + _merge(os_, ov)
        return _forward(node_input, node_attr, edge_vec, edge_scalars, edge_src, edge_dst, ln1_w0, ln1_b0, ln1_w1, ln2_w0, ln2_b0, ln2_w1, msrc_ws, msrc_wv, mdst_ws, mdst_bs, mdst_wv, rw1, rb1, rg1, rbe1, rw2, rb2, rg2, rbe2, rw3, roff, lin_ws, lin_bs, lin_wv, alpha_dot, proj_ws, proj_bs, proj_wv, f1_ws, f1_bs, f1_wv, f2_ws, f2_bs, f2_wv)
    x = _layernorm(x + _L0_gnn_ref(x, node_vec1, edge_attr_4, edge_attr_8, L0_gnn_Wsc0, L0_gnn_Wsc1, L0_gnn_Wl1_0, L0_gnn_Wl1_1, L0_gnn_Wfc1, L0_gnn_Wfc2, L0_gnn_Wfc3, L0_gnn_Wl2_s, L0_gnn_Wl2_v, L0_gnn_Wa, src, dst), axis=-1)
    x = _layernorm(x + _L1_gnn_ref(x, node_vec1, edge_attr_16, edge_attr_4, src, dst, L1_gnn_Wfc1, L1_gnn_Wfc2, L1_gnn_Wsc0, L1_gnn_Wsc1, L1_gnn_Wl1_0, L1_gnn_Wl1_1, L1_gnn_Wl2_s, L1_gnn_Wl2_v, L1_gnn_Wa), axis=-1)
    x = _layernorm(x + _L2_gnn_ref(x, node_vec1, src, dst, edge_attr_4, edge_attr_10, L2_gnn_W_si0, L2_gnn_W_si1, L2_gnn_W_l1_0, L2_gnn_W_l1_1, L2_gnn_W_l2_00, L2_gnn_W_l2_10, L2_gnn_W_l2_01, L2_gnn_W_l2_11, L2_gnn_W_fc1, L2_gnn_W_fc2), axis=-1)
    x = _layernorm(x + _L3_gnn_ref(x, node_vec1, edge_attr_3, edge_attr_64, src, dst, L3_gnn_ln1_w0, L3_gnn_ln1_b0, L3_gnn_ln1_w1, L3_gnn_ln2_w0, L3_gnn_ln2_b0, L3_gnn_ln2_w1, L3_gnn_msrc_ws, L3_gnn_msrc_wv, L3_gnn_mdst_ws, L3_gnn_mdst_bs, L3_gnn_mdst_wv, L3_gnn_rw1, L3_gnn_rb1, L3_gnn_rg1, L3_gnn_rbe1, L3_gnn_rw2, L3_gnn_rb2, L3_gnn_rg2, L3_gnn_rbe2, L3_gnn_rw3, L3_gnn_roff, L3_gnn_lin_ws, L3_gnn_lin_bs, L3_gnn_lin_wv, L3_gnn_alpha_dot, L3_gnn_proj_ws, L3_gnn_proj_bs, L3_gnn_proj_wv, L3_gnn_f1_ws, L3_gnn_f1_bs, L3_gnn_f1_wv, L3_gnn_f2_ws, L3_gnn_f2_bs, L3_gnn_f2_wv), axis=-1)
    return x

_drawn_inputs = setup_inputs


def setup_inputs(seed=0):
    import zlib

    import numpy as np

    out = dict(_drawn_inputs(seed))
    spreads = {'L3_gnn_ln1_w0': (1.0, 0.6),
     'L3_gnn_ln1_b0': (0.0, 0.535),
     'L3_gnn_ln1_w1': (1.0, 0.6),
     'L3_gnn_ln2_w0': (1.0, 0.6),
     'L3_gnn_ln2_b0': (0.0, 0.8),
     'L3_gnn_ln2_w1': (1.0, 0.6),
     'L3_gnn_mdst_bs': (0.0, 0.8),
     'L3_gnn_rb1': (0.0, 0.1),
     'L3_gnn_rg1': (1.0, 0.2),
     'L3_gnn_rbe1': (0.0, 0.362),
     'L3_gnn_rb2': (0.0, 0.1),
     'L3_gnn_rg2': (1.0, 0.2),
     'L3_gnn_rbe2': (0.0, 0.411),
     'L3_gnn_lin_bs': (0.0, 0.634),
     'L3_gnn_proj_bs': (0.0, 0.1),
     'L3_gnn_f1_bs': (0.0, 0.8),
     'L3_gnn_f2_bs': (0.0, 0.445)}
    factors = {'edge_attr_10': 8.0,
     'edge_attr_16': 8.0,
     'edge_attr_4': 6.56,
     'edge_attr_8': 8.0,
     'L0_gnn_Wl1_0': 8.0,
     'L0_gnn_Wl1_1': 8.0,
     'L0_gnn_Wfc1': 8.0,
     'L0_gnn_Wfc2': 8.0,
     'L0_gnn_Wfc3': 8.0,
     'L0_gnn_Wl2_s': 8.0,
     'L0_gnn_Wl2_v': 8.0,
     'L0_gnn_Wa': 8.0,
     'L1_gnn_Wfc1': 8.0,
     'L1_gnn_Wfc2': 8.0,
     'L1_gnn_Wl1_0': 8.0,
     'L1_gnn_Wl1_1': 8.0,
     'L1_gnn_Wl2_s': 8.0,
     'L1_gnn_Wl2_v': 8.0,
     'L1_gnn_Wa': 8.0,
     'L2_gnn_W_l1_0': 8.0,
     'L2_gnn_W_l1_1': 8.0,
     'L2_gnn_W_l2_00': 8.0,
     'L2_gnn_W_l2_10': 8.0,
     'L2_gnn_W_l2_01': 8.0,
     'L2_gnn_W_l2_11': 8.0,
     'L2_gnn_W_fc1': 8.0,
     'L2_gnn_W_fc2': 7.585,
     'L3_gnn_alpha_dot': 3.676}
    for name, (base, spread) in spreads.items():
        noise = np.random.default_rng([zlib.crc32(name.encode()), seed]).standard_normal(out[name].shape)
        drawn = base * np.exp(spread * noise) if base else spread * noise
        out[name] = jnp.asarray(drawn.astype(out[name].dtype))
    for name, factor in factors.items():
        out[name] = (out[name] * factor).astype(out[name].dtype)
    return out
```

```python
from contextlib import ExitStack

import numpy as np

import concourse.bass as bass
from concourse import mybir

ALU = mybir.AluOpType
ACT = mybir.ActivationFunctionType
AX = mybir.AxisListType
F32 = mybir.dt.float32
I32 = mybir.dt.int32

P = 125
J = 2
LANES = 4
ROWS = P * J * LANES
S, V, U = 64, 96, 32
F = S + V
W = P * J
MEAN, Q, A, ROW = F, F + 1, F + 2, F + 4
EPS = 1e-5


def lane_steps(sem, phase, **names):
    t = {e: [sem(f"{phase}_{e}_steps_lane{n}") for n in range(LANES)] for e in names}
    t["names"] = names
    t["turn"] = sem(f"{phase}_turns")
    return t


def count_at(t, i, engine, step):
    names = t["names"][engine]
    return i * len(names) + names.index(step) + 1


def prime(eng, t, engine):
    for n in range(LANES):
        eng.sem_inc(t[engine][n], len(t["names"][engine]))


def gate(eng, t):
    eng.sem_inc(t["turn"], 1)


def staggered(order, part):
    steps = []
    for step, begin in order:
        for n in range(LANES):
            behind, at = divmod(begin + n * part, LANES * part)
            steps.append((at, int(behind), n, step))
    return [(step, n, behind) for at, behind, n, step in sorted(steps)]


def run_rounds(eng, rounds, order, part, steps):
    mine = [(step, n, behind) for step, n, behind in staggered(order, part) if step in steps]
    for step, n, behind in mine:
        if not behind:
            steps[step](n, 0)
    with eng.Fori(1, rounds) as i:
        for step, n, behind in mine:
            steps[step](n, i - behind)
    for step, n, behind in mine:
        if behind:
            steps[step](n, rounds - 1)


FFN_PE = ["ffn_turned", "ffn_hidden", "ffn_out"]
FFN_ACT = ["ffn_scaled", "ffn_copied", "ffn_sigmoid"]
FFN_DVE = ["ffn_measured", "ffn_merged", "ffn_squared", "ffn_widened", "ffn_attr", "ffn_normed",
           "ffn_gated", "ffn_added", "out_measured", "out_merged", "out_widened", "out_normed"]
FFN_POOL = ["ffn_root", "out_root"]


def ffn_buffers(sb, w, banks):
    f = dict(w=w, banks=banks)
    for name, shape in (
            ("stats", [P, LANES, 4, 6]),
            ("moments", [P, LANES, 4, 2]),
            ("square", [P, LANES, 2]),
            ("wide", [P, LANES, 4]),
            ("root", [P, LANES, 4]),
            ("root_a", [P, LANES, 4]),
            ("sn", [P, LANES, J, S + 1]),
            ("vn", [P, LANES, J, V]),
            ("s_t", [S + 1, LANES, W]),
            ("v_t", [V, LANES, W]),
            ("sig", [128, LANES, 2 * W]),
            ("hid", [128, LANES, W]),
            ("hid_v01", [128, LANES, W]),
            ("hid_v2", [S + 1, LANES, W]),
            ("y", [P, LANES, J, F]),
            ("y_stats", [P, LANES, J, 6]),
            ("y_moments", [P, LANES, J, 2]),
            ("y_wide", [P, LANES, J]),
            ("y_root", [P, LANES, J]),
    ):
        f[name] = sb("ffn_" + name, shape)
    return f


def ffn_measure(v, f, t, i, n, xs, xv):
    for j in range(J):
        v.bn_stats(f["stats"][:, n, j, :], xs[j])
        ins = v.bn_stats(f["stats"][:, n, J + j, :], xv[j])
    ins.then_inc(t["dve"][n], 1)


def ffn_merge(v, f, t, i, n):
    v.wait_ge(t["dve"][n], count_at(t, i, "dve", "ffn_measured"))
    gate(v, t)
    for k in range(2 * J):
        ins = v.bn_aggr(f["moments"][:, n, k, :], f["stats"][:, n, k, :])
    ins.then_inc(t["dve"][n], 1)


def ffn_square(v, f, t, i, n):
    v.wait_ge(t["dve"][n], count_at(t, i, "dve", "ffn_merged"))
    mv = f["moments"][:, n, J:2 * J, 0:1]
    v.tensor_tensor(f["square"][:, n, :].unsqueeze(2), mv, mv, ALU.mult)
    v.tensor_scalar(f["wide"][:, n, 0:J].unsqueeze(2), f["moments"][:, n, 0:J, 1:2], EPS, None,
                    ALU.add).then_inc(t["dve"][n], 1)


def ffn_widen(v, f, t, i, n):
    v.wait_ge(t["dve"][n], count_at(t, i, "dve", "ffn_squared"))
    v.scalar_tensor_tensor(f["wide"][:, n, J:2 * J].unsqueeze(2), f["moments"][:, n, J:2 * J, 1:2], EPS,
                           f["square"][:, n, :].unsqueeze(2), ALU.add, ALU.add).then_inc(t["dve"][n], 1)


def ffn_root_attr(v, f, t, i, n, attr):
    v.wait_ge(t["pool"][n], count_at(t, i, "pool", "ffn_root"))
    v.tensor_tensor(f["root_a"][:, n, :].rearrange("p (k j) -> p k j", j=J),
                    f["root"][:, n, :].rearrange("p (k j) -> p k j", j=J),
                    attr.unsqueeze(1).broadcast_to([P, 2, J]), ALU.mult).then_inc(t["dve"][n], 1)


def ffn_normalize(v, f, t, i, n, xs):
    v.wait_ge(t["dve"][n], count_at(t, i, "dve", "ffn_attr"))
    for j in range(J):
        ins = v.tensor_scalar(f["sn"][:, n, j, 0:S], xs[j], f["moments"][:, n, j, 0:1],
                              f["root_a"][:, n, j:j + 1], ALU.subtract, ALU.mult)
    ins.then_inc(t["dve"][n], 1)


def ffn_gates(v, f, t, i, n):
    a, b = f["banks"][2 * n], f["banks"][2 * n + 1]
    v.wait_ge(t["act"][n], count_at(t, i, "act", "ffn_sigmoid"))
    v.tensor_tensor(f["hid"][:, n, :], b[:, 0:W], f["sig"][:, n, 0:W], ALU.mult)
    v.tensor_tensor(f["hid_v01"][:, n, :], a[:, 0:W], f["sig"][:, n, W:2 * W], ALU.mult)
    v.tensor_tensor(f["hid_v2"][0:S, n, :], a[0:S, W:2 * W], f["sig"][0:S, n, W:2 * W],
                    ALU.mult).then_inc(t["dve"][n], 1)


def ffn_add(v, f, t, i, n, attr_of, u):
    b = f["banks"][2 * n + 1]
    v.wait_ge(t["pe"][n], count_at(t, i, "pe", "ffn_out"))
    for j in range(J):
        ins = v.scalar_tensor_tensor(f["y"][:, n, j, :], b[0:P, j * F:(j + 1) * F], attr_of(j), u[j],
                                     ALU.mult, ALU.add)
    ins.then_inc(t["dve"][n], 1)


def out_measure(v, f, t, i, n):
    v.wait_ge(t["dve"][n], count_at(t, i, "dve", "ffn_added"))
    for j in range(J):
        ins = v.bn_stats(f["y_stats"][:, n, j, :], f["y"][:, n, j, :])
    ins.then_inc(t["dve"][n], 1)


def out_merge(v, f, t, i, n):
    v.wait_ge(t["dve"][n], count_at(t, i, "dve", "out_measured"))
    gate(v, t)
    for j in range(J):
        ins = v.bn_aggr(f["y_moments"][:, n, j, :], f["y_stats"][:, n, j, :])
    ins.then_inc(t["dve"][n], 1)


def out_widen(v, f, t, i, n):
    v.wait_ge(t["dve"][n], count_at(t, i, "dve", "out_merged"))
    v.tensor_scalar(f["y_wide"][:, n, :].unsqueeze(2), f["y_moments"][:, n, :, 1:2], EPS, None,
                    ALU.add).then_inc(t["dve"][n], 1)


def ffn_finish(v, f, t, i, n, out):
    v.wait_ge(t["pool"][n], count_at(t, i, "pool", "out_root"))
    for j in range(J):
        ins = v.tensor_scalar(out[j], f["y"][:, n, j, :], f["y_moments"][:, n, j, 0:1],
                              f["y_root"][:, n, j:j + 1], ALU.subtract, ALU.mult)
    ins.then_inc(t["dve"][n], 1)


def ffn_roots(p, f, t, i, n):
    p.wait_ge(t["dve"][n], count_at(t, i, "dve", "ffn_widened"))
    gate(p, t)
    p.tensor_tensor(f["root"][:, n, :], f["wide"][:, n, :], f["w"]["half"][:, 0:2 * J], ALU.pow
                    ).then_inc(t["pool"][n], 1)


def ffn_out_roots(p, f, t, i, n):
    p.wait_ge(t["dve"][n], count_at(t, i, "dve", "out_widened"))
    gate(p, t)
    p.tensor_tensor(f["y_root"][:, n, :], f["y_wide"][:, n, :], f["w"]["half"][:, 0:J], ALU.pow
                    ).then_inc(t["pool"][n], 1)


def ffn_scale(act, f, t, i, n, xv, attr):
    act.wait_ge(t["dve"][n], count_at(t, i, "dve", "ffn_attr"))
    act.activation(f["sn"][:, n, :, S:S + 1], attr.unsqueeze(2), ACT.Copy)
    for j in range(J):
        ins = act.activation(f["vn"][:, n, j, :], xv[j], ACT.Copy, scale=f["root_a"][:, n, J + j:J + j + 1])
    ins.then_inc(t["act"][n], 1)


def ffn_copy_turned(act, f, t, i, n):
    a = f["banks"][2 * n]
    act.wait_ge(t["pe"][n], count_at(t, i, "pe", "ffn_turned"))
    act.activation(f["s_t"][:, n, :], a[0:S + 1, 0:W], ACT.Copy)
    act.activation(f["v_t"][:, n, :], a[0:V, W:2 * W], ACT.Copy).then_inc(t["act"][n], 1)


def ffn_sigmoid(act, f, t, i, n):
    act.wait_ge(t["pe"][n], count_at(t, i, "pe", "ffn_hidden"))
    act.activation(f["sig"][:, n, :], f["banks"][2 * n + 1][:, 0:2 * W], ACT.Sigmoid
                   ).then_inc(t["act"][n], 1)


def ffn_turn(pe, f, t, i, n):
    a = f["banks"][2 * n]
    pe.wait_ge(t["dve"][n], count_at(t, i, "dve", "ffn_normed"))
    gate(pe, t)
    pe.wait_ge(t["act"][n], count_at(t, i, "act", "ffn_scaled"))
    gate(pe, t)
    for j in range(J):
        pe.transpose(a[0:S + 1, j * P:(j + 1) * P], f["sn"][:, n, j, :], f["w"]["ident"][0:P, 0:P])
        ins = pe.transpose(a[0:V, W + j * P:W + (j + 1) * P], f["vn"][:, n, j, :], f["w"]["ident"][0:P, 0:P])
    ins.then_inc(t["pe"][n], 1)


def ffn_hidden(pe, f, t, i, n):
    a, b = f["banks"][2 * n], f["banks"][2 * n + 1]
    pe.wait_ge(t["act"][n], count_at(t, i, "act", "ffn_copied"))
    gate(pe, t)
    f1s, f1v = f["w"]["f1_s"], f["w"]["f1_v"]
    pe.matmul(b[:, 0:W], f1s[:, 0:128], f["s_t"][:, n, :], start=True, stop=True)
    pe.matmul(b[:, W:2 * W], f1s[:, 128:256], f["s_t"][:, n, :], start=True, stop=True)
    pe.matmul(a[:, 0:W], f1v[:, 0:128], f["v_t"][:, n, :], start=True, stop=True)
    pe.matmul(a[0:S, W:2 * W], f1v[:, 128:192], f["v_t"][:, n, :], start=True, stop=True
              ).then_inc(t["pe"][n], 1)


def ffn_out(pe, f, t, i, n):
    b = f["banks"][2 * n + 1]
    pe.wait_ge(t["dve"][n], count_at(t, i, "dve", "ffn_gated"))
    gate(pe, t)
    for j in range(J):
        c, o = slice(j * P, (j + 1) * P), j * F
        pe.matmul(b[0:P, o:o + S], f["hid"][:, n, c], f["w"]["f2_s"][:, :], start=True, stop=True)
        pe.matmul(b[0:P, o + S:o + F], f["hid_v01"][:, n, c], f["w"]["f2_v01"][:, :], start=False,
                  stop=True, skip_group_check=True)
        ins = pe.matmul(b[0:P, o:o + F], f["hid_v2"][:, n, c], f["w"]["f2_v2"][:, :], start=False, stop=True,
                        skip_group_check=True)
    ins.then_inc(t["pe"][n], 1)


def lin_names(l):
    return [("L0_gnn_Wsc0", "L0_gnn_Wsc1", "L0_gnn_Wl1_0", "L0_gnn_Wl1_1"),
            ("L1_gnn_Wsc0", "L1_gnn_Wsc1", "L1_gnn_Wl1_0", "L1_gnn_Wl1_1"),
            ("L2_gnn_W_si0", "L2_gnn_W_si1", "L2_gnn_W_l1_0", "L2_gnn_W_l1_1")][l]



def prepare_weights(nc, sem, keep, sb, banks, inp, w):
    loaded = sem("weights_loaded")
    built = sem("weights_built")
    ident_made = sem("ident_made")
    sums_made = sem("column_sums_made")

    for name, shape in (("ident", [128, 128]), ("mod3", [V, 3]), ("half", [P, 16]), ("f2_s", [128, S]),
                        ("f1_s", [S + 1, 256]), ("f1_v", [V, 192]), ("f2_v01", [128, V]), ("f2_v2", [S + 1, F]),
                        ("proj_b", [P, S]),
                        *((f"{k}{l}", shape) for l in range(3) for k, shape in (
                            ("self_s", [S, S]), ("self_v", [V + 1, F]), ("lin_s", [S, 2 * S]), ("lin_v", [V, V])))):
        w[name] = keep(name, shape)
    w["minus_one"] = sb("minus_one", [V, V + 1])
    w["b0_column"] = sb("b0_column", [S, S + 1])
    loads = []

    def raw(name, shape, src, part=None):
        t = sb("raw_" + name, shape)
        loads.append((t[:, :], src))
        return t

    def thrice(name, src):
        t = sb("raw3_" + name, [V, src.shape[1]])
        loads.append((t[:, :], src.unsqueeze(1).broadcast_to([U, 3, src.shape[1]])))
        return t

    krons = []
    plain = []
    for l in range(3):
        n = lin_names(l)
        r = raw(n[0], [S, S], inp[n[0]])
        plain.append((w[f"self_s{l}"][:, :], r[:, :], S ** -0.5))
        krons.append((w[f"self_v{l}"][0:V, S:F], thrice(n[1], inp[n[1]]), U ** -0.5, False))
        r = raw(n[2], [S, S], inp[n[2]])
        plain.append((w[f"lin_s{l}"][:, 0:S], r[:, :], S ** -0.5))
        plain.append((w[f"lin_s{l}"][:, S:2 * S], r[:, :], S ** -0.5))
        krons.append((w[f"lin_v{l}"][:, :], thrice(n[3], inp[n[3]]), U ** -0.5, False))

    f1 = raw("f1_ws", [S, 192], inp["L3_gnn_f1_ws"])
    w0 = raw("ln2_w0", [S, 1], inp["L3_gnn_ln2_w0"].unsqueeze(1))
    b0 = raw("ln2_b0", [S, 1], inp["L3_gnn_ln2_b0"].unsqueeze(1))
    f1v = thrice("f1_wv", inp["L3_gnn_f1_wv"])
    w1 = thrice("ln2_w1", inp["L3_gnn_ln2_w1"].unsqueeze(1))
    f2v = sb("raw_f2_wv", [128, U])
    loads.append((f2v[0:64, :], inp["L3_gnn_f2_wv"]))
    loads.append((f2v[64:128, :], inp["L3_gnn_f2_wv"]))
    loads.append((w["f2_s"][:, :], inp["L3_gnn_f2_ws"]))
    f1b = sb("raw_f1_bs", [S + 1, 192])
    loads.append((f1b[S:S + 1, :], inp["L3_gnn_f1_bs"].unsqueeze(0)))
    f2b = sb("raw_f2_bs", [S + 1, S])
    loads.append((f2b[S:S + 1, :], inp["L3_gnn_f2_bs"].unsqueeze(0)))
    loads.append((w["proj_b"][:, :], inp["L3_gnn_proj_bs"].unsqueeze(0).broadcast_to([P, S])))

    with nc.Block() as block:
        @block.sync
        def _(sp):
            for dst, src in loads:
                sp.dma_start(dst, src).then_inc(loaded, 16)

        @block.gpsimd
        def _(p):
            p.memset(w["ident"][:, :], 0.0).then_inc(ident_made, 1)
            p.wait_ge(ident_made, 1)
            p.affine_select(out=w["ident"][:, :], in_=w["ident"][:, :], compare_op=ALU.not_equal, fill=1.0,
                            base=0, pattern=[[-1, 128]], channel_multiplier=1).then_inc(ident_made, 1)

        @block.vector
        def _(v):
            v.memset(w["half"][:, :], -0.5)
            v.memset(w["minus_one"][:, :], 0.0)
            v.memset(w["f2_v01"][:, :], 0.0)
            v.memset(w["f2_v2"][:, :], 0.0)
            v.memset(w["b0_column"][:, :], 0.0)
            for l in range(3):
                v.memset(w[f"self_v{l}"][:, :], 0.0)
            v.wait_ge(ident_made, 2)
            v.tensor_reduce(w["mod3"][:, :], w["ident"][0:V, 0:V].rearrange("p (u c) -> p c u", c=3), AX.X,
                            ALU.add).then_inc(built, 1)
            v.wait_ge(built, 1)
            v.memset(w["minus_one"][:, V:V + 1], -1.0)
            v.wait_ge(loaded, 16 * len(loads))
            for dst, src, k in plain:
                v.tensor_scalar(dst, src, k, None, ALU.mult)
            for dst, src, k, outer in krons:
                for c in range(3):
                    v.tensor_scalar(dst.rearrange("p (w c) -> p c w", c=3)[:, c, :], src[:, :],
                                    w["mod3"][:, c:c + 1], k, ALU.mult, ALU.mult)
            for c in range(3):
                v.tensor_scalar(w["f1_v"][:, c * 64:(c + 1) * 64], f1v[:, :], w["mod3"][:, c:c + 1], w1[:, 0:1],
                                ALU.mult, ALU.mult)
            for c in range(2):
                h = slice(c * 64, (c + 1) * 64)
                v.tensor_copy(w["f2_v01"][h, :].rearrange("p (k c) -> p c k", c=3)[:, c, :], f2v[h, :])
            v.tensor_copy(w["f2_v2"][0:S, S:F].rearrange("p (k c) -> p c k", c=3)[:, 2, :], f2v[0:64, :])
            v.tensor_copy(w["f2_v2"][S:S + 1, 0:S], f2b[S:S + 1, :])
            v.tensor_scalar(w["f1_s"][0:S, 0:192], f1[:, :], w0[:, 0:1], None, ALU.mult)
            v.tensor_scalar(w["f1_s"][0:S, 192:256], f1[:, 128:192], w0[:, 0:1], None, ALU.mult)
            v.tensor_copy(w["b0_column"][:, S:S + 1], b0[:, :]).then_inc(built, 1)
            v.wait_ge(sums_made, 1)
            for l in range(3):
                v.tensor_copy(w[f"self_v{l}"][V:V + 1, :], banks[l][V:V + 1, 0:F])
            v.tensor_tensor(w["f1_s"][S:S + 1, 0:192], banks[3][S:S + 1, 0:192], f1b[S:S + 1, :], ALU.add)
            v.tensor_tensor(w["f1_s"][S:S + 1, 192:256], banks[3][S:S + 1, 128:192], f1b[S:S + 1, 128:192],
                            ALU.add).then_inc(built, 1)

        @block.tensor
        def _(pe):
            pe.wait_ge(built, 2)
            for l in range(3):
                pe.matmul(banks[l][0:V + 1, 0:S], w["minus_one"][0:S, :], w[f"self_s{l}"][:, :],
                          start=True, stop=True)
                pe.matmul(banks[l][0:V + 1, S:F], w["minus_one"][:, :], w[f"self_v{l}"][0:V, S:F],
                          start=True, stop=True)
            pe.matmul(banks[3][0:S + 1, 0:192], w["b0_column"][:, :], f1[:, :],
                      start=True, stop=True).then_inc(sums_made, 1)


def all_nodes(nc, sem, sb, banks, inp, w, ffn, tables, out, nodes):
    rounds = nodes // ROWS
    own = nodes // P
    T = LANES * J
    names = dict(pe=[], act=[], dve=[], pool=["attr_copied"])
    for l in range(3):
        names["pe"] += [f"turned{l}", f"multiplied{l}"]
        names["act"] += [f"copied{l}"]
        names["dve"] += [f"added{l}", f"measured{l}", f"merged{l}", f"widened{l}"]
    names["dve"] += ["x3", "shifted"] + FFN_DVE
    names["pool"] += ["root3", "doubled"] + FFN_POOL
    names["pe"] += FFN_PE
    names["act"] += FFN_ACT
    t = lane_steps(sem, "nodes", **names)
    x_loaded = [sem(f"nodes_x_loaded_lane{n}") for n in range(LANES)]
    stored = [[sem(f"nodes_table{l}_stored_lane{n}") for n in range(LANES)] for l in range(4)]
    out_stored = [sem(f"nodes_out_stored_lane{n}") for n in range(LANES)]
    attr_loaded = sem("nodes_attr_loaded")
    ready = sem("nodes_constants_ready")
    part = 11.62
    order = [("load_x", 0.0), ("keep_busy0", 2.24), ("store0", 2.7), ("attr", 2.8), ("turn0", 3.0),
             ("copy0", 4.2), ("multiply0", 5.1), ("add0", 6.4), ("measure0", 7.1), ("merge0", 7.8),
             ("keep_busy1", 7.87), ("widen0", 8.0), ("store1", 8.3), ("turn1", 8.4), ("keep_busy2", 8.86),
             ("copy1", 9.2), ("multiply1", 10.1), ("add1", 11.4), ("measure1", 12.1), ("keep_busy3", 12.42),
             ("merge1", 12.8), ("widen1", 13.0), ("store2", 13.3), ("turn2", 13.4), ("copy2", 14.2),
             ("multiply2", 15.1), ("add2", 16.4), ("measure2", 17.1), ("merge2", 17.8), ("widen2", 18.1),
             ("store3", 18.4), ("root3", 18.6), ("divide", 19.4), ("shift", 20.1), ("measure", 20.4),
             ("double", 21.2), ("merge", 22.2), ("square", 24.4), ("widen", 24.6), ("roots", 24.9),
             ("root_attr", 26.0), ("normalize", 26.2), ("scale", 26.8), ("ffn_turn", 27.7), ("ffn_copy", 28.5),
             ("hidden", 29.4), ("sigmoid", 31.4), ("gates", 32.6), ("ffn_out", 34.2), ("residual", 36.0),
             ("out_measure", 36.7), ("out_merge", 37.4), ("out_widen", 37.6), ("out_roots", 38.0),
             ("finish", 38.7), ("store_out", 39.5)]
    fill = [(0, 0, 3), (0, 0, 2), (0, 1, 5), (0, 0, 4)]
    attr = sb("node_attr", [P, own])
    z = sb("nodes_z", [P, 4, T, ROW])
    s_t = sb("nodes_s_t", [S, LANES, W])
    v_t = sb("nodes_v_t", [V + 1, LANES, W])
    root3 = sb("nodes_root3", [P, LANES, J])
    x3 = sb("nodes_x3", [P, T, F])
    xps = sb("nodes_xps", [P, T, S])
    u = sb("nodes_u", [P, T, F])
    res = sb("nodes_res", [P, T, F])
    x_view = inp["x"].rearrange("(p r) f -> p r f", p=P)
    out_view = out.rearrange("(p r) f -> p r f", p=P)
    table_view = [x.rearrange("(p r) f -> p r f", p=P) for x in tables]

    def tiles(n):
        return slice(J * n, J * n + J)

    with nc.Block() as block:
        @block.sync
        def _(sp):
            for n in range(LANES):
                for l in range(4):
                    sp.sem_inc(stored[l][n], 16)
                sp.sem_inc(out_stored[n], 16)
            sp.dma_start(attr[:, :], inp["node_vec1"].rearrange("(p r) o -> p (r o)", p=P)).then_inc(attr_loaded, 16)
            sp.wait_ge(ready, 2)

            def load_x(n, i):
                sp.wait_ge(t["dve"][n], count_at(t, i, "dve", "added0"))
                gate(sp, t)
                sp.wait_ge(stored[0][n], 16 * i + 16)
                gate(sp, t)
                sp.dma_start(z[:, 0, tiles(n), 0:F], x_view[:, bass.ds(i * T + J * n, J), :]
                             ).then_inc(x_loaded[n], 16)

            def store_table(l):
                def store(n, i):
                    if l:
                        sp.wait_ge(t["dve"][n], count_at(t, i + 1, "dve", f"widened{l - 1}"))
                        gate(sp, t)
                    else:
                        sp.wait_ge(t["pool"][n], count_at(t, i + 1, "pool", "attr_copied"))
                        gate(sp, t)
                        sp.wait_ge(x_loaded[n], 16 * i + 16)
                        gate(sp, t)
                    sp.dma_start(table_view[l][:, bass.ds(i * T + J * n, J), :], z[:, l, tiles(n), :]
                                 ).then_inc(stored[l][n], 16)
                return store

            def store_out(n, i):
                sp.wait_ge(t["dve"][n], count_at(t, i + 1, "dve", "out_normed"))
                gate(sp, t)
                sp.dma_start(out_view[:, bass.ds(i * T + J * n, J), :], res[:, tiles(n), :]
                             ).then_inc(out_stored[n], 16)

            run_rounds(sp, rounds, order, part, dict(load_x=load_x, store_out=store_out,
                                               **{f"store{l}": store_table(l) for l in range(4)}))
            for n in range(LANES):
                for l in range(4):
                    sp.wait_ge(stored[l][n], 16 * rounds + 16)
                sp.wait_ge(out_stored[n], 16 * rounds + 16)

        @block.gpsimd
        def _(p):
            prime(p, t, "pool")
            p.wait_ge(attr_loaded, 16)
            p.wait_ge(ready, 2)

            def copy_attr(n, i):
                p.wait_ge(t["dve"][n], count_at(t, i, "dve", "ffn_added"))
                gate(p, t)
                for l in range(4):
                    p.wait_ge(stored[l][n], 16 * i + 16)
                    gate(p, t)
                p.tensor_copy(z[:, :, tiles(n), A:A + 1],
                              attr[:, bass.ds(i * T + J * n, J)].unsqueeze(1).unsqueeze(3)
                              .broadcast_to([P, 4, J, 1])).then_inc(t["pool"][n], 1)

            def take_root3(n, i):
                p.wait_ge(t["dve"][n], count_at(t, i + 1, "dve", "widened2"))
                gate(p, t)
                p.tensor_tensor(root3[:, n, :].unsqueeze(2), z[:, 3, tiles(n), Q:Q + 1],
                                w["half"][:, 0:J].unsqueeze(2), ALU.pow).then_inc(t["pool"][n], 1)

            def double(n, i):
                p.wait_ge(t["dve"][n], count_at(t, i + 1, "dve", "shifted"))
                gate(p, t)
                p.tensor_tensor(u[:, tiles(n), 0:S], x3[:, tiles(n), 0:S], xps[:, tiles(n), :], ALU.add)
                p.tensor_tensor(u[:, tiles(n), S:F], x3[:, tiles(n), S:F], x3[:, tiles(n), S:F], ALU.add
                                ).then_inc(t["pool"][n], 1)

            run_rounds(p, rounds, order, part, dict(
                attr=copy_attr, root3=take_root3, double=double,
                roots=lambda n, i: ffn_roots(p, ffn, t, i + 1, n),
                out_roots=lambda n, i: ffn_out_roots(p, ffn, t, i + 1, n)))

        @block.vector
        def _(v):
            v.memset(z[:, :, :, MEAN:ROW], 0.0).then_inc(ready, 1)
            v.memset(ffn["hid_v2"][S:S + 1, :, :], 1.0)
            v.wait_ge(ready, 1)
            v.memset(z[:, 0, :, Q:Q + 1], 1.0).then_inc(ready, 1)
            prime(v, t, "dve")

            def add(l):
                def step(n, i):
                    v.wait_ge(t["pe"][n], count_at(t, i + 1, "pe", f"multiplied{l}"))
                    v.wait_ge(t["pool"][n], count_at(t, i + 1, "pool", "attr_copied"))
                    for j in range(J):
                        k = J * n + j
                        ins = v.scalar_tensor_tensor(z[:, l + 1, k, 0:F], banks[2 * n + 1][0:P, j * F:(j + 1) * F],
                                                     z[:, l, k, A:A + 1], z[:, l, k, 0:F], ALU.mult, ALU.add)
                    ins.then_inc(t["dve"][n], 1)
                return step

            def measure(l):
                def step(n, i):
                    v.wait_ge(t["dve"][n], count_at(t, i + 1, "dve", f"added{l}"))
                    for j in range(J):
                        ins = v.bn_stats(ffn["y_stats"][:, n, j, :], z[:, l + 1, J * n + j, 0:F])
                    ins.then_inc(t["dve"][n], 1)
                return step

            def merge(l):
                def step(n, i):
                    v.wait_ge(t["dve"][n], count_at(t, i + 1, "dve", f"measured{l}"))
                    gate(v, t)
                    for j in range(J):
                        ins = v.bn_aggr(z[:, l + 1, J * n + j, MEAN:Q + 1], ffn["y_stats"][:, n, j, :])
                    ins.then_inc(t["dve"][n], 1)
                return step

            def widen(l):
                def step(n, i):
                    v.wait_ge(t["dve"][n], count_at(t, i + 1, "dve", f"merged{l}"))
                    v.scalar_tensor_tensor(z[:, l + 1, tiles(n), Q:Q + 1], z[:, l, tiles(n), Q:Q + 1], EPS,
                                           z[:, l + 1, tiles(n), Q:Q + 1], ALU.mult, ALU.add
                                           ).then_inc(t["dve"][n], 1)
                return step

            def divide(n, i):
                v.wait_ge(t["pool"][n], count_at(t, i + 1, "pool", "root3"))
                for j in range(J):
                    k = J * n + j
                    ins = v.tensor_scalar(x3[:, k, :], z[:, 3, k, 0:F], z[:, 3, k, MEAN:MEAN + 1],
                                          root3[:, n, j:j + 1], ALU.subtract, ALU.mult)
                ins.then_inc(t["dve"][n], 1)

            def shift(n, i):
                v.wait_ge(t["dve"][n], count_at(t, i + 1, "dve", "x3"))
                v.tensor_tensor(xps[:, tiles(n), :], x3[:, tiles(n), 0:S], w["proj_b"][:, :].unsqueeze(1)
                                .broadcast_to([P, J, S]), ALU.add).then_inc(t["dve"][n], 1)

            def measure_parts(n, i):
                v.wait_ge(t["dve"][n], count_at(t, i + 1, "dve", "shifted"))
                ffn_measure(v, ffn, t, i + 1, n, [xps[:, J * n + j, :] for j in range(J)],
                            [x3[:, J * n + j, S:F] for j in range(J)])

            def root_attr(n, i):
                ffn_root_attr(v, ffn, t, i + 1, n, z[:, 0, tiles(n), A:A + 1].rearrange("p j o -> p (j o)"))

            def normalize(n, i):
                ffn_normalize(v, ffn, t, i + 1, n, [xps[:, J * n + j, :] for j in range(J)])

            def residual(n, i):
                v.wait_ge(t["pool"][n], count_at(t, i + 1, "pool", "doubled"))
                ffn_add(v, ffn, t, i + 1, n, lambda j: z[:, 0, J * n + j, A:A + 1],
                        [u[:, J * n + j, :] for j in range(J)])

            def finish(n, i):
                v.wait_ge(out_stored[n], 16 * i + 16)
                ffn_finish(v, ffn, t, i + 1, n, [res[:, J * n + j, :] for j in range(J)])

            by_layer = {}
            for l in range(3):
                by_layer.update({f"add{l}": add(l), f"measure{l}": measure(l), f"merge{l}": merge(l),
                                 f"widen{l}": widen(l)})
            run_rounds(v, rounds, order, part, dict(
                **by_layer, divide=divide, shift=shift, measure=measure_parts,
                merge=lambda n, i: ffn_merge(v, ffn, t, i + 1, n), square=lambda n, i: ffn_square(v, ffn, t, i + 1, n),
                widen=lambda n, i: ffn_widen(v, ffn, t, i + 1, n), root_attr=root_attr, normalize=normalize,
                gates=lambda n, i: ffn_gates(v, ffn, t, i + 1, n), residual=residual,
                out_measure=lambda n, i: out_measure(v, ffn, t, i + 1, n),
                out_merge=lambda n, i: out_merge(v, ffn, t, i + 1, n),
                out_widen=lambda n, i: out_widen(v, ffn, t, i + 1, n), finish=finish))

        @block.scalar
        def _(act):
            prime(act, t, "act")

            def copy(l):
                def copy_turned(n, i):
                    act.wait_ge(t["pe"][n], count_at(t, i + 1, "pe", f"turned{l}"))
                    act.activation(s_t[:, n, :], banks[2 * n][0:S, 0:W], ACT.Copy)
                    act.activation(v_t[:, n, :], banks[2 * n][0:V + 1, W:2 * W], ACT.Copy
                                   ).then_inc(t["act"][n], 1)
                return copy_turned

            def scale(n, i):
                ffn_scale(act, ffn, t, i + 1, n, [x3[:, J * n + j, S:F] for j in range(J)],
                          z[:, 0, tiles(n), A:A + 1].rearrange("p j o -> p (j o)"))

            run_rounds(act, rounds, order, part, dict(
                copy0=copy(0), copy1=copy(1), copy2=copy(2), scale=scale,
                ffn_copy=lambda n, i: ffn_copy_turned(act, ffn, t, i + 1, n),
                sigmoid=lambda n, i: ffn_sigmoid(act, ffn, t, i + 1, n)))

        @block.tensor
        def _(pe):
            prime(pe, t, "pe")
            ident = w["ident"][0:P, 0:P]

            def keep_busy(k):
                lead, odd, count = fill[k]

                def step(n, i):
                    for _ in range(count):
                        pe.matmul(banks[2 * ((n + lead) % LANES) + odd][:, 0:128], w["ident"][:, :], w["ident"][:, :],
                                  start=True, stop=True)
                return step

            def turn(l):
                def turn_rows(n, i):
                    if l == 0:
                        pe.wait_ge(x_loaded[n], 16 * i + 16)
                        gate(pe, t)
                        pe.wait_ge(t["dve"][n], count_at(t, i, "dve", "ffn_added"))
                    else:
                        pe.wait_ge(t["dve"][n], count_at(t, i + 1, "dve", f"merged{l - 1}"))
                    gate(pe, t)
                    for j in range(J):
                        k = J * n + j
                        pe.transpose(banks[2 * n][0:S, j * P:(j + 1) * P], z[:, l, k, 0:S], ident)
                        ins = pe.transpose(banks[2 * n][0:V + 1, W + j * P:W + (j + 1) * P], z[:, l, k, S:F + 1],
                                           ident)
                    ins.then_inc(t["pe"][n], 1)
                return turn_rows

            def multiply(l):
                def multiply_rows(n, i):
                    pe.wait_ge(t["act"][n], count_at(t, i + 1, "act", f"copied{l}"))
                    gate(pe, t)
                    for j in range(J):
                        c, o = slice(j * P, (j + 1) * P), j * F
                        pe.matmul(banks[2 * n + 1][0:P, o:o + S], s_t[:, n, c], w[f"self_s{l}"][:, :],
                                  start=True, stop=True)
                        ins = pe.matmul(banks[2 * n + 1][0:P, o:o + F], v_t[:, n, c], w[f"self_v{l}"][:, :],
                                        start=False, stop=True, skip_group_check=True)
                    ins.then_inc(t["pe"][n], 1)
                return multiply_rows

            run_rounds(pe, rounds, order, part, dict(
                **{f"keep_busy{k}": keep_busy(k) for k in range(len(fill))},
                **{f"turn{l}": turn(l) for l in range(3)}, **{f"multiply{l}": multiply(l) for l in range(3)},
                ffn_turn=lambda n, i: ffn_turn(pe, ffn, t, i + 1, n),
                hidden=lambda n, i: ffn_hidden(pe, ffn, t, i + 1, n),
                ffn_out=lambda n, i: ffn_out(pe, ffn, t, i + 1, n)))


def edge_weights(nc, sem, sb, inp, w, l):
    loaded = sem(f"edge{l}_weights_loaded")
    zeroed = sem(f"edge{l}_weights_zeroed")
    loads = []

    def raw(name, shape, src, at=None):
        t = sb(f"edge{l}_raw_{name}", shape)
        loads.append((t[:, :] if at is None else t[at, :], src))
        return t

    n = f"L{l}_gnn_"
    if l < 2:
        first, last = inp[n + "Wfc1"], inp[n + ("Wfc3" if l == 0 else "Wfc2")]
        s_s, s_v = inp[n + "Wl2_s"][0:S, :], inp[n + "Wl2_s"][S:S + U, :]
        v_s, v_v = inp[n + "Wl2_v"][0:S, :], inp[n + "Wl2_v"][S:S + U, :]
        wa = inp[n + "Wa"]
        fan = (S + U) ** -0.5 * (32.0 ** -0.5 if l == 0 else 1.0)
        last_factor = S ** -0.5
    else:
        first, last = inp[n + "W_fc1"], inp[n + "W_fc2"]
        s_s, s_v, v_s, v_v = (inp[n + "W_l2_" + k] for k in ("00", "10", "01", "11"))
        wa = None
        fan = (S + U) ** -0.5 * 16.0 ** -0.5 * 0.5
        last_factor = 2.0 ** 0.5 * 100 ** -0.5
    basis, hid = first.shape
    w["fc1"] = raw("fc1", [basis, hid], first)
    w["fc2"] = raw("fc2", [S, S], inp[n + "Wfc2"]) if l == 0 else None
    r_last = raw("last", [hid, 192], last)
    w["fc_last"] = sb(f"edge{l}_fc_last", [hid, 128 + 2 * V])
    r_ss = raw("s_s", [128, S], s_s, slice(0, S))
    r_vs = raw("v_s", [128, U], v_s, slice(S, 128))
    r_sv = raw("s_v", [V, S], s_v.unsqueeze(1).broadcast_to([U, 3, S]))
    r_vv = raw("v_v", [V, U], v_v.unsqueeze(1).broadcast_to([U, 3, U]))
    if wa is not None:
        r_wa = raw("wa_s", [S, 1], wa[0:S, :])
        r_wav = raw("wa_v", [V, 1], wa[S:S + U, :].unsqueeze(1).broadcast_to([U, 3, 1]))
    w["msg_a"] = sb(f"edge{l}_msg_a", [128, 1 + S + U])
    w["msg_c"] = sb(f"edge{l}_msg_c", [V, V])
    w["msg_d"] = sb(f"edge{l}_msg_d", [V, 3 * (1 + S)])

    with nc.Block() as block:
        @block.sync
        def _(sp):
            for dst, src in loads:
                sp.dma_start(dst, src).then_inc(loaded, 16)

        @block.vector
        def _(v):
            v.memset(w["msg_a"][:, :], 0.0)
            v.memset(w["msg_d"][:, :], 0.0).then_inc(zeroed, 1)
            v.wait_ge(zeroed, 1)
            v.wait_ge(loaded, 16 * len(loads))
            v.tensor_scalar(w["fc_last"][:, 0:128], r_last[:, 0:128], last_factor, None, ALU.mult)
            for k in range(2):
                v.tensor_scalar(w["fc_last"][:, 128 + k * V:128 + (k + 1) * V].rearrange("p (u c) -> p u c", c=3),
                                r_last[:, 128 + k * U:128 + (k + 1) * U].unsqueeze(2).broadcast_to([hid, U, 3]),
                                last_factor, None, ALU.mult)
            v.tensor_scalar(w["msg_a"][0:S, 1:1 + S], r_ss[0:S, :], fan, None, ALU.mult)
            v.tensor_scalar(w["msg_a"][S:128, 1 + S:1 + S + U], r_vs[S:128, :], fan, None, ALU.mult)
            if wa is not None:
                v.tensor_scalar(w["msg_a"][0:S, 0:1], r_wa[:, :], fan, None, ALU.mult)
            for c in range(3):
                m = w["mod3"][:, c:c + 1]
                v.tensor_scalar(w["msg_c"][:, :].rearrange("p (w c) -> p c w", c=3)[:, c, :], r_vv[:, :], m, fan,
                                ALU.mult, ALU.mult)
                o = c * (1 + S)
                v.tensor_scalar(w["msg_d"][:, o + 1:o + 1 + S], r_sv[:, :], m, fan * 3 ** -0.5, ALU.mult, ALU.mult)
                if wa is not None:
                    v.tensor_scalar(w["msg_d"][:, o:o + 1], r_wav[:, :], m, fan * 3 ** -0.5, ALU.mult, ALU.mult)
    return basis, hid


def edge_index(nc, sem, sb, scratch, banks, inp, w, nodes, edges):
    index = {}
    tiles = edges // P
    pairs = tiles // J
    padded = tiles + LANES * J
    index["before"] = sb("dst_before", [P, padded])
    index["dst_f"] = sb("dst_f", [P, padded])
    index["src_i"] = sb("src_i", [P, padded], I32)
    index["dst_i"] = sb("dst_i", [P, padded], I32)
    index["into_i"] = sb("into_i", [P, padded], I32)
    rows = [scratch(f"{k}_rows", [pairs, W], I32) for k in ("src", "dst", "next")]
    rows_f = [scratch(f"{k}_rows_f", [pairs, W]) for k in ("src", "dst", "next")]
    nxt = scratch("dst_next", [P, padded])
    same = scratch("dst_same", [P, padded])
    loaded = sem("index_loaded")
    zeroed = sem("index_zeroed")
    floats = sem("index_floats")
    turned = sem("index_turned")
    split = sem("index_split")
    moved = sem("index_moved")
    row_view = [inp[k].rearrange("(q c) -> q c", c=W) for k in ("src", "dst")]
    dst = inp["dst"]
    with nc.Block() as block:
        @block.sync
        def _(sp):
            for k in range(2):
                sp.dma_start(rows[k][:, :], row_view[k]).then_inc(loaded, 16)
            sp.wait_ge(zeroed, 1)
            sp.dma_start(rows[2][0:pairs - 1, :], dst[1:1 + (pairs - 1) * W].rearrange("(q c) -> q c", c=W)
                         ).then_inc(loaded, 16)
            sp.dma_start(rows[2][pairs - 1:pairs, 0:W - 1], dst[1 + (pairs - 1) * W:edges].unsqueeze(0)
                         ).then_inc(loaded, 16)
            sp.wait_ge(split, 1)
            sp.dma_start(index["before"][P - 1:P, 1:tiles], index["dst_f"][P - 1:P, 0:tiles - 1]).then_inc(moved, 16)
            sp.wait_ge(moved, 16)

        @block.vector
        def _(v):
            v.memset(rows[2][:, :], -1).then_inc(zeroed, 1)
            v.memset(index["before"][:, :], -1.0)
            v.memset(index["dst_f"][:, :], 0.0)
            v.memset(nxt[:, :], 0.0)
            v.memset(index["src_i"][:, :], 0)
            v.memset(index["dst_i"][:, :], 0)
            v.memset(index["into_i"][:, :], 0)
            v.wait_ge(loaded, 64)
            for k in range(3):
                ins = v.tensor_copy(rows_f[k][:, :], rows[k][:, :])
            ins.then_inc(floats, 1)
            v.wait_ge(turned, 1)

            def columns(t, j):
                return t[:, 0:tiles].rearrange("p (q j) -> p j q", j=J)[:, j, :]

            for j in range(J):
                o = slice(j * 128, j * 128 + pairs)
                v.tensor_copy(columns(index["src_i"], j), banks[0][0:P, o])
                v.tensor_copy(columns(index["dst_i"], j), banks[1][0:P, o])
                v.tensor_copy(columns(index["dst_f"], j), banks[1][0:P, o])
                ins = v.tensor_copy(columns(nxt, j), banks[2][0:P, o])
            ins.then_inc(split, 1)
            v.wait_ge(split, 1)
            v.tensor_tensor(same[:, :], index["dst_f"][:, :], nxt[:, :], ALU.is_equal).then_inc(split, 1)
            v.wait_ge(split, 2)
            v.scalar_tensor_tensor(index["into_i"][:, :], same[:, :], float(nodes), index["dst_f"][:, :],
                                   ALU.mult, ALU.add)

        @block.tensor
        def _(pe):
            pe.wait_ge(floats, 1)
            for k in range(3):
                for j in range(J):
                    ins = pe.transpose(banks[k][0:P, j * 128:j * 128 + pairs],
                                       rows_f[k][:, j * P:(j + 1) * P], w["ident"][0:pairs, 0:pairs])
            ins.then_inc(turned, 1)
    return index


def edge_buffers(sb):
    e = {}
    T = LANES * J
    for name, shape, dtype in (
            ("rows", [P, LANES, 2, J, ROW], F32),
            ("src_now", [P, T], I32),
            ("dst_now", [P, T], I32),
            ("into_now", [P, T], I32),
            ("key_now", [P, 2, T], F32),
            ("dst_row", [P, LANES, W], I32),
            ("first", [P, 1], F32),
            ("y", [P, T, 4], F32),
            ("attrs", [P, T, 64], F32),
            ("root", [P, LANES, 2, J], F32),
            ("root_a", [P, LANES, J], F32),
            ("xs", [P, LANES, J, F], F32),
            ("xd", [P, LANES, J, F], F32),
            ("attr_t", [64, LANES, W], F32),
            ("s_t", [S, LANES, W], F32),
            ("v_t", [V, LANES, W], F32),
            ("ds_t", [S, LANES, W], F32),
            ("dv_t", [V, LANES, W], F32),
            ("h", [128, LANES, W], F32),
            ("h2", [128, LANES, W], F32),
            ("f01", [128, LANES, W], F32),
            ("fv", [V, LANES, W], F32),
            ("p01", [128, LANES, W], F32),
            ("p2", [V, LANES, W], F32),
            ("p3", [V, LANES, W], F32),
            ("same0", [P, LANES, W], F32),
            ("same1", [P, LANES, P], F32),
            ("carry", [P, LANES, W], F32),
            ("msg", [P, LANES, J, 184], F32),
            ("sums", [P, LANES, J, 184], F32),
            ("new", [P, LANES, J, ROW], F32),
            ("part", [P, LANES, J], F32),
            ("factor", [P, LANES, J], F32),
            ("stats", [P, LANES, J, 6], F32),
    ):
        e[name] = sb("edge_" + name, shape, dtype)
    return e


def masks(v, t, e, i, n):
    k = J * n
    v.tensor_scalar(e["same0"][:, n, :], e["dst_row"][:, n, :], e["key_now"][:, 0, k:k + 1], None, ALU.is_equal)
    v.tensor_scalar(e["same1"][:, n, :], e["dst_row"][:, n, P:W], e["key_now"][:, 0, k + 1:k + 2], None, ALU.is_equal)
    v.tensor_scalar(e["carry"][:, n, :], e["dst_row"][:, n, :], e["key_now"][:, 1, k:k + 1], None, ALU.is_equal
                    ).then_inc(t["dve"][n], 1)


def run_sums(pe, e, banks, n, m):
    before = e["sums"][:, (n - 1) % LANES, J - 1, 0:m]
    pe.matmul(banks[2 * n][0:P, 0:m], e["same0"][:, n, 0:P], e["msg"][:, n, 0, 0:m], start=True, stop=False)
    pe.matmul(banks[2 * n][0:P, 0:m], e["carry"][:, n, 0:P], before, start=False, stop=True)
    pe.matmul(banks[2 * n + 1][0:P, 0:m], e["same0"][:, n, P:W], e["msg"][:, n, 0, 0:m], start=True, stop=False)
    pe.matmul(banks[2 * n + 1][0:P, 0:m], e["same1"][:, n, :], e["msg"][:, n, 1, 0:m], start=False, stop=False)
    return pe.matmul(banks[2 * n + 1][0:P, 0:m], e["carry"][:, n, P:W], before, start=False, stop=True)


def edges_layer(nc, sem, sb, banks, inp, w, e, index, tables, l, nodes, edges):
    basis, hid = edge_weights(nc, sem, sb, inp, w, l)
    T = LANES * J
    rounds = edges // ROWS
    M = 1 + F + 1
    attrs = inp[("edge_attr_8", "edge_attr_16", "edge_attr_10")[l]].rearrange("(t p) f -> p t f", p=P)
    y_view = inp["edge_attr_4"].rearrange("(t p) f -> p t f", p=P)
    source, target = tables[l], tables[l + 1]
    two = ["hidden2"] * (l == 0), ["activated2"] * (l == 0)
    factors = [["half_factor"], ["count", "inverse", "part", "half_factor"], []][l]
    t = lane_steps(sem, f"edges{l}",
              pe=["attr_turned", "src_turned", "hidden1", "dst_turned", *two[0], "linear", "weights", "messages",
                  "summed"],
              act=["attr_kept", "attr_copied", "src_copied", "activated1", "dst_copied", *two[1], "linear_copied",
                   "sums_copied"],
              dve=["root_attr", "normed", "masked", "products", "combined0", "combined1", "combined2", "combined3",
                   *factors, "factor", "self_added", "added", "measured", "merged", "widened"],
              pool=["roots"])
    gathered = [sem(f"edges{l}_rows_gathered_lane{n}") for n in range(LANES)]
    attrs_loaded, scattered = sem(f"edges{l}_attrs_loaded"), sem(f"edges{l}_rows_scattered")
    index_copied = sem(f"edges{l}_index_copied")
    ready = sem(f"edges{l}_ready")

    def combine(v, t, i, n):
        y = [[e["y"][:, J * n + j, c:c + 1] for c in range(4)] for j in range(J)]
        v.wait_ge(t["pe"][n], count_at(t, i + 1, "pe", "messages"))
        for j in range(J):
            bank = banks[2 * n + j]
            v.tensor_scalar(e["msg"][:, n, j, 0:1 + S], bank[0:P, 0:1 + S], y[j][0], None, ALU.mult)
            ins = v.tensor_scalar(e["msg"][:, n, j, 1 + S:1 + F], bank[0:P, 97:193], y[j][0], None, ALU.mult)
        ins.then_inc(t["dve"][n], 1)
        for c in range(3):
            v.wait_ge(t["dve"][n], count_at(t, i + 1, "dve", f"combined{c}"))
            for j in range(J):
                bank, o = banks[2 * n + j], 193 + c * (1 + S)
                v.scalar_tensor_tensor(e["msg"][:, n, j, 0:1 + S], bank[0:P, o:o + 1 + S], y[j][c + 1],
                                       e["msg"][:, n, j, 0:1 + S], ALU.mult, ALU.add)
                mv = e["msg"][:, n, j, 1 + S:1 + F].rearrange("p (w c) -> p c w", c=3)[:, c, :]
                ins = v.scalar_tensor_tensor(mv, bank[0:P, 1 + S:97], y[j][c + 1], mv, ALU.mult, ALU.add)
            ins.then_inc(t["dve"][n], 1)

    def update(v, t, i, n):
        attr = e["new"][:, n, :, A:A + 1]
        part, factor = e["part"][:, n, :].unsqueeze(2), e["factor"][:, n, :].unsqueeze(2)
        alpha, count = e["sums"][:, n, :, 0:1], e["sums"][:, n, :, M - 1:M]
        v.wait_ge(t["act"][n], count_at(t, i + 1, "act", "sums_copied"))
        if l == 0:
            v.tensor_tensor(part, alpha, attr, ALU.mult).then_inc(t["dve"][n], 1)
            v.wait_ge(t["dve"][n], count_at(t, i + 1, "dve", "half_factor"))
            v.tensor_tensor(factor, part, attr, ALU.mult).then_inc(t["dve"][n], 1)
        elif l == 1:
            v.tensor_scalar(part, count, 1.0, None, ALU.max).then_inc(t["dve"][n], 1)
            v.wait_ge(t["dve"][n], count_at(t, i + 1, "dve", "count"))
            v.reciprocal(part, part).then_inc(t["dve"][n], 1)
            v.wait_ge(t["dve"][n], count_at(t, i + 1, "dve", "inverse"))
            v.tensor_tensor(part, part, attr, ALU.mult).then_inc(t["dve"][n], 1)
            v.wait_ge(t["dve"][n], count_at(t, i + 1, "dve", "part"))
            v.tensor_tensor(factor, alpha, part, ALU.mult).then_inc(t["dve"][n], 1)
            v.wait_ge(t["dve"][n], count_at(t, i + 1, "dve", "half_factor"))
            v.tensor_tensor(factor, factor, part, ALU.mult).then_inc(t["dve"][n], 1)
        else:
            v.tensor_copy(factor, attr).then_inc(t["dve"][n], 1)
        for j in range(J):
            ins = v.scalar_tensor_tensor(e["new"][:, n, j, 0:F], banks[2 * n + j][0:P, 192:192 + F],
                                         e["new"][:, n, j, A:A + 1], e["xd"][:, n, j, :], ALU.mult, ALU.add)
        ins.then_inc(t["dve"][n], 1)
        v.wait_ge(t["dve"][n], count_at(t, i + 1, "dve", "self_added"))
        for j in range(J):
            ins = v.scalar_tensor_tensor(e["new"][:, n, j, 0:F], e["sums"][:, n, j, 1:1 + F], e["factor"][:, n, j:j + 1],
                                         e["new"][:, n, j, 0:F], ALU.mult, ALU.add)
        ins.then_inc(t["dve"][n], 1)
        v.wait_ge(t["dve"][n], count_at(t, i + 1, "dve", "added"))
        for j in range(J):
            ins = v.bn_stats(e["stats"][:, n, j, :], e["new"][:, n, j, 0:F])
        ins.then_inc(t["dve"][n], 1)
        v.wait_ge(t["dve"][n], count_at(t, i + 1, "dve", "measured"))
        gate(v, t)
        for j in range(J):
            ins = v.bn_aggr(e["new"][:, n, j, MEAN:Q + 1], e["stats"][:, n, j, :])
        ins.then_inc(t["dve"][n], 1)
        v.wait_ge(t["dve"][n], count_at(t, i + 1, "dve", "merged"))
        v.tensor_scalar(e["new"][:, n, :, Q:Q + 1], e["new"][:, n, :, Q:Q + 1], EPS, None, ALU.add
                        ).then_inc(t["dve"][n], 1)

    func, scale = [(ACT.Gelu_apprx_tanh, 8 ** -0.5), (ACT.Silu, 0.25), (ACT.Relu, 10 ** -0.5)][l]

    with nc.Block() as block:
        @block.sync
        def _(sp):
            with sp.Fori(0, rounds) as i:
                for n in range(LANES):
                    sp.wait_ge(t["pe"][n], count_at(t, i, "pe", "attr_turned"))
                    gate(sp, t)
                    sp.wait_ge(t["dve"][n], count_at(t, i, "dve", "combined3"))
                    gate(sp, t)
                sp.dma_start(e["attrs"][:, :, 0:basis], attrs[:, bass.ds(i * T, T), :]).then_inc(attrs_loaded, 16)
                sp.dma_start(e["y"][:, :, :], y_view[:, bass.ds(i * T, T), :]).then_inc(attrs_loaded, 16)
                sp.dma_start(e["dst_row"][:, :, :].rearrange("p n c -> p (n c)"),
                             inp["dst"][bass.ds(i * ROWS, ROWS)].unsqueeze(0).broadcast_to([P, ROWS])
                             ).then_inc(attrs_loaded, 16)

        @block.gpsimd
        def _(p):
            prime(p, t, "pool")

            def copy_indices(i):
                p.tensor_copy(e["src_now"][:, :], index["src_i"][:, bass.ds(i * T, T)])
                p.tensor_copy(e["dst_now"][:, :], index["dst_i"][:, bass.ds(i * T, T)]).then_inc(index_copied, 1)

            def gather(n):
                for j in range(J):
                    for side, idx in enumerate((e["src_now"], e["dst_now"])):
                        k = J * n + j
                        p.indirect_dma_start(e["rows"][:, n, side, j, :], None, source,
                                             bass.IndirectOffsetOnAxis(ap=idx[:, k:k + 1], axis=0)
                                             ).then_inc(gathered[n], 16)

            p.dma_start(e["first"][:, :], inp["node_vec1"][0:P, :]).then_inc(scattered, 16)
            copy_indices(0)
            p.wait_ge(index_copied, 1)
            for n in range(LANES):
                gather(n)
            with p.Fori(0, rounds) as i:
                for n in range(LANES):
                    p.wait_ge(gathered[n], 64 * i + 64)
                    gate(p, t)
                    p.tensor_tensor(e["root"][:, n, :, :].unsqueeze(3), e["rows"][:, n, :, :, Q:Q + 1],
                                    w["half"][:, 0:2 * J].rearrange("p (s j) -> p s j", j=J).unsqueeze(3), ALU.pow
                                    ).then_inc(t["pool"][n], 1)
                for n in range(LANES):
                    p.wait_ge(t["dve"][n], count_at(t, i, "dve", "masked"))
                    gate(p, t)
                p.wait_ge(scattered, 16 * T * i + 16)
                gate(p, t)
                p.tensor_copy(e["into_now"][:, :], index["into_i"][:, bass.ds(i * T, T)])
                p.tensor_copy(e["key_now"][:, 0, :], index["dst_f"][:, bass.ds(i * T, T)])
                p.tensor_copy(e["key_now"][:, 1, :], index["before"][:, bass.ds(i * T, T)])
                copy_indices(i + 1)
                p.wait_ge(index_copied, i + 2)
                gate(p, t)
                for n in range(LANES):
                    p.wait_ge(t["dve"][n], count_at(t, i + 1, "dve", "normed"))
                    gate(p, t)
                    p.wait_ge(t["act"][n], count_at(t, i + 1, "act", "attr_kept"))
                    gate(p, t)
                    gather(n)
                for n in range(LANES):
                    p.wait_ge(t["dve"][n], count_at(t, i + 1, "dve", "widened"))
                    gate(p, t)
                    for j in range(J):
                        k = J * n + j
                        p.indirect_dma_start(target, bass.IndirectOffsetOnAxis(ap=e["into_now"][:, k:k + 1], axis=0),
                                             e["new"][:, n, j, :], None, bounds_check=nodes - 1, oob_is_err=False
                                             ).then_inc(scattered, 16)
            for n in range(LANES):
                p.wait_ge(gathered[n], 64 * (rounds + 1))
            p.wait_ge(scattered, 16 * T * rounds + 16)

        @block.vector
        def _(v):
            v.memset(e["msg"][:, :, :, M - 1:M], 1.0)
            v.memset(e["new"][:, :, :, MEAN:ROW], 0.0)
            v.memset(e["sums"][:, :, :, :], 0.0).then_inc(ready, 1)
            v.wait_ge(ready, 1)
            prime(v, t, "dve")
            with v.Fori(0, rounds) as i:
                for n in range(LANES):
                    v.wait_ge(t["pool"][n], count_at(t, i + 1, "pool", "roots"))
                    v.tensor_tensor(e["root_a"][:, n, :].unsqueeze(2), e["root"][:, n, 0, :].unsqueeze(2),
                                    e["rows"][:, n, 0, :, A:A + 1], ALU.mult).then_inc(t["dve"][n], 1)
                    v.wait_ge(t["dve"][n], count_at(t, i + 1, "dve", "root_attr"))
                    for j in range(J):
                        v.tensor_scalar(e["xs"][:, n, j, :], e["rows"][:, n, 0, j, 0:F], e["rows"][:, n, 0, j, MEAN:Q],
                                        e["root_a"][:, n, j:j + 1], ALU.subtract, ALU.mult)
                        ins = v.tensor_scalar(e["xd"][:, n, j, :], e["rows"][:, n, 1, j, 0:F], e["rows"][:, n, 1, j, MEAN:Q],
                                              e["root"][:, n, 1, j:j + 1], ALU.subtract, ALU.mult)
                    ins.then_inc(t["dve"][n], 1)
                v.wait_ge(index_copied, i + 2)
                v.wait_ge(attrs_loaded, 48 * i + 48)
                for n in range(LANES):
                    masks(v, t, e, i + 1, n)
                for n in range(LANES):
                    a, b = banks[2 * n], banks[2 * n + 1]
                    v.wait_ge(t["pe"][n], count_at(t, i + 1, "pe", "weights"))
                    v.tensor_tensor(e["p01"][:, n, :], a[:, 0:W], e["f01"][:, n, :], ALU.mult)
                    v.tensor_tensor(e["p2"][:, n, :], b[0:V, 0:W], e["fv"][:, n, :], ALU.mult)
                    v.tensor_tensor(e["p3"][:, n, :], b[0:V, W:2 * W], e["fv"][:, n, :], ALU.mult
                                    ).then_inc(t["dve"][n], 1)
                for n in range(LANES):
                    combine(v, t, i, n)
                for n in range(LANES):
                    update(v, t, i, n)

        @block.scalar
        def _(act):
            prime(act, t, "act")
            act.wait_ge(ready, 1)
            with act.Fori(0, rounds) as i:
                for n in range(LANES):
                    act.wait_ge(gathered[n], 64 * i + 64)
                    act.wait_ge(scattered, 16 * T * i + 16)
                    act.activation(e["new"][:, n, :, A:A + 1], e["rows"][:, n, 1, :, A:A + 1], ACT.Copy
                                   ).then_inc(t["act"][n], 1)
                for n in range(LANES):
                    act.wait_ge(t["pe"][n], count_at(t, i + 1, "pe", "attr_turned"))
                    act.activation(e["attr_t"][0:basis, n, :], banks[2 * n + 1][0:basis, 0:W], ACT.Copy
                                   ).then_inc(t["act"][n], 1)
                for n in range(LANES):
                    act.wait_ge(t["pe"][n], count_at(t, i + 1, "pe", "src_turned"))
                    act.activation(e["s_t"][:, n, :], banks[2 * n][0:S, 0:W], ACT.Copy)
                    act.activation(e["v_t"][:, n, :], banks[2 * n][0:V, W:2 * W], ACT.Copy
                                   ).then_inc(t["act"][n], 1)
                for n in range(LANES):
                    act.wait_ge(t["pe"][n], count_at(t, i + 1, "pe", "hidden1"))
                    act.activation(e["h"][0:hid if l else S, n, :], banks[2 * n + 1][0:hid if l else S, W:2 * W], func,
                                   scale=scale).then_inc(t["act"][n], 1)
                for n in range(LANES):
                    act.wait_ge(t["pe"][n], count_at(t, i + 1, "pe", "dst_turned"))
                    act.activation(e["ds_t"][:, n, :], banks[2 * n][0:S, 0:W], ACT.Copy)
                    act.activation(e["dv_t"][:, n, :], banks[2 * n][0:V, W:2 * W], ACT.Copy
                                   ).then_inc(t["act"][n], 1)
                if l == 0:
                    for n in range(LANES):
                        act.wait_ge(t["pe"][n], count_at(t, i + 1, "pe", "hidden2"))
                        act.activation(e["h2"][0:S, n, :], banks[2 * n + 1][0:S, 0:W], func, scale=S ** -0.5
                                       ).then_inc(t["act"][n], 1)
                for n in range(LANES):
                    act.wait_ge(t["pe"][n], count_at(t, i + 1, "pe", "linear"))
                    act.activation(e["f01"][:, n, :], banks[2 * n][:, 0:W], ACT.Copy)
                    act.activation(e["fv"][:, n, :], banks[2 * n][0:V, W:2 * W], ACT.Copy
                                   ).then_inc(t["act"][n], 1)
                for n in range(LANES):
                    act.wait_ge(t["pe"][n], count_at(t, i + 1, "pe", "summed"))
                    for j in range(J):
                        ins = act.activation(e["sums"][:, n, j, 0:M], banks[2 * n + j][0:P, 0:M], ACT.Copy)
                    ins.then_inc(t["act"][n], 1)

        @block.tensor
        def _(pe):
            prime(pe, t, "pe")
            ident = w["ident"][0:P, 0:P]
            last_h = e["h2"] if l == 0 else e["h"]

            def turn(x, bank, n):
                for j in range(J):
                    pe.transpose(bank[0:S, j * P:(j + 1) * P], x[:, n, j, 0:S], ident)
                    ins = pe.transpose(bank[0:V, W + j * P:W + (j + 1) * P], x[:, n, j, S:F], ident)
                ins.then_inc(t["pe"][n], 1)

            with pe.Fori(0, rounds) as i:
                pe.wait_ge(attrs_loaded, 48 * i + 48)
                gate(pe, t)
                for n in range(LANES):
                    pe.wait_ge(t["dve"][n], count_at(t, i, "dve", "self_added"))
                    gate(pe, t)
                    pe.wait_ge(t["act"][n], count_at(t, i, "act", "sums_copied"))
                    gate(pe, t)
                    for j in range(J):
                        ins = pe.transpose(banks[2 * n + 1][0:basis, j * P:(j + 1) * P],
                                           e["attrs"][:, J * n + j, 0:basis], ident)
                    ins.then_inc(t["pe"][n], 1)
                for n in range(LANES):
                    pe.wait_ge(t["dve"][n], count_at(t, i + 1, "dve", "normed"))
                    gate(pe, t)
                    turn(e["xs"], banks[2 * n], n)
                for n in range(LANES):
                    pe.wait_ge(t["act"][n], count_at(t, i + 1, "act", "attr_copied"))
                    gate(pe, t)
                    hid1 = w["fc1"].shape[1]
                    pe.matmul(banks[2 * n + 1][0:hid1, W:2 * W], w["fc1"][:, :], e["attr_t"][0:basis, n, :],
                              start=True, stop=True).then_inc(t["pe"][n], 1)
                for n in range(LANES):
                    pe.wait_ge(t["act"][n], count_at(t, i + 1, "act", "src_copied"))
                    gate(pe, t)
                    turn(e["xd"], banks[2 * n], n)
                if l == 0:
                    for n in range(LANES):
                        pe.wait_ge(t["act"][n], count_at(t, i + 1, "act", "activated1"))
                        gate(pe, t)
                        pe.matmul(banks[2 * n + 1][0:S, 0:W], w["fc2"][:, :], e["h"][0:S, n, :],
                                  start=True, stop=True).then_inc(t["pe"][n], 1)
                for n in range(LANES):
                    pe.wait_ge(t["act"][n], count_at(t, i + 1, "act", "dst_copied"))
                    gate(pe, t)
                    pe.matmul(banks[2 * n][:, 0:W], w[f"lin_s{l}"][:, :], e["s_t"][:, n, :], start=True, stop=True)
                    pe.matmul(banks[2 * n][0:V, W:2 * W], w[f"lin_v{l}"][:, :], e["v_t"][:, n, :],
                              start=True, stop=True).then_inc(t["pe"][n], 1)
                for n in range(LANES):
                    pe.wait_ge(t["act"][n], count_at(t, i + 1, "act", "linear_copied"))
                    gate(pe, t)
                    h = last_h[0:hid, n, :]
                    pe.matmul(banks[2 * n][:, 0:W], w["fc_last"][:, 0:128], h, start=True, stop=True)
                    pe.matmul(banks[2 * n + 1][0:V, 0:W], w["fc_last"][:, 128:128 + V], h, start=True, stop=True)
                    pe.matmul(banks[2 * n + 1][0:V, W:2 * W], w["fc_last"][:, 128 + V:128 + 2 * V], h,
                              start=True, stop=True).then_inc(t["pe"][n], 1)
                for n in range(LANES):
                    pe.wait_ge(t["dve"][n], count_at(t, i + 1, "dve", "products"))
                    gate(pe, t)
                    for j in range(J):
                        c, bank = slice(j * P, (j + 1) * P), banks[2 * n + j]
                        pe.matmul(bank[0:P, 0:97], e["p01"][:, n, c], w["msg_a"][:, :], start=True, stop=True)
                        pe.matmul(bank[0:P, 97:193], e["p2"][:, n, c], w["msg_c"][:, :], start=True, stop=True)
                        ins = pe.matmul(bank[0:P, 193:388], e["p3"][:, n, c], w["msg_d"][:, :], start=True, stop=True)
                    ins.then_inc(t["pe"][n], 1)
                for n in range(LANES):
                    pe.wait_ge(t["dve"][n], count_at(t, i + 1, "dve", "combined3"))
                    gate(pe, t)
                    pe.wait_ge(t["act"][n - 1], count_at(t, i + 1 if n else i, "act", "sums_copied"))
                    gate(pe, t)
                    run_sums(pe, e, banks, n, M)
                    for j in range(J):
                        c, bank = slice(j * P, (j + 1) * P), banks[2 * n + j]
                        pe.matmul(bank[0:P, 192:192 + S], e["ds_t"][:, n, c], w[f"self_s{l}"][:, :],
                                  start=True, stop=True)
                        ins = pe.matmul(bank[0:P, 192 + S:192 + F], e["dv_t"][:, n, c], w[f"self_v{l}"][0:V, S:F],
                                        start=True, stop=True)
                    ins.then_inc(t["pe"][n], 1)


VALS, X3, ATTR, KEPT = 0, F, 2 * F, 2 * F + 4
HEADS = 8


def attention_weights(nc, sem, keep, sb, banks, inp, w):
    loaded = sem("att_weights_loaded")
    built = sem("att_weights_built")
    summed = sem("att_weights_summed")
    g = {k: inp["L3_gnn_" + k] for k in (
        "ln1_w0 ln1_b0 ln1_w1 msrc_ws msrc_wv mdst_ws mdst_bs mdst_wv rw1 rb1 rg1 rbe1 rw2 rb2 rg2 rbe2 rw3 roff "
        "lin_ws lin_bs lin_wv alpha_dot proj_ws proj_wv").split()}
    for name, shape in (("src_s", [S, 128]), ("dst_s", [S, 128]), ("src_v", [V, V]), ("dst_v", [V, V]),
                        ("ms_bias", [128, 1]), ("rw1", [64, 64]), ("rw2", [64, 64]), ("rw3", [64, 128 + 3 * V]),
                        ("rb1", [P, 64]), ("rb2", [P, 64]), ("rg", [64, 4]), ("rbe", [64, 4]),
                        ("roff12", [128, 1]), ("roff", [V, 3]), ("lin_a", [128, 160]), ("lin_4", [V, 128]),
                        ("lin_3", [V, V]), ("lin_5", [V, V]), ("lin_b", [P, 128]), ("alpha_dot", [P, 64]),
                        ("proj_s", [S, S]), ("proj_v", [V, V]), ("spread", [3, V])):
        w[name] = keep("att_" + name, shape)
    loads = []

    def thrice(src):
        return src.unsqueeze(1).broadcast_to([U, 3, src.shape[1]])

    def raw(name, shape, *parts):
        t = sb("att_raw_" + name, shape)
        for at, src in parts:
            loads.append((t[at, :], src))
        return t

    every = slice(None)
    src_s = raw("src_s", [S, 64], (every, g["msrc_ws"]))
    dst_s = raw("dst_s", [S, 64], (every, g["mdst_ws"]))
    src_v = raw("src_v", [V, U], (every, thrice(g["msrc_wv"])))
    dst_v = raw("dst_v", [V, U], (every, thrice(g["mdst_wv"])))
    w0 = raw("w0", [S, 1], (every, g["ln1_w0"].unsqueeze(1)))
    b0 = raw("b0", [S, 1], (every, g["ln1_b0"].unsqueeze(1)))
    w1 = raw("w1", [V, 1], (every, thrice(g["ln1_w1"].unsqueeze(1))))
    bias = raw("bias", [128, 1], (slice(0, 64), g["mdst_bs"].unsqueeze(1)), (slice(64, 128), g["mdst_bs"].unsqueeze(1)))
    rw2 = raw("rw2", [64, 64], (every, g["rw2"]))
    rw3 = raw("rw3", [64, 224], (every, g["rw3"]))
    both = sb("att_raw_both", [S, 2, 128])
    lin_v0 = raw("lin_v0", [128, U], (slice(64, 128), g["lin_wv"][0:S, :]))
    lin_3 = raw("lin_3", [V, U], (every, thrice(g["lin_wv"][S:S + U, :])))
    lin_5 = raw("lin_5", [V, U], (every, thrice(g["lin_wv"][S + U:S + 2 * U, :])))
    proj_v = raw("proj_v", [V, U], (every, thrice(g["proj_wv"])))
    lin_s = raw("lin_s", [S, 128], (every, g["lin_ws"][0:S, :]))
    for name, src in (("rw1", g["rw1"]), ("proj_s", g["proj_ws"]), ("lin_4", thrice(g["lin_ws"][S:S + U, :])),
                      ("rb1", g["rb1"].unsqueeze(0).broadcast_to([P, 64])),
                      ("rb2", g["rb2"].unsqueeze(0).broadcast_to([P, 64])),
                      ("lin_b", g["lin_bs"].unsqueeze(0).broadcast_to([P, 128])),
                      ("alpha_dot", g["alpha_dot"].rearrange("h k -> (h k)").unsqueeze(0).broadcast_to([P, 64])),
                      ("roff12", g["roff"][0:128].unsqueeze(1))):
        loads.append((w[name][:, :], src))
    for k in range(3):
        loads.append((w["roff"][:, k:k + 1], thrice(g["roff"][128 + k * U:128 + (k + 1) * U].unsqueeze(1))))
    for k in range(2):
        loads.append((w["rg"][:, k:k + 1], g[f"rg{k + 1}"].unsqueeze(1)))
        loads.append((w["rbe"][:, k:k + 1], g[f"rbe{k + 1}"].unsqueeze(1)))

    def kron(v, dst, src, factor):
        for c in range(3):
            v.tensor_scalar(dst[:, :].rearrange("p (w c) -> p c w", c=3)[:, c, :], src[:, :],
                            w["mod3"][:, c:c + 1], factor, ALU.mult, ALU.mult)

    with nc.Block() as block:
        @block.sync
        def _(sp):
            for dst, src in loads:
                sp.dma_start(dst, src).then_inc(loaded, 16)

        @block.vector
        def _(v):
            v.memset(w["lin_a"][:, :], 0.0).then_inc(built, 1)
            v.wait_ge(built, 1)
            v.wait_ge(loaded, 16 * len(loads))
            for k in range(2):
                h = slice(k * 64, (k + 1) * 64)
                v.tensor_scalar(w["src_s"][:, h], src_s[:, :], w0[:, 0:1], None, ALU.mult)
                v.tensor_scalar(w["dst_s"][:, h], dst_s[:, :], w0[:, 0:1], None, ALU.mult)
                v.tensor_copy(both[:, 0, h], src_s[:, :])
                v.tensor_copy(both[:, 1, h], dst_s[:, :])
            kron(v, w["src_v"], src_v, w1[:, 0:1])
            kron(v, w["dst_v"], dst_v, w1[:, 0:1])
            kron(v, w["lin_3"], lin_3, 1.0)
            kron(v, w["lin_5"], lin_5, 1.5 ** 0.5)
            kron(v, w["proj_v"], proj_v, 1.0)
            v.tensor_copy(w["lin_a"][0:S, 0:128], lin_s[:, :])
            v.tensor_scalar(w["lin_a"][S:128, 128:160], lin_v0[S:128, :], 3 ** 0.5, None, ALU.mult)
            v.tensor_scalar(w["rw2"][:, :], rw2[:, :], 0.5, None, ALU.mult)
            v.tensor_scalar(w["rw3"][:, 0:128], rw3[:, 0:128], 0.5, None, ALU.mult)
            for k in range(3):
                v.tensor_scalar(w["rw3"][:, 128 + k * V:128 + (k + 1) * V].rearrange("p (u c) -> p u c", c=3),
                                rw3[:, 128 + k * U:128 + (k + 1) * U].unsqueeze(2).broadcast_to([64, U, 3]),
                                0.5, None, ALU.mult)
            v.tensor_scalar(w["rg"][:, 2:4], w["rg"][:, 0:2], 0.5, None, ALU.mult)
            v.tensor_scalar(w["rbe"][:, 2:4], w["rbe"][:, 0:2], 0.5, None, ALU.mult).then_inc(built, 1)
            v.wait_ge(summed, 1)
            v.tensor_tensor(w["ms_bias"][:, :], banks[0][:, 0:1], bias[:, :], ALU.add)
            v.tensor_copy(w["spread"][:, :], banks[1][0:3, 0:V])

        @block.tensor
        def _(pe):
            pe.wait_ge(built, 2)
            pe.matmul(banks[0][:, 0:1], both[:, 0, :], b0[:, :], start=True, stop=False)
            pe.matmul(banks[0][:, 0:1], both[:, 1, :], b0[:, :], start=False, stop=True)
            pe.transpose(banks[1][0:3, 0:V], w["mod3"][:, :], w["ident"][0:V, 0:V]).then_inc(summed, 1)


def attention_edges(nc, sem, sb, banks, inp, w, e, index, table, kept, logits, edges):
    T = LANES * J
    rounds = edges // ROWS
    attrs = inp["edge_attr_64"].rearrange("(t p) f -> p t f", p=P)
    vec_view = inp["edge_attr_3"].rearrange("(t p) f -> p t f", p=P)
    kept_view = kept.rearrange("(t p) f -> p t f", p=P)
    logit_view = logits.rearrange("(t p) h -> p t h", p=P)
    radial = [s + k for k in ("1", "2") for s in ("h_added", "h_measured", "h_merged", "h_widened", "h_normed",
                                                  "h_gated")]
    t = lane_steps(sem, "att",
              pe=["attr_turned", "hidden1", "h_turned1", "hidden2", "h_turned2", "src_turned", "dst_turned",
                  "vec_turned", "vec_spread", "linear", "weights", "outputs"],
              act=["attr_copied", "h_activated1", "h_activated2", "src_copied", "dst_copied", "attr_kept",
                   "vec_copied", "spread_copied", "linear_copied", "values_copied", "tanh"],
              dve=["measured", "merged", "differences", "squares", "summed", "widened", "x3", "normed",
                   *radial, "products", "product4", "biased", *[f"cross{k}" for k in range(3)],
                   "leak", "leaked", "dotted", "logits"],
              pool=["roots", "h_roots1", "h_roots2"])
    gathered = [sem(f"att_rows_gathered_lane{n}") for n in range(LANES)]
    attrs_loaded, kept_stored = sem("att_attrs_loaded"), sem("att_kept_stored")
    cleared = sem("att_columns_cleared")
    index_copied = sem("att_index_copied")
    stats = sb("att_stats", [P, LANES, 2, 2 * J, 6])
    mom = sb("att_moments", [P, LANES, 2, 2 * J, 2])
    diff = sb("att_diff", [P, LANES, 2 * J])
    vec_sq = sb("att_vec_sq", [P, LANES, J, 3])
    wide = sb("att_wide", [P, LANES, 12])
    root = sb("att_root", [P, LANES, 12])
    r = sb("att_r", [P, LANES, 2, J, 3])
    r_t = sb("att_r_t", [3, LANES, W])
    spread = sb("att_spread_r", [V, LANES, W])
    hx = sb("att_hx", [P, LANES, J, 64])
    hn = sb("att_hn", [P, LANES, J, 64])
    h_stats = sb("att_h_stats", [P, LANES, J, 6])
    h_mom = sb("att_h_moments", [P, LANES, J, 2])
    h_wide = sb("att_h_wide", [P, LANES, J])
    h_root = sb("att_h_root", [P, LANES, J])
    h_u = sb("att_h_u", [64, LANES, W])
    h_tanh = sb("att_h_tanh", [64, LANES, W])
    p5 = sb("att_p5", [V, LANES, W])
    keep = sb("att_keep", [P, T, KEPT])
    alpha = sb("att_alpha", [P, LANES, J, 64])
    tanh = sb("att_tanh", [P, LANES, J, 64])
    logit = sb("att_logit", [P, T, HEADS])

    with nc.Block() as block:
        @block.sync
        def _(sp):
            sp.sem_inc(kept_stored, 16)
            with sp.Fori(0, rounds) as i:
                for n in range(LANES):
                    sp.wait_ge(t["pe"][n], count_at(t, i, "pe", "attr_turned"))
                    gate(sp, t)
                    sp.wait_ge(t["dve"][n], count_at(t, i, "dve", "x3"))
                    gate(sp, t)
                sp.dma_start(e["attrs"][:, :, :], attrs[:, bass.ds(i * T, T), :]).then_inc(attrs_loaded, 16)
                sp.dma_start(e["y"][:, :, 0:3], vec_view[:, bass.ds(i * T, T), :]).then_inc(attrs_loaded, 16)
                for n in range(LANES):
                    sp.wait_ge(t["dve"][n], count_at(t, i + 1, "dve", "logits"))
                    gate(sp, t)
                    sp.wait_ge(t["act"][n], count_at(t, i + 1, "act", "attr_kept"))
                    gate(sp, t)
                sp.dma_start(kept_view[:, bass.ds(i * T, T), :], keep[:, :, :]).then_inc(kept_stored, 16)
                sp.dma_start(logit_view[:, bass.ds(i * T, T), :], logit[:, :, :]).then_inc(kept_stored, 16)
            sp.wait_ge(kept_stored, 32 * rounds + 16)

        @block.gpsimd
        def _(p):
            prime(p, t, "pool")

            def copy_indices(i):
                p.tensor_copy(e["src_now"][:, :], index["src_i"][:, bass.ds(i * T, T)])
                p.tensor_copy(e["dst_now"][:, :], index["dst_i"][:, bass.ds(i * T, T)]).then_inc(index_copied, 1)

            def gather(n):
                for j in range(J):
                    for side, idx in enumerate((e["src_now"], e["dst_now"])):
                        k = J * n + j
                        p.indirect_dma_start(e["rows"][:, n, side, j, :], None, table,
                                             bass.IndirectOffsetOnAxis(ap=idx[:, k:k + 1], axis=0)
                                             ).then_inc(gathered[n], 16)

            copy_indices(0)
            p.wait_ge(index_copied, 1)
            for n in range(LANES):
                gather(n)
            with p.Fori(0, rounds) as i:
                for n in range(LANES):
                    p.wait_ge(t["dve"][n], count_at(t, i + 1, "dve", "widened"))
                    gate(p, t)
                    p.tensor_tensor(root[:, n, :], wide[:, n, :], w["half"][:, 0:12], ALU.pow
                                    ).then_inc(t["pool"][n], 1)
                for k in ("1", "2"):
                    for n in range(LANES):
                        p.wait_ge(t["dve"][n], count_at(t, i + 1, "dve", "h_widened" + k))
                        gate(p, t)
                        p.tensor_tensor(h_root[:, n, :], h_wide[:, n, :], w["half"][:, 0:J], ALU.pow
                                        ).then_inc(t["pool"][n], 1)
                for n in range(LANES):
                    p.wait_ge(gathered[n], 64 * i + 64)
                    gate(p, t)
                copy_indices(i + 1)
                p.wait_ge(index_copied, i + 2)
                gate(p, t)
                for n in range(LANES):
                    p.wait_ge(t["dve"][n], count_at(t, i + 1, "dve", "normed"))
                    gate(p, t)
                    p.wait_ge(t["act"][n], count_at(t, i + 1, "act", "attr_kept"))
                    gate(p, t)
                    gather(n)
            for n in range(LANES):
                p.wait_ge(gathered[n], 64 * (rounds + 1))

        @block.vector
        def _(v):
            v.memset(keep[:, :, ATTR:KEPT], 0.0).then_inc(cleared, 1)
            prime(v, t, "dve")

            def one(ins, n):
                ins.then_inc(t["dve"][n], 1)

            def after(i, n, step):
                v.wait_ge(t["dve"][n], count_at(t, i + 1, "dve", step))

            with v.Fori(0, rounds) as i:
                v.wait_ge(attrs_loaded, 32 * i + 32)
                for n in range(LANES):
                    rows = e["rows"][:, n, :, :, :].rearrange("p s j f -> p (s j) f")
                    v.wait_ge(gathered[n], 64 * i + 64)
                    for k in range(2 * J):
                        v.bn_stats(stats[:, n, 0, k, :], rows[:, k, 0:S])
                        ins = v.bn_stats(stats[:, n, 1, k, :], rows[:, k, S:F])
                    v.tensor_tensor(vec_sq[:, n, :, :], e["y"][:, J * n:J * n + J, 0:3], e["y"][:, J * n:J * n + J, 0:3],
                                    ALU.mult).then_inc(t["dve"][n], 1)
                    after(i, n, "measured")
                    gate(v, t)
                    for k in range(2 * J):
                        v.bn_aggr(mom[:, n, 0, k, :], stats[:, n, 0, k, :])
                        ins = v.bn_aggr(mom[:, n, 1, k, :], stats[:, n, 1, k, :])
                    one(ins, n)
                    after(i, n, "merged")
                    q, mean = rows[:, :, Q:Q + 1], rows[:, :, MEAN:Q]
                    d = diff[:, n, :].unsqueeze(2)
                    v.scalar_tensor_tensor(wide[:, n, 0:4].unsqueeze(2), q, EPS, mom[:, n, 0, :, 1:2],
                                           ALU.mult, ALU.add)
                    v.tensor_copy(wide[:, n, 8:10].unsqueeze(2), e["rows"][:, n, 1, :, Q:Q + 1])
                    v.tensor_reduce(wide[:, n, 10:12], vec_sq[:, n, :, :], AX.X, ALU.add)
                    one(v.tensor_tensor(d, mom[:, n, 1, :, 0:1], mean, ALU.subtract), n)
                    after(i, n, "differences")
                    v.tensor_scalar(wide[:, n, 10:12], wide[:, n, 10:12], 1e-12, None, ALU.add)
                    one(v.tensor_tensor(d, d, d, ALU.mult), n)
                    after(i, n, "squares")
                    one(v.tensor_tensor(d, d, mom[:, n, 1, :, 1:2], ALU.add), n)
                    after(i, n, "summed")
                    one(v.scalar_tensor_tensor(wide[:, n, 4:8].unsqueeze(2), q, EPS, d, ALU.mult, ALU.add), n)
                for n in range(LANES):
                    v.wait_ge(t["pool"][n], count_at(t, i + 1, "pool", "roots"))
                    v.wait_ge(kept_stored, 32 * i + 16)
                    for j in range(J):
                        v.tensor_scalar(keep[:, J * n + j, X3:X3 + F], e["rows"][:, n, 1, j, 0:F],
                                        e["rows"][:, n, 1, j, MEAN:Q], root[:, n, 8 + j:9 + j], ALU.subtract, ALU.mult)
                        v.tensor_scalar(r[:, n, 0, j, :], e["y"][:, J * n + j, 0:3], root[:, n, 10 + j:11 + j], None,
                                        ALU.mult)
                        ins = v.tensor_scalar(r[:, n, 1, j, :], e["y"][:, J * n + j, 0:3], root[:, n, 10 + j:11 + j],
                                              -1.0, ALU.mult, ALU.mult)
                    one(ins, n)
                    for j in range(J):
                        for side, x in enumerate((e["xs"], e["xd"])):
                            k = side * J + j
                            v.tensor_scalar(x[:, n, j, 0:S], e["rows"][:, n, side, j, 0:S], mom[:, n, 0, k, 0:1],
                                            root[:, n, k:k + 1], ALU.subtract, ALU.mult)
                            ins = v.tensor_scalar(x[:, n, j, S:F], e["rows"][:, n, side, j, S:F],
                                                  e["rows"][:, n, side, j, MEAN:Q], root[:, n, 4 + k:5 + k],
                                                  ALU.subtract, ALU.mult)
                    one(ins, n)
                for m, k in enumerate(("1", "2")):
                    for n in range(LANES):
                        v.wait_ge(t["pe"][n], count_at(t, i + 1, "pe", "hidden" + k))
                        one(v.tensor_tensor(hx[:, n, :, :],
                                            banks[2 * n + 1][0:P, 256:384].rearrange("p (j f) -> p j f", j=J),
                                            w["rb" + k][:, :].unsqueeze(1).broadcast_to([P, J, 64]), ALU.add), n)
                        after(i, n, "h_added" + k)
                        for j in range(J):
                            ins = v.bn_stats(h_stats[:, n, j, :], hx[:, n, j, :])
                        one(ins, n)
                        after(i, n, "h_measured" + k)
                        gate(v, t)
                        for j in range(J):
                            ins = v.bn_aggr(h_mom[:, n, j, :], h_stats[:, n, j, :])
                        one(ins, n)
                        after(i, n, "h_merged" + k)
                        one(v.tensor_scalar(h_wide[:, n, :].unsqueeze(2), h_mom[:, n, :, 1:2], EPS, None, ALU.add), n)
                    for n in range(LANES):
                        v.wait_ge(t["pool"][n], count_at(t, i + 1, "pool", "h_roots" + k))
                        for j in range(J):
                            ins = v.tensor_scalar(hn[:, n, j, :], hx[:, n, j, :], h_mom[:, n, j, 0:1],
                                                  h_root[:, n, j:j + 1], ALU.subtract, ALU.mult)
                        one(ins, n)
                    for n in range(LANES):
                        v.wait_ge(t["act"][n], count_at(t, i + 1, "act", "h_activated" + k))
                        one(v.scalar_tensor_tensor((e["h"], e["h2"])[m][0:64, n, :], h_tanh[:, n, :], 1.0, h_u[:, n, :],
                                                   ALU.add, ALU.mult), n)
                for n in range(LANES):
                    a, b = banks[2 * n], banks[2 * n + 1]
                    v.wait_ge(t["pe"][n], count_at(t, i + 1, "pe", "weights"))
                    v.scalar_tensor_tensor(e["p01"][:, n, :], a[:, 0:W], w["roff12"][:, 0:1], e["f01"][:, n, :],
                                           ALU.add, ALU.mult)
                    v.scalar_tensor_tensor(e["p2"][:, n, :], a[0:V, W:2 * W], w["roff"][:, 0:1], e["fv"][:, n, :],
                                           ALU.add, ALU.mult)
                    v.scalar_tensor_tensor(e["p3"][:, n, :], b[0:V, 0:W], w["roff"][:, 1:2], e["fv"][:, n, :],
                                           ALU.add, ALU.mult)
                    one(v.scalar_tensor_tensor(p5[:, n, :], b[0:V, W:2 * W], w["roff"][:, 2:3], e["fv"][:, n, :],
                                               ALU.add, ALU.mult), n)
                    after(i, n, "products")
                    one(v.tensor_tensor(e["p3"][:, n, :], e["p3"][:, n, :], spread[:, n, :], ALU.mult), n)
                for n in range(LANES):
                    v.wait_ge(t["pe"][n], count_at(t, i + 1, "pe", "outputs"))
                    for j in range(J):
                        k, bank = J * n + j, banks[2 * n + j]
                        v.tensor_tensor(alpha[:, n, j, :], bank[0:P, 0:64], w["lin_b"][:, 0:64], ALU.add)
                        ins = v.tensor_tensor(keep[:, k, 0:S], bank[0:P, 64:128], w["lin_b"][:, 64:128], ALU.add)
                    one(ins, n)
                for n in range(LANES):
                    v.wait_ge(t["act"][n], count_at(t, i + 1, "act", "values_copied"))
                    for step in range(3):
                        if step:
                            after(i, n, f"cross{step - 1}")
                        for j in range(J):
                            k, bank = J * n + j, banks[2 * n + j]
                            out = keep[:, k, S:F].rearrange("p (w c) -> p c w", c=3)
                            x = bank[0:P, 256:352].rearrange("p (w c) -> p c w", c=3)
                            for d in range(3):
                                src, sign, comp = ((bank[0:P, 128:160], 0, d), (x[:, (d + 1) % 3, :], 0, (d + 2) % 3),
                                                   (x[:, (d + 2) % 3, :], 1, (d + 1) % 3))[step]
                                ins = v.scalar_tensor_tensor(out[:, d, :], src, r[:, n, sign, j, comp:comp + 1],
                                                             out[:, d, :], ALU.mult, ALU.add)
                        one(ins, n)
                    v.wait_ge(t["act"][n], count_at(t, i + 1, "act", "tanh"))
                    one(v.tensor_scalar(tanh[:, n, :, :], tanh[:, n, :, :], 0.4, 0.6, ALU.mult, ALU.add), n)
                    after(i, n, "leak")
                    one(v.tensor_tensor(alpha[:, n, :, :], alpha[:, n, :, :], tanh[:, n, :, :], ALU.mult), n)
                    after(i, n, "leaked")
                    one(v.tensor_tensor(alpha[:, n, :, :], alpha[:, n, :, :],
                                        w["alpha_dot"][:, :].unsqueeze(1).broadcast_to([P, J, 64]), ALU.mult), n)
                    after(i, n, "dotted")
                    one(v.tensor_reduce(logit[:, J * n:J * n + J, :],
                                        alpha[:, n, :, :].rearrange("p j (h k) -> p j h k", h=HEADS), AX.X, ALU.add), n)

        @block.scalar
        def _(act):
            prime(act, t, "act")
            act.wait_ge(cleared, 1)
            with act.Fori(0, rounds) as i:
                def wait(engine, n, step):
                    act.wait_ge(t[engine][n], count_at(t, i + 1, engine, step))

                def one(ins, n):
                    ins.then_inc(t["act"][n], 1)

                for n in range(LANES):
                    wait("pe", n, "attr_turned")
                    one(act.activation(e["attr_t"][:, n, :], banks[2 * n + 1][0:64, 0:W], ACT.Copy), n)
                for k in range(2):
                    for n in range(LANES):
                        wait("pe", n, f"h_turned{k + 1}")
                        x = banks[2 * n + 1][0:64, 0:W]
                        act.activation(h_u[:, n, :], x, ACT.Identity, bias=w["rbe"][:, k:k + 1],
                                       scale=w["rg"][:, k:k + 1])
                        one(act.activation(h_tanh[:, n, :], x, ACT.Tanh, bias=w["rbe"][:, 2 + k:3 + k],
                                           scale=w["rg"][:, 2 + k:3 + k]), n)
                for step, s_t, v_t in (("src", e["s_t"], e["v_t"]), ("dst", e["ds_t"], e["dv_t"])):
                    for n in range(LANES):
                        wait("pe", n, step + "_turned")
                        act.activation(s_t[:, n, :], banks[2 * n][0:S, 0:W], ACT.Copy)
                        one(act.activation(v_t[:, n, :], banks[2 * n][0:V, W:2 * W], ACT.Copy), n)
                for n in range(LANES):
                    wait("dve", n, "x3")
                    one(act.activation(keep[:, J * n:J * n + J, ATTR:ATTR + 1], e["rows"][:, n, 1, :, A:A + 1],
                                       ACT.Copy), n)
                for n in range(LANES):
                    wait("pe", n, "vec_turned")
                    one(act.activation(r_t[:, n, :], banks[2 * n + 1][0:3, 0:W], ACT.Copy), n)
                for n in range(LANES):
                    wait("pe", n, "vec_spread")
                    one(act.activation(spread[:, n, :], banks[2 * n + 1][0:V, W:2 * W], ACT.Copy), n)
                for n in range(LANES):
                    wait("pe", n, "linear")
                    act.activation(e["f01"][:, n, :], banks[2 * n][:, 0:W], ACT.Identity, bias=w["ms_bias"][:, 0:1])
                    one(act.activation(e["fv"][:, n, :], banks[2 * n][0:V, W:2 * W], ACT.Copy), n)
                for n in range(LANES):
                    wait("dve", n, "biased")
                    for j in range(J):
                        ins = act.activation(keep[:, J * n + j, S:F], banks[2 * n + j][0:P, 160:256], ACT.Copy)
                    one(ins, n)
                for n in range(LANES):
                    wait("dve", n, "biased")
                    one(act.activation(tanh[:, n, :, :], alpha[:, n, :, :], ACT.Tanh, scale=0.5), n)

        @block.tensor
        def _(pe):
            prime(pe, t, "pe")
            ident = w["ident"][0:P, 0:P]
            with pe.Fori(0, rounds) as i:
                def wait(engine, n, step):
                    pe.wait_ge(t[engine][n], count_at(t, i + 1, engine, step))
                    gate(pe, t)

                def one(ins, n):
                    ins.then_inc(t["pe"][n], 1)

                pe.wait_ge(attrs_loaded, 32 * i + 32)
                gate(pe, t)
                for n in range(LANES):
                    pe.wait_ge(t["dve"][n], count_at(t, i, "dve", "cross2"))
                    gate(pe, t)
                    for j in range(J):
                        ins = pe.transpose(banks[2 * n + 1][0:64, j * P:(j + 1) * P], e["attrs"][:, J * n + j, :], ident)
                    one(ins, n)
                for k in ("1", "2"):
                    for n in range(LANES):
                        if k == "1":
                            wait("act", n, "attr_copied")
                        else:
                            wait("dve", n, "h_gated1")
                        x = e["attr_t"] if k == "1" else e["h"]
                        for j in range(J):
                            ins = pe.matmul(banks[2 * n + 1][0:P, 256 + j * 64:320 + j * 64],
                                            x[0:64, n, j * P:(j + 1) * P], w["rw" + k][:, :], start=True, stop=True)
                        one(ins, n)
                    for n in range(LANES):
                        wait("dve", n, "h_normed" + k)
                        for j in range(J):
                            ins = pe.transpose(banks[2 * n + 1][0:64, j * P:(j + 1) * P], hn[:, n, j, :], ident)
                        one(ins, n)
                for step, x in (("src", e["xs"]), ("dst", e["xd"])):
                    for n in range(LANES):
                        if step == "dst":
                            wait("act", n, "src_copied")
                        else:
                            wait("dve", n, "normed")
                        for j in range(J):
                            pe.transpose(banks[2 * n][0:S, j * P:(j + 1) * P], x[:, n, j, 0:S], ident)
                            ins = pe.transpose(banks[2 * n][0:V, W + j * P:W + (j + 1) * P], x[:, n, j, S:F], ident)
                        one(ins, n)
                for n in range(LANES):
                    wait("act", n, "h_activated2")
                    for j in range(J):
                        ins = pe.transpose(banks[2 * n + 1][0:3, j * P:(j + 1) * P], r[:, n, 0, j, :], ident)
                    one(ins, n)
                for n in range(LANES):
                    wait("act", n, "vec_copied")
                    one(pe.matmul(banks[2 * n + 1][0:V, W:2 * W], w["spread"][:, :], r_t[:, n, :],
                                  start=True, stop=True), n)
                for n in range(LANES):
                    wait("act", n, "dst_copied")
                    a = banks[2 * n]
                    pe.matmul(a[:, 0:W], w["src_s"][:, :], e["s_t"][:, n, :], start=True, stop=False)
                    pe.matmul(a[:, 0:W], w["dst_s"][:, :], e["ds_t"][:, n, :], start=False, stop=True)
                    pe.matmul(a[0:V, W:2 * W], w["src_v"][:, :], e["v_t"][:, n, :], start=True, stop=False)
                    one(pe.matmul(a[0:V, W:2 * W], w["dst_v"][:, :], e["dv_t"][:, n, :], start=False, stop=True), n)
                for n in range(LANES):
                    wait("act", n, "linear_copied")
                    wait("act", n, "spread_copied")
                    wait("dve", n, "h_gated2")
                    a, b, h = banks[2 * n], banks[2 * n + 1], e["h2"][0:64, n, :]
                    pe.matmul(a[:, 0:W], w["rw3"][:, 0:128], h, start=True, stop=True)
                    pe.matmul(a[0:V, W:2 * W], w["rw3"][:, 128:128 + V], h, start=True, stop=True)
                    pe.matmul(b[0:V, 0:W], w["rw3"][:, 128 + V:128 + 2 * V], h, start=True, stop=True)
                    one(pe.matmul(b[0:V, W:2 * W], w["rw3"][:, 128 + 2 * V:128 + 3 * V], h, start=True, stop=True), n)
                for n in range(LANES):
                    wait("dve", n, "product4")
                    for j in range(J):
                        c, bank = slice(j * P, (j + 1) * P), banks[2 * n + j]
                        pe.matmul(bank[0:P, 0:160], e["p01"][:, n, c], w["lin_a"][:, :], start=True, stop=True)
                        pe.matmul(bank[0:P, 0:128], e["p3"][:, n, c], w["lin_4"][:, :], start=False, stop=True,
                                  skip_group_check=True)
                        pe.matmul(bank[0:P, 160:256], e["p2"][:, n, c], w["lin_3"][:, :], start=True, stop=True)
                        ins = pe.matmul(bank[0:P, 256:352], p5[:, n, c], w["lin_5"][:, :], start=True, stop=True)
                    one(ins, n)


def attention_softmax(nc, sem, sb, banks, inp, w, logits, probs, edges):
    C = edges // P
    BIG = 1e30
    loaded = sem("softmax_loaded")
    vec = sem("softmax_vector_steps")
    tri_made = sem("softmax_triangles_made")
    turned = sem("softmax_ends_turned")
    exped = sem("softmax_exp_done")
    stored = sem("softmax_stored")
    spread_made = sem("softmax_ends_spread")
    lg = sb("sm_logits", [P, C, HEADS])
    m = [[sb(f"sm_max{k}{x}", [P, C, HEADS]) for x in range(2)] for k in range(2)]
    cand = sb("sm_candidates", [P, C, HEADS])
    d_i = sb("sm_dst_i", [P, C], I32)
    d = sb("sm_dst", [P, C])
    off = sb("sm_off", [P, C])
    tri = sb("sm_triangles", [P, 2, P])
    ends = sb("sm_ends", [P, 2, 1 + HEADS, P])
    ends_t = sb("sm_ends_t", [P, 2, 1 + HEADS, P])
    far = sb("sm_far", [P, 2, P])
    cross = sb("sm_cross", [P, 2, HEADS])

    with nc.Block() as block:
        @block.sync
        def _(sp):
            sp.dma_start(lg[:, :, :], logits.rearrange("(p c) h -> p c h", p=P)).then_inc(loaded, 16)
            sp.dma_start(d_i[:, :], inp["dst"].rearrange("(p c) -> p c", p=P)).then_inc(loaded, 16)
            sp.wait_ge(exped, 1)
            sp.dma_start(probs.rearrange("(p c) h -> p c h", p=P), lg[:, :, :]).then_inc(stored, 16)
            sp.wait_ge(stored, 16)

        @block.gpsimd
        def _(p):
            p.memset(tri[:, :, :], 1.0).then_inc(tri_made, 1)
            p.wait_ge(tri_made, 1)
            p.affine_select(out=tri[:, 0, :], in_=tri[:, 0, :], compare_op=ALU.is_gt, fill=0.0, base=0,
                            pattern=[[-1, P]], channel_multiplier=1)
            p.affine_select(out=tri[:, 1, :], in_=tri[:, 1, :], compare_op=ALU.is_gt, fill=0.0, base=0,
                            pattern=[[1, P]], channel_multiplier=-1).then_inc(tri_made, 1)

        @block.vector
        def _(v):
            count = 0

            def then(ins):
                nonlocal count
                count += 1
                ins.then_inc(vec, 1)
                v.wait_ge(vec, count)

            v.wait_ge(loaded, 32)
            v.tensor_copy(d[:, :], d_i[:, :])
            v.tensor_copy(m[0][0][:, :, :], lg[:, :, :])
            then(v.tensor_copy(m[1][0][:, :, :], lg[:, :, :]))
            step, at = 1, 0
            while step < C:
                n = C - step
                then(v.tensor_tensor(off[:, 0:n], d[:, step:C], d[:, 0:n], ALU.is_equal))
                then(v.tensor_scalar(off[:, 0:n], off[:, 0:n], BIG, -BIG, ALU.mult, ALU.add))
                away = off[:, 0:n].unsqueeze(2).broadcast_to([P, n, HEADS])
                f, b = m[0][at], m[1][at]
                f2, b2 = m[0][1 - at], m[1][1 - at]
                then(v.tensor_tensor(cand[:, 0:n, :], f[:, 0:n, :], away, ALU.add))
                v.tensor_tensor(f2[:, step:C, :], f[:, step:C, :], cand[:, 0:n, :], ALU.max)
                then(v.tensor_copy(f2[:, 0:step, :], f[:, 0:step, :]))
                then(v.tensor_tensor(cand[:, 0:n, :], b[:, step:C, :], away, ALU.add))
                v.tensor_tensor(b2[:, 0:n, :], b[:, 0:n, :], cand[:, 0:n, :], ALU.max)
                then(v.tensor_copy(b2[:, n:C, :], b[:, n:C, :]))
                step, at = 2 * step, 1 - at
            fwd, bwd = m[0][at], m[1][at]
            for k, (x, c) in enumerate(((fwd, C - 1), (bwd, 0))):
                v.tensor_copy(ends[:, k, 0, :], d[:, c:c + 1].broadcast_to([P, P]))
                ins = v.tensor_copy(ends[:, k, 1:1 + HEADS, :], x[:, c, :].unsqueeze(2).broadcast_to([P, HEADS, P]))
            ins.then_inc(spread_made, 1)
            v.wait_ge(turned, 1)
            for k in range(2):
                for q in range(3):
                    ins = v.tensor_copy(ends_t[:, k, 3 * q:3 * q + 3, :].rearrange("p h c -> p (h c)"),
                                        banks[3 * k + q][0:P, 0:3 * P])
            then(ins)
            v.wait_ge(tri_made, 2)
            for k, c in enumerate((0, C - 1)):
                then(v.scalar_tensor_tensor(far[:, k, :], ends_t[:, k, 0, :], d[:, c:c + 1], tri[:, k, :],
                                            ALU.is_equal, ALU.mult))
                then(v.tensor_scalar(far[:, k, :], far[:, k, :], BIG, -BIG, ALU.mult, ALU.add))
                then(v.tensor_tensor(ends_t[:, k, 1:1 + HEADS, :], ends_t[:, k, 1:1 + HEADS, :],
                                     far[:, k, :].unsqueeze(1).broadcast_to([P, HEADS, P]), ALU.add))
                then(v.tensor_reduce(cross[:, k, :], ends_t[:, k, 1:1 + HEADS, :], AX.X, ALU.max))
            then(v.tensor_tensor(fwd[:, :, :], fwd[:, :, :], bwd[:, :, :], ALU.max))
            for k, c in enumerate((0, C - 1)):
                then(v.tensor_scalar(off[:, :], d[:, :], d[:, c:c + 1], BIG, ALU.is_equal, ALU.mult))
                then(v.tensor_scalar(off[:, :], off[:, :], -BIG, None, ALU.add))
                then(v.tensor_tensor(cand[:, :, :], off[:, :].unsqueeze(2).broadcast_to([P, C, HEADS]),
                                     cross[:, k, :].unsqueeze(1).broadcast_to([P, C, HEADS]), ALU.add))
                then(v.tensor_tensor(fwd[:, :, :], fwd[:, :, :], cand[:, :, :], ALU.max))
            then(v.tensor_tensor(lg[:, :, :], lg[:, :, :], fwd[:, :, :], ALU.subtract))
            v.tensor_copy(off[:, 0:1], d[:, 0:1]).then_inc(spread_made, 1)

        @block.tensor
        def _(pe):
            pe.wait_ge(spread_made, 1)
            for k in range(2):
                for h in range(1 + HEADS):
                    ins = pe.transpose(banks[3 * k + h // 3][0:P, (h % 3) * P:(h % 3 + 1) * P], ends[:, k, h, :],
                                       w["ident"][0:P, 0:P])
            ins.then_inc(turned, 1)

        @block.scalar
        def _(act):
            act.wait_ge(spread_made, 2)
            act.activation(lg[:, :, :], lg[:, :, :], ACT.Exp).then_inc(exped, 1)


def attention_nodes(nc, sem, sb, banks, inp, w, e, ffn, index, kept, probs, out, nodes, edges):
    T = LANES * J
    rounds = edges // ROWS
    M = F + HEADS
    kept_view = kept.rearrange("(t p) f -> p t f", p=P)
    probs_view = probs.rearrange("(t p) h -> p t h", p=P)
    t = lane_steps(sem, "dest",
              pe=["summed", "turned", "projected"] + FFN_PE,
              act=["sums_copied", "turned_copied"] + FFN_ACT,
              dve=["masked", "weighted", "denominator", "inverse", "divided", "with_bias", "x", "doubled"] + FFN_DVE,
              pool=FFN_POOL)
    rows_loaded, scattered = sem("dest_rows_loaded"), sem("dest_rows_scattered")
    index_copied, ready = sem("dest_index_copied"), sem("dest_sums_cleared")
    rows = sb("dest_rows", [P, T, KEPT])
    p_row = sb("dest_probs", [P, T, HEADS])
    inverse = sb("dest_inverse", [P, LANES, J, HEADS])
    mean = sb("dest_mean", [P, LANES, J, F])
    base = sb("dest_base", [P, LANES, J, F])
    xp = sb("dest_xp", [P, LANES, J, F])
    u = sb("dest_u", [P, LANES, J, F])
    res = sb("dest_res", [P, LANES, J, F])

    with nc.Block() as block:
        @block.sync
        def _(sp):
            with sp.Fori(0, rounds) as i:
                for n in range(LANES):
                    sp.wait_ge(t["dve"][n], count_at(t, i, "dve", "ffn_added"))
                    gate(sp, t)
                sp.dma_start(rows[:, :, :], kept_view[:, bass.ds(i * T, T), :]).then_inc(rows_loaded, 16)
                sp.dma_start(p_row[:, :, :], probs_view[:, bass.ds(i * T, T), :]).then_inc(rows_loaded, 16)
                sp.dma_start(e["dst_row"][:, :, :].rearrange("p n c -> p (n c)"),
                             inp["dst"][bass.ds(i * ROWS, ROWS)].unsqueeze(0).broadcast_to([P, ROWS])
                             ).then_inc(rows_loaded, 16)

        @block.gpsimd
        def _(p):
            prime(p, t, "pool")
            p.dma_start(e["first"][:, :], inp["node_vec1"][0:P, :]).then_inc(scattered, 16)
            with p.Fori(0, rounds) as i:
                for n in range(LANES):
                    p.wait_ge(t["dve"][n], count_at(t, i, "dve", "masked"))
                    gate(p, t)
                p.wait_ge(scattered, 16 * T * i + 16)
                gate(p, t)
                p.tensor_copy(e["into_now"][:, :], index["into_i"][:, bass.ds(i * T, T)])
                p.tensor_copy(e["key_now"][:, 0, :], index["dst_f"][:, bass.ds(i * T, T)])
                p.tensor_copy(e["key_now"][:, 1, :], index["before"][:, bass.ds(i * T, T)]).then_inc(index_copied, 1)
                p.wait_ge(index_copied, i + 1)
                gate(p, t)
                for n in range(LANES):
                    ffn_roots(p, ffn, t, i + 1, n)
                for n in range(LANES):
                    ffn_out_roots(p, ffn, t, i + 1, n)
                for n in range(LANES):
                    p.wait_ge(t["dve"][n], count_at(t, i + 1, "dve", "out_normed"))
                    gate(p, t)
                    for j in range(J):
                        k = J * n + j
                        p.indirect_dma_start(out, bass.IndirectOffsetOnAxis(ap=e["into_now"][:, k:k + 1], axis=0),
                                             res[:, n, j, :], None, bounds_check=nodes - 1, oob_is_err=False
                                             ).then_inc(scattered, 16)
            p.wait_ge(scattered, 16 * T * rounds + 16)

        @block.vector
        def _(v):
            v.memset(ffn["hid_v2"][S:S + 1, :, :], 1.0)
            v.memset(e["sums"][:, :, :, :], 0.0).then_inc(ready, 1)
            prime(v, t, "dve")

            def one(ins, n):
                ins.then_inc(t["dve"][n], 1)

            def after(i, n, step):
                v.wait_ge(t["dve"][n], count_at(t, i + 1, "dve", step))

            with v.Fori(0, rounds) as i:
                v.wait_ge(index_copied, i + 1)
                v.wait_ge(rows_loaded, 48 * i + 48)
                for n in range(LANES):
                    masks(v, t, e, i + 1, n)
                    for j in range(J):
                        k = J * n + j
                        p = p_row[:, k, :].unsqueeze(2)
                        v.tensor_tensor(e["msg"][:, n, j, 0:S].rearrange("p (h k) -> p h k", h=HEADS),
                                        rows[:, k, VALS:VALS + S].rearrange("p (h k) -> p h k", h=HEADS),
                                        p.broadcast_to([P, HEADS, 8]), ALU.mult)
                        v.tensor_tensor(e["msg"][:, n, j, S:F].rearrange("p (h k) -> p h k", h=HEADS),
                                        rows[:, k, VALS + S:VALS + F].rearrange("p (h k) -> p h k", h=HEADS),
                                        p.broadcast_to([P, HEADS, 12]), ALU.mult)
                        ins = v.tensor_copy(e["msg"][:, n, j, F:M], p_row[:, k, :])
                    one(ins, n)
                for n in range(LANES):
                    v.wait_ge(t["act"][n], count_at(t, i + 1, "act", "sums_copied"))
                    one(v.tensor_scalar(inverse[:, n, :, :], e["sums"][:, n, :, F:M], 1e-12, None, ALU.add), n)
                    after(i, n, "denominator")
                    one(v.reciprocal(inverse[:, n, :, :], inverse[:, n, :, :]), n)
                    after(i, n, "inverse")
                    for j in range(J):
                        q = inverse[:, n, j, :].unsqueeze(2)
                        for at, width in ((0, 8), (S, 12)):
                            o = slice(at, at + HEADS * width)
                            ins = v.tensor_tensor(mean[:, n, j, o].rearrange("p (h k) -> p h k", h=HEADS),
                                                  e["sums"][:, n, j, o].rearrange("p (h k) -> p h k", h=HEADS),
                                                  q.broadcast_to([P, HEADS, width]), ALU.mult)
                    one(ins, n)
                for n in range(LANES):
                    x3 = rows[:, J * n:J * n + J, X3:X3 + F]
                    v.tensor_copy(base[:, n, :, S:F], x3[:, :, S:F])
                    one(v.tensor_tensor(base[:, n, :, 0:S], x3[:, :, 0:S],
                                        w["proj_b"][:, :].unsqueeze(1).broadcast_to([P, J, S]), ALU.add), n)
                    after(i, n, "with_bias")
                    v.wait_ge(t["pe"][n], count_at(t, i + 1, "pe", "projected"))
                    one(v.tensor_tensor(xp[:, n, :, :],
                                        banks[2 * n + 1][0:P, 0:J * F].rearrange("p (j f) -> p j f", j=J),
                                        base[:, n, :, :], ALU.add), n)
                    after(i, n, "x")
                    one(v.tensor_tensor(u[:, n, :, :], xp[:, n, :, :], x3, ALU.add), n)
                    ffn_measure(v, ffn, t, i + 1, n, [xp[:, n, j, 0:S] for j in range(J)],
                                [xp[:, n, j, S:F] for j in range(J)])
                    ffn_merge(v, ffn, t, i + 1, n)
                    ffn_square(v, ffn, t, i + 1, n)
                    ffn_widen(v, ffn, t, i + 1, n)
                for n in range(LANES):
                    ffn_root_attr(v, ffn, t, i + 1, n,
                                  rows[:, J * n:J * n + J, ATTR:ATTR + 1].rearrange("p j o -> p (j o)"))
                    ffn_normalize(v, ffn, t, i + 1, n, [xp[:, n, j, 0:S] for j in range(J)])
                for n in range(LANES):
                    ffn_gates(v, ffn, t, i + 1, n)
                for n in range(LANES):
                    ffn_add(v, ffn, t, i + 1, n, lambda j: rows[:, J * n + j, ATTR:ATTR + 1],
                            [u[:, n, j, :] for j in range(J)])
                    out_measure(v, ffn, t, i + 1, n)
                    out_merge(v, ffn, t, i + 1, n)
                    out_widen(v, ffn, t, i + 1, n)
                for n in range(LANES):
                    v.wait_ge(scattered, 16 * T * i + 16)
                    ffn_finish(v, ffn, t, i + 1, n, [res[:, n, j, :] for j in range(J)])

        @block.scalar
        def _(act):
            prime(act, t, "act")
            with act.Fori(0, rounds) as i:
                for n in range(LANES):
                    act.wait_ge(t["pe"][n], count_at(t, i + 1, "pe", "summed"))
                    for j in range(J):
                        ins = act.activation(e["sums"][:, n, j, 0:M], banks[2 * n + j][0:P, 0:M], ACT.Copy)
                    ins.then_inc(t["act"][n], 1)
                for n in range(LANES):
                    act.wait_ge(t["pe"][n], count_at(t, i + 1, "pe", "turned"))
                    act.activation(e["s_t"][:, n, :], banks[2 * n][0:S, 0:W], ACT.Copy)
                    act.activation(e["v_t"][:, n, :], banks[2 * n][0:V, W:2 * W], ACT.Copy
                                   ).then_inc(t["act"][n], 1)
                for n in range(LANES):
                    ffn_scale(act, ffn, t, i + 1, n, [xp[:, n, j, S:F] for j in range(J)],
                              rows[:, J * n:J * n + J, ATTR:ATTR + 1].rearrange("p j o -> p (j o)"))
                for n in range(LANES):
                    ffn_copy_turned(act, ffn, t, i + 1, n)
                for n in range(LANES):
                    ffn_sigmoid(act, ffn, t, i + 1, n)

        @block.tensor
        def _(pe):
            prime(pe, t, "pe")
            ident = w["ident"][0:P, 0:P]
            pe.wait_ge(ready, 1)
            with pe.Fori(0, rounds) as i:
                for n in range(LANES):
                    pe.wait_ge(t["dve"][n], count_at(t, i, "dve", "ffn_added"))
                    gate(pe, t)
                    pe.wait_ge(t["dve"][n], count_at(t, i + 1, "dve", "weighted"))
                    gate(pe, t)
                    pe.wait_ge(t["act"][n - 1], count_at(t, i + 1 if n else i, "act", "sums_copied"))
                    gate(pe, t)
                    run_sums(pe, e, banks, n, M).then_inc(t["pe"][n], 1)
                for n in range(LANES):
                    pe.wait_ge(t["dve"][n], count_at(t, i + 1, "dve", "divided"))
                    gate(pe, t)
                    for j in range(J):
                        pe.transpose(banks[2 * n][0:S, j * P:(j + 1) * P], mean[:, n, j, 0:S], ident)
                        ins = pe.transpose(banks[2 * n][0:V, W + j * P:W + (j + 1) * P], mean[:, n, j, S:F], ident)
                    ins.then_inc(t["pe"][n], 1)
                for n in range(LANES):
                    pe.wait_ge(t["act"][n], count_at(t, i + 1, "act", "turned_copied"))
                    gate(pe, t)
                    for j in range(J):
                        c, o = slice(j * P, (j + 1) * P), j * F
                        pe.matmul(banks[2 * n + 1][0:P, o:o + S], e["s_t"][:, n, c], w["proj_s"][:, :],
                                  start=True, stop=True)
                        ins = pe.matmul(banks[2 * n + 1][0:P, o + S:o + F], e["v_t"][:, n, c], w["proj_v"][:, :],
                                        start=True, stop=True)
                    ins.then_inc(t["pe"][n], 1)
                for n in range(LANES):
                    ffn_turn(pe, ffn, t, i + 1, n)
                for n in range(LANES):
                    ffn_hidden(pe, ffn, t, i + 1, n)
                for n in range(LANES):
                    ffn_out(pe, ffn, t, i + 1, n)


def semaphores(nc):
    taken = []

    def sem(name):
        taken.append(nc.alloc_semaphore(name=name))
        return taken[-1]

    def free():
        nc.clear_and_free_semaphores(taken)
        nc.all_engine_barrier()

    return sem, free


def program(nc, inp, out, nodes, edges, layers=4):
    tables = [nc.dram_tensor(f"table{l}", (nodes, ROW), F32).ap() for l in range(4)]
    kept = nc.dram_tensor("kept", (edges, KEPT), F32).ap()
    logits = nc.dram_tensor("logits", (edges, HEADS), F32).ap()
    probs = nc.dram_tensor("probs", (edges, HEADS), F32).ap()
    with ExitStack() as ctx:
        def place(scope, prefix=""):
            return lambda name, shape, dtype=F32: scope.enter_context(nc.sbuf_tensor(prefix + name, shape, dtype))

        banks = [ctx.enter_context(nc.psum_tensor(f"bank{n}", [128, 512], F32)) for n in range(8)]
        w = {}
        keep = place(ctx)
        with ExitStack() as phase:
            sem, free = semaphores(nc)
            prepare_weights(nc, sem, keep, place(phase), banks, inp, w)
            free()
        with ExitStack() as phase:
            sem, free = semaphores(nc)
            all_nodes(nc, sem, place(phase), banks, inp, w, ffn_buffers(place(phase), w, banks), tables, out, nodes)
            free()
        with ExitStack() as phase:
            sem, free = semaphores(nc)
            index = edge_index(nc, sem, keep, place(phase), banks, inp, w, nodes, edges)
            free()
        with ExitStack() as phase:
            e = edge_buffers(place(phase))
            for l in range(min(layers, 3)):
                with ExitStack() as layer:
                    sem, free = semaphores(nc)
                    edges_layer(nc, sem, place(layer), banks, inp, w, e, index, tables, l, nodes, edges)
                    free()
        if layers < 4:
            return
        with ExitStack() as phase:
            sem, free = semaphores(nc)
            attention_weights(nc, sem, keep, place(phase), banks, inp, w)
            free()
        with ExitStack() as phase:
            sem, free = semaphores(nc)
            attention_edges(nc, sem, place(phase), banks, inp, w, edge_buffers(place(phase, "att_")), index,
                            tables[3], kept, logits, edges)
            free()
        with ExitStack() as phase:
            sem, free = semaphores(nc)
            attention_softmax(nc, sem, place(phase), banks, inp, w, logits, probs, edges)
            free()
        with ExitStack() as phase:
            sem, free = semaphores(nc)
            attention_nodes(nc, sem, place(phase), banks, inp, w, edge_buffers(place(phase, "dest_")),
                            ffn_buffers(place(phase, "dest_"), w, banks), index, kept, probs, out, nodes, edges)
            free()


def kernel(**inputs):
    import concourse.bacc as bacc
    from concourse.bass_utils import run_bass_kernel_spmd

    nc = bacc.Bacc("TRN2", target_bir_lowering=False, num_devices=1)
    arrays = {name: np.ascontiguousarray(a) for name, a in inputs.items()}
    inp = {name: nc.dram_tensor(name, a.shape, mybir.dt.from_np(a.dtype), kind="ExternalInput").ap()
           for name, a in arrays.items()}
    nodes, edges = arrays["x"].shape[0], arrays["src"].shape[0]
    out = nc.dram_tensor("out", (nodes, F), F32, kind="ExternalOutput").ap()
    program(nc, inp, out, nodes, edges)
    return run_bass_kernel_spmd(nc, [arrays], core_ids=[0]).results[0]["out"]
```

```python
from contextlib import ExitStack

import numpy as np

import concourse.bass as bass
from concourse import mybir

ALU = mybir.AluOpType
ACT = mybir.ActivationFunctionType
AX = mybir.AxisListType
F32 = mybir.dt.float32
I32 = mybir.dt.int32

P = 125
J = 2
LANES = 4
ROWS = P * J * LANES
S, V, U = 64, 96, 32
F = S + V
W = P * J
MEAN, Q, A, ROW = F, F + 1, F + 2, F + 4
EPS = 1e-5


def lane_steps(sem, phase, **names):
    t = {e: [sem(f"{phase}_{e}_steps_lane{n}") for n in range(LANES)] for e in names}
    t["names"] = names
    t["turn"] = sem(f"{phase}_turns")
    return t


def count_at(t, i, engine, step):
    names = t["names"][engine]
    return i * len(names) + names.index(step) + 1


def prime(eng, t, engine):
    for n in range(LANES):
        eng.sem_inc(t[engine][n], len(t["names"][engine]))


def gate(eng, t):
    eng.sem_inc(t["turn"], 1)


def staggered(order, part):
    steps = []
    for step, begin in order:
        for n in range(LANES):
            behind, at = divmod(begin + n * part, LANES * part)
            steps.append((at, int(behind), n, step))
    return [(step, n, behind) for at, behind, n, step in sorted(steps, key=lambda entry: entry[0])]


def run_rounds(eng, rounds, order, part, steps):
    mine = [(step, n, behind) for step, n, behind in staggered(order, part) if step in steps]
    for step, n, behind in mine:
        if not behind:
            steps[step](n, 0)
    with eng.Fori(1, rounds) as i:
        for step, n, behind in mine:
            steps[step](n, i - behind)
    for step, n, behind in mine:
        if behind:
            steps[step](n, rounds - 1)


def keep_busy(pe, banks, w, fill):
    def fill_step(lead, odd, count):
        def step(n, i):
            for _ in range(count):
                pe.matmul(banks[2 * ((n + lead) % LANES) + odd][:, 0:128], w["ident"][:, :], w["ident"][:, :],
                          start=True, stop=True)
        return step

    return {f"keep_busy{k}": fill_step(*entry) for k, entry in enumerate(fill)}


FFN_PE = ["ffn_turned", "ffn_hidden", "ffn_out"]
FFN_ACT = ["ffn_scaled", "ffn_copied", "ffn_sigmoid"]
FFN_DVE = ["ffn_measured", "ffn_merged", "ffn_squared", "ffn_widened", "ffn_attr", "ffn_normed",
           "ffn_gated", "ffn_added", "out_measured", "out_merged", "out_widened", "out_normed"]
FFN_POOL = ["ffn_root", "out_root"]


def ffn_buffers(sb, w, banks):
    f = dict(w=w, banks=banks)
    for name, shape in (
            ("stats", [P, LANES, 4, 6]),
            ("moments", [P, LANES, 4, 2]),
            ("square", [P, LANES, 2]),
            ("wide", [P, LANES, 4]),
            ("root", [P, LANES, 4]),
            ("root_a", [P, LANES, 4]),
            ("sn", [P, LANES, J, S + 1]),
            ("vn", [P, LANES, J, V]),
            ("s_t", [S + 1, LANES, W]),
            ("v_t", [V, LANES, W]),
            ("sig", [128, LANES, 2 * W]),
            ("hid", [128, LANES, W]),
            ("hid_v01", [128, LANES, W]),
            ("hid_v2", [S + 1, LANES, W]),
            ("y", [P, LANES, J, F]),
            ("y_stats", [P, LANES, J, 6]),
            ("y_moments", [P, LANES, J, 2]),
            ("y_wide", [P, LANES, J]),
            ("y_root", [P, LANES, J]),
    ):
        f[name] = sb("ffn_" + name, shape)
    return f


def ffn_measure(v, f, t, i, n, xs, xv):
    for j in range(J):
        v.bn_stats(f["stats"][:, n, j, :], xs[j])
        ins = v.bn_stats(f["stats"][:, n, J + j, :], xv[j])
    ins.then_inc(t["dve"][n], 1)


def ffn_merge(v, f, t, i, n):
    v.wait_ge(t["dve"][n], count_at(t, i, "dve", "ffn_measured"))
    gate(v, t)
    for k in range(2 * J):
        ins = v.bn_aggr(f["moments"][:, n, k, :], f["stats"][:, n, k, :])
    ins.then_inc(t["dve"][n], 1)


def ffn_square(v, f, t, i, n):
    v.wait_ge(t["dve"][n], count_at(t, i, "dve", "ffn_merged"))
    mv = f["moments"][:, n, J:2 * J, 0:1]
    v.tensor_tensor(f["square"][:, n, :].unsqueeze(2), mv, mv, ALU.mult)
    v.tensor_scalar(f["wide"][:, n, 0:J].unsqueeze(2), f["moments"][:, n, 0:J, 1:2], EPS, None,
                    ALU.add).then_inc(t["dve"][n], 1)


def ffn_widen(v, f, t, i, n):
    v.wait_ge(t["dve"][n], count_at(t, i, "dve", "ffn_squared"))
    v.scalar_tensor_tensor(f["wide"][:, n, J:2 * J].unsqueeze(2), f["moments"][:, n, J:2 * J, 1:2], EPS,
                           f["square"][:, n, :].unsqueeze(2), ALU.add, ALU.add).then_inc(t["dve"][n], 1)


def ffn_root_attr(v, f, t, i, n, attr):
    v.wait_ge(t["pool"][n], count_at(t, i, "pool", "ffn_root"))
    v.tensor_tensor(f["root_a"][:, n, :].rearrange("p (k j) -> p k j", j=J),
                    f["root"][:, n, :].rearrange("p (k j) -> p k j", j=J),
                    attr.unsqueeze(1).broadcast_to([P, 2, J]), ALU.mult).then_inc(t["dve"][n], 1)


def ffn_normalize(v, f, t, i, n, xs):
    v.wait_ge(t["dve"][n], count_at(t, i, "dve", "ffn_attr"))
    for j in range(J):
        ins = v.tensor_scalar(f["sn"][:, n, j, 0:S], xs[j], f["moments"][:, n, j, 0:1],
                              f["root_a"][:, n, j:j + 1], ALU.subtract, ALU.mult)
    ins.then_inc(t["dve"][n], 1)


def ffn_gates(v, f, t, i, n):
    a, b = f["banks"][2 * n], f["banks"][2 * n + 1]
    v.wait_ge(t["act"][n], count_at(t, i, "act", "ffn_sigmoid"))
    v.tensor_tensor(f["hid"][:, n, :], b[:, 0:W], f["sig"][:, n, 0:W], ALU.mult)
    v.tensor_tensor(f["hid_v01"][:, n, :], a[:, 0:W], f["sig"][:, n, W:2 * W], ALU.mult)
    v.tensor_tensor(f["hid_v2"][0:S, n, :], a[0:S, W:2 * W], f["sig"][0:S, n, W:2 * W],
                    ALU.mult).then_inc(t["dve"][n], 1)


def ffn_add(v, f, t, i, n, attr_of, u):
    b = f["banks"][2 * n + 1]
    v.wait_ge(t["pe"][n], count_at(t, i, "pe", "ffn_out"))
    for j in range(J):
        ins = v.scalar_tensor_tensor(f["y"][:, n, j, :], b[0:P, j * F:(j + 1) * F], attr_of(j), u[j],
                                     ALU.mult, ALU.add)
    ins.then_inc(t["dve"][n], 1)


def out_measure(v, f, t, i, n):
    v.wait_ge(t["dve"][n], count_at(t, i, "dve", "ffn_added"))
    for j in range(J):
        ins = v.bn_stats(f["y_stats"][:, n, j, :], f["y"][:, n, j, :])
    ins.then_inc(t["dve"][n], 1)


def out_merge(v, f, t, i, n):
    v.wait_ge(t["dve"][n], count_at(t, i, "dve", "out_measured"))
    gate(v, t)
    for j in range(J):
        ins = v.bn_aggr(f["y_moments"][:, n, j, :], f["y_stats"][:, n, j, :])
    ins.then_inc(t["dve"][n], 1)


def out_widen(v, f, t, i, n):
    v.wait_ge(t["dve"][n], count_at(t, i, "dve", "out_merged"))
    v.tensor_scalar(f["y_wide"][:, n, :].unsqueeze(2), f["y_moments"][:, n, :, 1:2], EPS, None,
                    ALU.add).then_inc(t["dve"][n], 1)


def ffn_finish(v, f, t, i, n, out):
    v.wait_ge(t["pool"][n], count_at(t, i, "pool", "out_root"))
    for j in range(J):
        ins = v.tensor_scalar(out[j], f["y"][:, n, j, :], f["y_moments"][:, n, j, 0:1],
                              f["y_root"][:, n, j:j + 1], ALU.subtract, ALU.mult)
    ins.then_inc(t["dve"][n], 1)


def ffn_roots(p, f, t, i, n):
    p.wait_ge(t["dve"][n], count_at(t, i, "dve", "ffn_widened"))
    gate(p, t)
    p.tensor_tensor(f["root"][:, n, :], f["wide"][:, n, :], f["w"]["half"][:, 0:2 * J], ALU.pow
                    ).then_inc(t["pool"][n], 1)


def ffn_out_roots(p, f, t, i, n):
    p.wait_ge(t["dve"][n], count_at(t, i, "dve", "out_widened"))
    gate(p, t)
    p.tensor_tensor(f["y_root"][:, n, :], f["y_wide"][:, n, :], f["w"]["half"][:, 0:J], ALU.pow
                    ).then_inc(t["pool"][n], 1)


def ffn_scale(act, f, t, i, n, xv, attr):
    act.wait_ge(t["dve"][n], count_at(t, i, "dve", "ffn_attr"))
    act.activation(f["sn"][:, n, :, S:S + 1], attr.unsqueeze(2), ACT.Copy)
    for j in range(J):
        ins = act.activation(f["vn"][:, n, j, :], xv[j], ACT.Copy, scale=f["root_a"][:, n, J + j:J + j + 1])
    ins.then_inc(t["act"][n], 1)


def ffn_copy_turned(act, f, t, i, n):
    a = f["banks"][2 * n]
    act.wait_ge(t["pe"][n], count_at(t, i, "pe", "ffn_turned"))
    act.activation(f["s_t"][:, n, :], a[0:S + 1, 0:W], ACT.Copy)
    act.activation(f["v_t"][:, n, :], a[0:V, W:2 * W], ACT.Copy).then_inc(t["act"][n], 1)


def ffn_sigmoid(act, f, t, i, n):
    act.wait_ge(t["pe"][n], count_at(t, i, "pe", "ffn_hidden"))
    act.activation(f["sig"][:, n, :], f["banks"][2 * n + 1][:, 0:2 * W], ACT.Sigmoid
                   ).then_inc(t["act"][n], 1)


def ffn_turn(pe, f, t, i, n):
    a = f["banks"][2 * n]
    pe.wait_ge(t["dve"][n], count_at(t, i, "dve", "ffn_normed"))
    gate(pe, t)
    pe.wait_ge(t["act"][n], count_at(t, i, "act", "ffn_scaled"))
    gate(pe, t)
    for j in range(J):
        pe.transpose(a[0:S + 1, j * P:(j + 1) * P], f["sn"][:, n, j, :], f["w"]["ident"][0:P, 0:P])
        ins = pe.transpose(a[0:V, W + j * P:W + (j + 1) * P], f["vn"][:, n, j, :], f["w"]["ident"][0:P, 0:P])
    ins.then_inc(t["pe"][n], 1)


def ffn_hidden(pe, f, t, i, n):
    a, b = f["banks"][2 * n], f["banks"][2 * n + 1]
    pe.wait_ge(t["act"][n], count_at(t, i, "act", "ffn_copied"))
    gate(pe, t)
    f1s, f1v = f["w"]["f1_s"], f["w"]["f1_v"]
    pe.matmul(b[:, 0:W], f1s[:, 0:128], f["s_t"][:, n, :], start=True, stop=True)
    pe.matmul(b[:, W:2 * W], f1s[:, 128:256], f["s_t"][:, n, :], start=True, stop=True)
    pe.matmul(a[:, 0:W], f1v[:, 0:128], f["v_t"][:, n, :], start=True, stop=True)
    pe.matmul(a[0:S, W:2 * W], f1v[:, 128:192], f["v_t"][:, n, :], start=True, stop=True
              ).then_inc(t["pe"][n], 1)


def ffn_out(pe, f, t, i, n):
    b = f["banks"][2 * n + 1]
    pe.wait_ge(t["dve"][n], count_at(t, i, "dve", "ffn_gated"))
    gate(pe, t)
    for j in range(J):
        c, o = slice(j * P, (j + 1) * P), j * F
        pe.matmul(b[0:P, o:o + S], f["hid"][:, n, c], f["w"]["f2_s"][:, :], start=True, stop=True)
        pe.matmul(b[0:P, o + S:o + F], f["hid_v01"][:, n, c], f["w"]["f2_v01"][:, :], start=False,
                  stop=True, skip_group_check=True)
        ins = pe.matmul(b[0:P, o:o + F], f["hid_v2"][:, n, c], f["w"]["f2_v2"][:, :], start=False, stop=True,
                        skip_group_check=True)
    ins.then_inc(t["pe"][n], 1)


def lin_names(l):
    return [("L0_gnn_Wsc0", "L0_gnn_Wsc1", "L0_gnn_Wl1_0", "L0_gnn_Wl1_1"),
            ("L1_gnn_Wsc0", "L1_gnn_Wsc1", "L1_gnn_Wl1_0", "L1_gnn_Wl1_1"),
            ("L2_gnn_W_si0", "L2_gnn_W_si1", "L2_gnn_W_l1_0", "L2_gnn_W_l1_1")][l]



def prepare_weights(nc, sem, keep, sb, banks, inp, w):
    loaded = sem("weights_loaded")
    built = sem("weights_built")
    ident_made = sem("ident_made")
    sums_made = sem("column_sums_made")

    for name, shape in (("ident", [128, 128]), ("mod3", [V, 3]), ("half", [P, 16]), ("f2_s", [128, S]),
                        ("f1_s", [S + 1, 256]), ("f1_v", [V, 192]), ("f2_v01", [128, V]), ("f2_v2", [S + 1, F]),
                        ("proj_b", [P, S]),
                        *((f"{k}{l}", shape) for l in range(3) for k, shape in (
                            ("self_s", [S, S]), ("self_v", [V + 1, F]), ("lin_s", [S, 2 * S]), ("lin_v", [V, V])))):
        w[name] = keep(name, shape)
    w["minus_one"] = sb("minus_one", [V, V + 1])
    w["b0_column"] = sb("b0_column", [S, S + 1])
    loads = []

    def raw(name, shape, src, part=None):
        t = sb("raw_" + name, shape)
        loads.append((t[:, :], src))
        return t

    def thrice(name, src):
        t = sb("raw3_" + name, [V, src.shape[1]])
        loads.append((t[:, :], src.unsqueeze(1).broadcast_to([U, 3, src.shape[1]])))
        return t

    krons = []
    plain = []
    for l in range(3):
        n = lin_names(l)
        r = raw(n[0], [S, S], inp[n[0]])
        plain.append((w[f"self_s{l}"][:, :], r[:, :], S ** -0.5))
        krons.append((w[f"self_v{l}"][0:V, S:F], thrice(n[1], inp[n[1]]), U ** -0.5, False))
        r = raw(n[2], [S, S], inp[n[2]])
        plain.append((w[f"lin_s{l}"][:, 0:S], r[:, :], S ** -0.5))
        plain.append((w[f"lin_s{l}"][:, S:2 * S], r[:, :], S ** -0.5))
        krons.append((w[f"lin_v{l}"][:, :], thrice(n[3], inp[n[3]]), U ** -0.5, False))

    f1 = raw("f1_ws", [S, 192], inp["L3_gnn_f1_ws"])
    w0 = raw("ln2_w0", [S, 1], inp["L3_gnn_ln2_w0"].unsqueeze(1))
    b0 = raw("ln2_b0", [S, 1], inp["L3_gnn_ln2_b0"].unsqueeze(1))
    f1v = thrice("f1_wv", inp["L3_gnn_f1_wv"])
    w1 = thrice("ln2_w1", inp["L3_gnn_ln2_w1"].unsqueeze(1))
    f2v = sb("raw_f2_wv", [128, U])
    loads.append((f2v[0:64, :], inp["L3_gnn_f2_wv"]))
    loads.append((f2v[64:128, :], inp["L3_gnn_f2_wv"]))
    loads.append((w["f2_s"][:, :], inp["L3_gnn_f2_ws"]))
    f1b = sb("raw_f1_bs", [S + 1, 192])
    loads.append((f1b[S:S + 1, :], inp["L3_gnn_f1_bs"].unsqueeze(0)))
    f2b = sb("raw_f2_bs", [S + 1, S])
    loads.append((f2b[S:S + 1, :], inp["L3_gnn_f2_bs"].unsqueeze(0)))
    loads.append((w["proj_b"][:, :], inp["L3_gnn_proj_bs"].unsqueeze(0).broadcast_to([P, S])))

    with nc.Block() as block:
        @block.sync
        def _(sp):
            for dst, src in loads:
                sp.dma_start(dst, src).then_inc(loaded, 16)

        @block.gpsimd
        def _(p):
            p.memset(w["ident"][:, :], 0.0).then_inc(ident_made, 1)
            p.wait_ge(ident_made, 1)
            p.affine_select(out=w["ident"][:, :], in_=w["ident"][:, :], compare_op=ALU.not_equal, fill=1.0,
                            base=0, pattern=[[-1, 128]], channel_multiplier=1).then_inc(ident_made, 1)

        @block.vector
        def _(v):
            v.memset(w["half"][:, :], -0.5)
            v.memset(w["minus_one"][:, :], 0.0)
            v.memset(w["f2_v01"][:, :], 0.0)
            v.memset(w["f2_v2"][:, :], 0.0)
            v.memset(w["b0_column"][:, :], 0.0)
            for l in range(3):
                v.memset(w[f"self_v{l}"][:, :], 0.0)
            v.wait_ge(ident_made, 2)
            v.tensor_reduce(w["mod3"][:, :], w["ident"][0:V, 0:V].rearrange("p (u c) -> p c u", c=3), AX.X,
                            ALU.add).then_inc(built, 1)
            v.wait_ge(built, 1)
            v.memset(w["minus_one"][:, V:V + 1], -1.0)
            v.wait_ge(loaded, 16 * len(loads))
            for dst, src, k in plain:
                v.tensor_scalar(dst, src, k, None, ALU.mult)
            for dst, src, k, outer in krons:
                for c in range(3):
                    v.tensor_scalar(dst.rearrange("p (w c) -> p c w", c=3)[:, c, :], src[:, :],
                                    w["mod3"][:, c:c + 1], k, ALU.mult, ALU.mult)
            for c in range(3):
                v.tensor_scalar(w["f1_v"][:, c * 64:(c + 1) * 64], f1v[:, :], w["mod3"][:, c:c + 1], w1[:, 0:1],
                                ALU.mult, ALU.mult)
            for c in range(2):
                h = slice(c * 64, (c + 1) * 64)
                v.tensor_copy(w["f2_v01"][h, :].rearrange("p (k c) -> p c k", c=3)[:, c, :], f2v[h, :])
            v.tensor_copy(w["f2_v2"][0:S, S:F].rearrange("p (k c) -> p c k", c=3)[:, 2, :], f2v[0:64, :])
            v.tensor_copy(w["f2_v2"][S:S + 1, 0:S], f2b[S:S + 1, :])
            v.tensor_scalar(w["f1_s"][0:S, 0:192], f1[:, :], w0[:, 0:1], None, ALU.mult)
            v.tensor_scalar(w["f1_s"][0:S, 192:256], f1[:, 128:192], w0[:, 0:1], None, ALU.mult)
            v.tensor_copy(w["b0_column"][:, S:S + 1], b0[:, :]).then_inc(built, 1)
            v.wait_ge(sums_made, 1)
            for l in range(3):
                v.tensor_copy(w[f"self_v{l}"][V:V + 1, :], banks[l][V:V + 1, 0:F])
            v.tensor_tensor(w["f1_s"][S:S + 1, 0:192], banks[3][S:S + 1, 0:192], f1b[S:S + 1, :], ALU.add)
            v.tensor_tensor(w["f1_s"][S:S + 1, 192:256], banks[3][S:S + 1, 128:192], f1b[S:S + 1, 128:192],
                            ALU.add).then_inc(built, 1)

        @block.tensor
        def _(pe):
            pe.wait_ge(built, 2)
            for l in range(3):
                pe.matmul(banks[l][0:V + 1, 0:S], w["minus_one"][0:S, :], w[f"self_s{l}"][:, :],
                          start=True, stop=True)
                pe.matmul(banks[l][0:V + 1, S:F], w["minus_one"][:, :], w[f"self_v{l}"][0:V, S:F],
                          start=True, stop=True)
            pe.matmul(banks[3][0:S + 1, 0:192], w["b0_column"][:, :], f1[:, :],
                      start=True, stop=True).then_inc(sums_made, 1)


def all_nodes(nc, sem, sb, banks, inp, w, ffn, tables, out, nodes):
    rounds = nodes // ROWS
    own = nodes // P
    T = LANES * J
    names = dict(pe=[], act=[], dve=[], pool=["attr_copied"])
    for l in range(3):
        names["pe"] += [f"turned{l}", f"multiplied{l}"]
        names["act"] += [f"copied{l}"]
        names["dve"] += [f"added{l}", f"measured{l}", f"merged{l}", f"widened{l}"]
    names["dve"] += ["x3", "shifted"] + FFN_DVE
    names["pool"] += ["root3", "doubled"] + FFN_POOL
    names["pe"] += FFN_PE
    names["act"] += FFN_ACT
    t = lane_steps(sem, "nodes", **names)
    x_loaded = [sem(f"nodes_x_loaded_lane{n}") for n in range(LANES)]
    stored = [[sem(f"nodes_table{l}_stored_lane{n}") for n in range(LANES)] for l in range(4)]
    out_stored = [sem(f"nodes_out_stored_lane{n}") for n in range(LANES)]
    attr_loaded = sem("nodes_attr_loaded")
    ready = sem("nodes_constants_ready")
    part = 11.62
    order = [("load_x", 0.0), ("keep_busy0", 2.24), ("store0", 2.7), ("attr", 2.8), ("turn0", 3.0),
             ("copy0", 4.2), ("multiply0", 5.1), ("add0", 6.4), ("measure0", 7.1), ("merge0", 7.8),
             ("keep_busy1", 7.87), ("widen0", 8.0), ("store1", 8.3), ("turn1", 8.4), ("keep_busy2", 8.86),
             ("copy1", 9.2), ("multiply1", 10.1), ("add1", 11.4), ("measure1", 12.1), ("keep_busy3", 12.42),
             ("merge1", 12.8), ("widen1", 13.0), ("store2", 13.3), ("turn2", 13.4), ("copy2", 14.2),
             ("multiply2", 15.1), ("add2", 16.4), ("measure2", 17.1), ("merge2", 17.8), ("widen2", 18.1),
             ("store3", 18.4), ("root3", 18.6), ("divide", 19.4), ("shift", 20.1), ("measure", 20.4),
             ("double", 21.2), ("merge", 22.2), ("square", 24.4), ("widen", 24.6), ("roots", 24.9),
             ("root_attr", 26.0), ("normalize", 26.2), ("scale", 26.8), ("ffn_turn", 27.7), ("ffn_copy", 28.5),
             ("hidden", 29.4), ("sigmoid", 31.4), ("gates", 32.6), ("ffn_out", 34.2), ("residual", 36.0),
             ("out_measure", 36.7), ("out_merge", 37.4), ("out_widen", 37.6), ("out_roots", 38.0),
             ("finish", 38.7), ("store_out", 39.5)]
    fill = [(0, 0, 3), (0, 0, 2), (0, 1, 5), (0, 0, 4)]
    attr = sb("node_attr", [P, own])
    z = sb("nodes_z", [P, 4, T, ROW])
    s_t = sb("nodes_s_t", [S, LANES, W])
    v_t = sb("nodes_v_t", [V + 1, LANES, W])
    root3 = sb("nodes_root3", [P, LANES, J])
    x3 = sb("nodes_x3", [P, T, F])
    xps = sb("nodes_xps", [P, T, S])
    u = sb("nodes_u", [P, T, F])
    res = sb("nodes_res", [P, T, F])
    x_view = inp["x"].rearrange("(p r) f -> p r f", p=P)
    out_view = out.rearrange("(p r) f -> p r f", p=P)
    table_view = [x.rearrange("(p r) f -> p r f", p=P) for x in tables]

    def tiles(n):
        return slice(J * n, J * n + J)

    with nc.Block() as block:
        @block.sync
        def _(sp):
            for n in range(LANES):
                for l in range(4):
                    sp.sem_inc(stored[l][n], 16)
                sp.sem_inc(out_stored[n], 16)
            sp.dma_start(attr[:, :], inp["node_vec1"].rearrange("(p r) o -> p (r o)", p=P)).then_inc(attr_loaded, 16)
            sp.wait_ge(ready, 2)

            def load_x(n, i):
                sp.wait_ge(t["dve"][n], count_at(t, i, "dve", "added0"))
                gate(sp, t)
                sp.wait_ge(stored[0][n], 16 * i + 16)
                gate(sp, t)
                sp.dma_start(z[:, 0, tiles(n), 0:F], x_view[:, bass.ds(i * T + J * n, J), :]
                             ).then_inc(x_loaded[n], 16)

            def store_table(l):
                def store(n, i):
                    if l:
                        sp.wait_ge(t["dve"][n], count_at(t, i + 1, "dve", f"widened{l - 1}"))
                        gate(sp, t)
                    else:
                        sp.wait_ge(t["pool"][n], count_at(t, i + 1, "pool", "attr_copied"))
                        gate(sp, t)
                        sp.wait_ge(x_loaded[n], 16 * i + 16)
                        gate(sp, t)
                    sp.dma_start(table_view[l][:, bass.ds(i * T + J * n, J), :], z[:, l, tiles(n), :]
                                 ).then_inc(stored[l][n], 16)
                return store

            def store_out(n, i):
                sp.wait_ge(t["dve"][n], count_at(t, i + 1, "dve", "out_normed"))
                gate(sp, t)
                sp.dma_start(out_view[:, bass.ds(i * T + J * n, J), :], res[:, tiles(n), :]
                             ).then_inc(out_stored[n], 16)

            run_rounds(sp, rounds, order, part, dict(load_x=load_x, store_out=store_out,
                                               **{f"store{l}": store_table(l) for l in range(4)}))
            for n in range(LANES):
                for l in range(4):
                    sp.wait_ge(stored[l][n], 16 * rounds + 16)
                sp.wait_ge(out_stored[n], 16 * rounds + 16)

        @block.gpsimd
        def _(p):
            prime(p, t, "pool")
            p.wait_ge(attr_loaded, 16)
            p.wait_ge(ready, 2)

            def copy_attr(n, i):
                p.wait_ge(t["dve"][n], count_at(t, i, "dve", "ffn_added"))
                gate(p, t)
                for l in range(4):
                    p.wait_ge(stored[l][n], 16 * i + 16)
                    gate(p, t)
                p.tensor_copy(z[:, :, tiles(n), A:A + 1],
                              attr[:, bass.ds(i * T + J * n, J)].unsqueeze(1).unsqueeze(3)
                              .broadcast_to([P, 4, J, 1])).then_inc(t["pool"][n], 1)

            def take_root3(n, i):
                p.wait_ge(t["dve"][n], count_at(t, i + 1, "dve", "widened2"))
                gate(p, t)
                p.tensor_tensor(root3[:, n, :].unsqueeze(2), z[:, 3, tiles(n), Q:Q + 1],
                                w["half"][:, 0:J].unsqueeze(2), ALU.pow).then_inc(t["pool"][n], 1)

            def double(n, i):
                p.wait_ge(t["dve"][n], count_at(t, i + 1, "dve", "shifted"))
                gate(p, t)
                p.tensor_tensor(u[:, tiles(n), 0:S], x3[:, tiles(n), 0:S], xps[:, tiles(n), :], ALU.add)
                p.tensor_tensor(u[:, tiles(n), S:F], x3[:, tiles(n), S:F], x3[:, tiles(n), S:F], ALU.add
                                ).then_inc(t["pool"][n], 1)

            run_rounds(p, rounds, order, part, dict(
                attr=copy_attr, root3=take_root3, double=double,
                roots=lambda n, i: ffn_roots(p, ffn, t, i + 1, n),
                out_roots=lambda n, i: ffn_out_roots(p, ffn, t, i + 1, n)))

        @block.vector
        def _(v):
            v.memset(z[:, :, :, MEAN:ROW], 0.0).then_inc(ready, 1)
            v.memset(ffn["hid_v2"][S:S + 1, :, :], 1.0)
            v.wait_ge(ready, 1)
            v.memset(z[:, 0, :, Q:Q + 1], 1.0).then_inc(ready, 1)
            prime(v, t, "dve")

            def add(l):
                def step(n, i):
                    v.wait_ge(t["pe"][n], count_at(t, i + 1, "pe", f"multiplied{l}"))
                    v.wait_ge(t["pool"][n], count_at(t, i + 1, "pool", "attr_copied"))
                    for j in range(J):
                        k = J * n + j
                        ins = v.scalar_tensor_tensor(z[:, l + 1, k, 0:F], banks[2 * n + 1][0:P, j * F:(j + 1) * F],
                                                     z[:, l, k, A:A + 1], z[:, l, k, 0:F], ALU.mult, ALU.add)
                    ins.then_inc(t["dve"][n], 1)
                return step

            def measure(l):
                def step(n, i):
                    v.wait_ge(t["dve"][n], count_at(t, i + 1, "dve", f"added{l}"))
                    for j in range(J):
                        ins = v.bn_stats(ffn["y_stats"][:, n, j, :], z[:, l + 1, J * n + j, 0:F])
                    ins.then_inc(t["dve"][n], 1)
                return step

            def merge(l):
                def step(n, i):
                    v.wait_ge(t["dve"][n], count_at(t, i + 1, "dve", f"measured{l}"))
                    gate(v, t)
                    for j in range(J):
                        ins = v.bn_aggr(z[:, l + 1, J * n + j, MEAN:Q + 1], ffn["y_stats"][:, n, j, :])
                    ins.then_inc(t["dve"][n], 1)
                return step

            def widen(l):
                def step(n, i):
                    v.wait_ge(t["dve"][n], count_at(t, i + 1, "dve", f"merged{l}"))
                    v.scalar_tensor_tensor(z[:, l + 1, tiles(n), Q:Q + 1], z[:, l, tiles(n), Q:Q + 1], EPS,
                                           z[:, l + 1, tiles(n), Q:Q + 1], ALU.mult, ALU.add
                                           ).then_inc(t["dve"][n], 1)
                return step

            def divide(n, i):
                v.wait_ge(t["pool"][n], count_at(t, i + 1, "pool", "root3"))
                for j in range(J):
                    k = J * n + j
                    ins = v.tensor_scalar(x3[:, k, :], z[:, 3, k, 0:F], z[:, 3, k, MEAN:MEAN + 1],
                                          root3[:, n, j:j + 1], ALU.subtract, ALU.mult)
                ins.then_inc(t["dve"][n], 1)

            def shift(n, i):
                v.wait_ge(t["dve"][n], count_at(t, i + 1, "dve", "x3"))
                v.tensor_tensor(xps[:, tiles(n), :], x3[:, tiles(n), 0:S], w["proj_b"][:, :].unsqueeze(1)
                                .broadcast_to([P, J, S]), ALU.add).then_inc(t["dve"][n], 1)

            def measure_parts(n, i):
                v.wait_ge(t["dve"][n], count_at(t, i + 1, "dve", "shifted"))
                ffn_measure(v, ffn, t, i + 1, n, [xps[:, J * n + j, :] for j in range(J)],
                            [x3[:, J * n + j, S:F] for j in range(J)])

            def root_attr(n, i):
                ffn_root_attr(v, ffn, t, i + 1, n, z[:, 0, tiles(n), A:A + 1].rearrange("p j o -> p (j o)"))

            def normalize(n, i):
                ffn_normalize(v, ffn, t, i + 1, n, [xps[:, J * n + j, :] for j in range(J)])

            def residual(n, i):
                v.wait_ge(t["pool"][n], count_at(t, i + 1, "pool", "doubled"))
                ffn_add(v, ffn, t, i + 1, n, lambda j: z[:, 0, J * n + j, A:A + 1],
                        [u[:, J * n + j, :] for j in range(J)])

            def finish(n, i):
                v.wait_ge(out_stored[n], 16 * i + 16)
                ffn_finish(v, ffn, t, i + 1, n, [res[:, J * n + j, :] for j in range(J)])

            by_layer = {}
            for l in range(3):
                by_layer.update({f"add{l}": add(l), f"measure{l}": measure(l), f"merge{l}": merge(l),
                                 f"widen{l}": widen(l)})
            run_rounds(v, rounds, order, part, dict(
                **by_layer, divide=divide, shift=shift, measure=measure_parts,
                merge=lambda n, i: ffn_merge(v, ffn, t, i + 1, n), square=lambda n, i: ffn_square(v, ffn, t, i + 1, n),
                widen=lambda n, i: ffn_widen(v, ffn, t, i + 1, n), root_attr=root_attr, normalize=normalize,
                gates=lambda n, i: ffn_gates(v, ffn, t, i + 1, n), residual=residual,
                out_measure=lambda n, i: out_measure(v, ffn, t, i + 1, n),
                out_merge=lambda n, i: out_merge(v, ffn, t, i + 1, n),
                out_widen=lambda n, i: out_widen(v, ffn, t, i + 1, n), finish=finish))

        @block.scalar
        def _(act):
            prime(act, t, "act")

            def copy(l):
                def copy_turned(n, i):
                    act.wait_ge(t["pe"][n], count_at(t, i + 1, "pe", f"turned{l}"))
                    act.activation(s_t[:, n, :], banks[2 * n][0:S, 0:W], ACT.Copy)
                    act.activation(v_t[:, n, :], banks[2 * n][0:V + 1, W:2 * W], ACT.Copy
                                   ).then_inc(t["act"][n], 1)
                return copy_turned

            def scale(n, i):
                ffn_scale(act, ffn, t, i + 1, n, [x3[:, J * n + j, S:F] for j in range(J)],
                          z[:, 0, tiles(n), A:A + 1].rearrange("p j o -> p (j o)"))

            run_rounds(act, rounds, order, part, dict(
                copy0=copy(0), copy1=copy(1), copy2=copy(2), scale=scale,
                ffn_copy=lambda n, i: ffn_copy_turned(act, ffn, t, i + 1, n),
                sigmoid=lambda n, i: ffn_sigmoid(act, ffn, t, i + 1, n)))

        @block.tensor
        def _(pe):
            prime(pe, t, "pe")
            ident = w["ident"][0:P, 0:P]

            def turn(l):
                def turn_rows(n, i):
                    if l == 0:
                        pe.wait_ge(x_loaded[n], 16 * i + 16)
                        gate(pe, t)
                        pe.wait_ge(t["dve"][n], count_at(t, i, "dve", "ffn_added"))
                    else:
                        pe.wait_ge(t["dve"][n], count_at(t, i + 1, "dve", f"merged{l - 1}"))
                    gate(pe, t)
                    for j in range(J):
                        k = J * n + j
                        pe.transpose(banks[2 * n][0:S, j * P:(j + 1) * P], z[:, l, k, 0:S], ident)
                        ins = pe.transpose(banks[2 * n][0:V + 1, W + j * P:W + (j + 1) * P], z[:, l, k, S:F + 1],
                                           ident)
                    ins.then_inc(t["pe"][n], 1)
                return turn_rows

            def multiply(l):
                def multiply_rows(n, i):
                    pe.wait_ge(t["act"][n], count_at(t, i + 1, "act", f"copied{l}"))
                    gate(pe, t)
                    for j in range(J):
                        c, o = slice(j * P, (j + 1) * P), j * F
                        pe.matmul(banks[2 * n + 1][0:P, o:o + S], s_t[:, n, c], w[f"self_s{l}"][:, :],
                                  start=True, stop=True)
                        ins = pe.matmul(banks[2 * n + 1][0:P, o:o + F], v_t[:, n, c], w[f"self_v{l}"][:, :],
                                        start=False, stop=True, skip_group_check=True)
                    ins.then_inc(t["pe"][n], 1)
                return multiply_rows

            run_rounds(pe, rounds, order, part, dict(
                **keep_busy(pe, banks, w, fill),
                **{f"turn{l}": turn(l) for l in range(3)}, **{f"multiply{l}": multiply(l) for l in range(3)},
                ffn_turn=lambda n, i: ffn_turn(pe, ffn, t, i + 1, n),
                hidden=lambda n, i: ffn_hidden(pe, ffn, t, i + 1, n),
                ffn_out=lambda n, i: ffn_out(pe, ffn, t, i + 1, n)))


def edge_weights(nc, sem, sb, inp, w, l):
    loaded = sem(f"edge{l}_weights_loaded")
    zeroed = sem(f"edge{l}_weights_zeroed")
    loads = []

    def raw(name, shape, src, at=None):
        t = sb(f"edge{l}_raw_{name}", shape)
        loads.append((t[:, :] if at is None else t[at, :], src))
        return t

    n = f"L{l}_gnn_"
    if l < 2:
        first, last = inp[n + "Wfc1"], inp[n + ("Wfc3" if l == 0 else "Wfc2")]
        s_s, s_v = inp[n + "Wl2_s"][0:S, :], inp[n + "Wl2_s"][S:S + U, :]
        v_s, v_v = inp[n + "Wl2_v"][0:S, :], inp[n + "Wl2_v"][S:S + U, :]
        wa = inp[n + "Wa"]
        fan = (S + U) ** -0.5 * (32.0 ** -0.5 if l == 0 else 1.0)
        last_factor = S ** -0.5
    else:
        first, last = inp[n + "W_fc1"], inp[n + "W_fc2"]
        s_s, s_v, v_s, v_v = (inp[n + "W_l2_" + k] for k in ("00", "10", "01", "11"))
        wa = None
        fan = (S + U) ** -0.5 * 16.0 ** -0.5 * 0.5
        last_factor = 2.0 ** 0.5 * 100 ** -0.5
    basis, hid = first.shape
    w["fc1"] = raw("fc1", [basis, hid], first)
    w["fc2"] = raw("fc2", [S, S], inp[n + "Wfc2"]) if l == 0 else None
    r_last = raw("last", [hid, 192], last)
    w["fc_last"] = sb(f"edge{l}_fc_last", [hid, 128 + 2 * V])
    r_ss = raw("s_s", [128, S], s_s, slice(0, S))
    r_vs = raw("v_s", [128, U], v_s, slice(S, 128))
    r_sv = raw("s_v", [V, S], s_v.unsqueeze(1).broadcast_to([U, 3, S]))
    r_vv = raw("v_v", [V, U], v_v.unsqueeze(1).broadcast_to([U, 3, U]))
    if wa is not None:
        r_wa = raw("wa_s", [S, 1], wa[0:S, :])
        r_wav = raw("wa_v", [V, 1], wa[S:S + U, :].unsqueeze(1).broadcast_to([U, 3, 1]))
    w["msg_a"] = sb(f"edge{l}_msg_a", [128, 1 + S + U])
    w["msg_c"] = sb(f"edge{l}_msg_c", [V, V])
    w["msg_d"] = sb(f"edge{l}_msg_d", [V, 3 * (1 + S)])

    with nc.Block() as block:
        @block.sync
        def _(sp):
            for dst, src in loads:
                sp.dma_start(dst, src).then_inc(loaded, 16)

        @block.vector
        def _(v):
            v.memset(w["msg_a"][:, :], 0.0)
            v.memset(w["msg_d"][:, :], 0.0).then_inc(zeroed, 1)
            v.wait_ge(zeroed, 1)
            v.wait_ge(loaded, 16 * len(loads))
            v.tensor_scalar(w["fc_last"][:, 0:128], r_last[:, 0:128], last_factor, None, ALU.mult)
            for k in range(2):
                v.tensor_scalar(w["fc_last"][:, 128 + k * V:128 + (k + 1) * V].rearrange("p (u c) -> p u c", c=3),
                                r_last[:, 128 + k * U:128 + (k + 1) * U].unsqueeze(2).broadcast_to([hid, U, 3]),
                                last_factor, None, ALU.mult)
            v.tensor_scalar(w["msg_a"][0:S, 1:1 + S], r_ss[0:S, :], fan, None, ALU.mult)
            v.tensor_scalar(w["msg_a"][S:128, 1 + S:1 + S + U], r_vs[S:128, :], fan, None, ALU.mult)
            if wa is not None:
                v.tensor_scalar(w["msg_a"][0:S, 0:1], r_wa[:, :], fan, None, ALU.mult)
            for c in range(3):
                m = w["mod3"][:, c:c + 1]
                v.tensor_scalar(w["msg_c"][:, :].rearrange("p (w c) -> p c w", c=3)[:, c, :], r_vv[:, :], m, fan,
                                ALU.mult, ALU.mult)
                o = c * (1 + S)
                v.tensor_scalar(w["msg_d"][:, o + 1:o + 1 + S], r_sv[:, :], m, fan * 3 ** -0.5, ALU.mult, ALU.mult)
                if wa is not None:
                    v.tensor_scalar(w["msg_d"][:, o:o + 1], r_wav[:, :], m, fan * 3 ** -0.5, ALU.mult, ALU.mult)
    return basis, hid


def edge_index(nc, sem, sb, scratch, banks, inp, w, nodes, edges):
    index = {}
    tiles = edges // P
    pairs = tiles // J
    padded = tiles + LANES * J
    index["ends"] = sb("edge_ends", [P, 2, padded], I32)
    index["keys"] = sb("edge_keys", [P, 2, padded])
    index["src_i"], index["dst_i"] = index["ends"][:, 0, :], index["ends"][:, 1, :]
    index["dst_f"], index["before"] = index["keys"][:, 0, :], index["keys"][:, 1, :]
    index["into_i"] = sb("into_i", [P, padded], I32)
    rows = [scratch(f"{k}_rows", [pairs, W], I32) for k in ("src", "dst", "next")]
    rows_f = [scratch(f"{k}_rows_f", [pairs, W]) for k in ("src", "dst", "next")]
    nxt = scratch("dst_next", [P, padded])
    same = scratch("dst_same", [P, padded])
    loaded = sem("index_loaded")
    zeroed = sem("index_zeroed")
    floats = sem("index_floats")
    turned = sem("index_turned")
    split = sem("index_split")
    moved = sem("index_moved")
    row_view = [inp[k].rearrange("(q c) -> q c", c=W) for k in ("src", "dst")]
    dst = inp["dst"]
    with nc.Block() as block:
        @block.sync
        def _(sp):
            for k in range(2):
                sp.dma_start(rows[k][:, :], row_view[k]).then_inc(loaded, 16)
            sp.wait_ge(zeroed, 1)
            sp.dma_start(rows[2][0:pairs - 1, :], dst[1:1 + (pairs - 1) * W].rearrange("(q c) -> q c", c=W)
                         ).then_inc(loaded, 16)
            sp.dma_start(rows[2][pairs - 1:pairs, 0:W - 1], dst[1 + (pairs - 1) * W:edges].unsqueeze(0)
                         ).then_inc(loaded, 16)
            sp.wait_ge(split, 1)
            sp.dma_start(index["before"][P - 1:P, 1:tiles], index["dst_f"][P - 1:P, 0:tiles - 1]).then_inc(moved, 16)
            sp.wait_ge(moved, 16)

        @block.vector
        def _(v):
            v.memset(rows[2][:, :], -1).then_inc(zeroed, 1)
            v.memset(index["before"][:, :], -1.0)
            v.memset(index["dst_f"][:, :], 0.0)
            v.memset(nxt[:, :], 0.0)
            v.memset(index["src_i"][:, :], 0)
            v.memset(index["dst_i"][:, :], 0)
            v.memset(index["into_i"][:, :], 0)
            v.wait_ge(loaded, 64)
            for k in range(3):
                ins = v.tensor_copy(rows_f[k][:, :], rows[k][:, :])
            ins.then_inc(floats, 1)
            v.wait_ge(turned, 1)

            def columns(t, j):
                return t[:, 0:tiles].rearrange("p (q j) -> p j q", j=J)[:, j, :]

            for j in range(J):
                o = slice(j * 128, j * 128 + pairs)
                v.tensor_copy(columns(index["src_i"], j), banks[0][0:P, o])
                v.tensor_copy(columns(index["dst_i"], j), banks[1][0:P, o])
                v.tensor_copy(columns(index["dst_f"], j), banks[1][0:P, o])
                ins = v.tensor_copy(columns(nxt, j), banks[2][0:P, o])
            ins.then_inc(split, 1)
            v.wait_ge(split, 1)
            v.tensor_tensor(same[:, :], index["dst_f"][:, :], nxt[:, :], ALU.is_equal).then_inc(split, 1)
            v.wait_ge(split, 2)
            v.scalar_tensor_tensor(index["into_i"][:, :], same[:, :], float(nodes), index["dst_f"][:, :],
                                   ALU.mult, ALU.add)

        @block.tensor
        def _(pe):
            pe.wait_ge(floats, 1)
            for k in range(3):
                for j in range(J):
                    ins = pe.transpose(banks[k][0:P, j * 128:j * 128 + pairs],
                                       rows_f[k][:, j * P:(j + 1) * P], w["ident"][0:pairs, 0:pairs])
            ins.then_inc(turned, 1)
    return index


def edge_buffers(sb):
    e = {}
    T = LANES * J
    for name, shape, dtype in (
            ("rows", [P, LANES, 2, J, ROW], F32),
            ("ends_now", [P, 2, T], I32),
            ("into_now", [P, T], I32),
            ("key_now", [P, 2, T], F32),
            ("dst_row", [P, LANES, W], I32),
            ("first", [P, LANES], F32),
            ("y", [P, T, 4], F32),
            ("attrs", [P, T, 64], F32),
            ("root", [P, LANES, 2, J], F32),
            ("root_a", [P, LANES, J], F32),
            ("xs", [P, LANES, J, F], F32),
            ("xd", [P, LANES, J, F], F32),
            ("attr_t", [64, LANES, W], F32),
            ("s_t", [S, LANES, W], F32),
            ("v_t", [V, LANES, W], F32),
            ("ds_t", [S, LANES, W], F32),
            ("dv_t", [V, LANES, W], F32),
            ("h", [128, LANES, W], F32),
            ("h2", [128, LANES, W], F32),
            ("f01", [128, LANES, W], F32),
            ("fv", [V, LANES, W], F32),
            ("p01", [128, LANES, W], F32),
            ("p2", [V, LANES, W], F32),
            ("p3", [V, LANES, W], F32),
            ("same0", [P, LANES, W], F32),
            ("same1", [P, LANES, P], F32),
            ("carry", [P, LANES, W], F32),
            ("msg", [P, LANES, J, 184], F32),
            ("sums", [P, LANES, J, 184], F32),
            ("new", [P, LANES, J, ROW], F32),
            ("part", [P, LANES, J], F32),
            ("factor", [P, LANES, J], F32),
            ("stats", [P, LANES, J, 6], F32),
    ):
        e[name] = sb("edge_" + name, shape, dtype)
    return e


def masks(v, t, e, i, n):
    k = J * n
    v.tensor_scalar(e["same0"][:, n, :], e["dst_row"][:, n, :], e["key_now"][:, 0, k:k + 1], None, ALU.is_equal)
    v.tensor_scalar(e["same1"][:, n, :], e["dst_row"][:, n, P:W], e["key_now"][:, 0, k + 1:k + 2], None, ALU.is_equal)
    v.tensor_scalar(e["carry"][:, n, :], e["dst_row"][:, n, :], e["key_now"][:, 1, k:k + 1], None, ALU.is_equal
                    ).then_inc(t["dve"][n], 1)


def run_sums(pe, e, banks, n, m):
    before = e["sums"][:, (n - 1) % LANES, J - 1, 0:m]
    pe.matmul(banks[2 * n][0:P, 0:m], e["same0"][:, n, 0:P], e["msg"][:, n, 0, 0:m], start=True, stop=False)
    pe.matmul(banks[2 * n][0:P, 0:m], e["carry"][:, n, 0:P], before, start=False, stop=True)
    pe.matmul(banks[2 * n + 1][0:P, 0:m], e["same0"][:, n, P:W], e["msg"][:, n, 0, 0:m], start=True, stop=False)
    pe.matmul(banks[2 * n + 1][0:P, 0:m], e["same1"][:, n, :], e["msg"][:, n, 1, 0:m], start=False, stop=False)
    return pe.matmul(banks[2 * n + 1][0:P, 0:m], e["carry"][:, n, P:W], before, start=False, stop=True)


def edges_layer(nc, sem, sb, banks, inp, w, e, index, tables, l, nodes, edges):
    basis, hid = edge_weights(nc, sem, sb, inp, w, l)
    T = LANES * J
    rounds = edges // ROWS
    M = 1 + F + 1
    attrs = inp[("edge_attr_8", "edge_attr_16", "edge_attr_10")[l]].rearrange("(t p) f -> p t f", p=P)
    y_view = inp["edge_attr_4"].rearrange("(t p) f -> p t f", p=P)
    source, target = tables[l], tables[l + 1]
    two = ["hidden2"] * (l == 0), ["activated2"] * (l == 0)
    factors = [["half_factor"], ["count", "inverse", "part", "half_factor"], []][l]
    t = lane_steps(sem, f"edges{l}",
              pe=["attr_turned", "src_turned", "hidden1", "dst_turned", *two[0], "linear", "weights", "messages",
                  "summed"],
              act=["attr_kept", "attr_copied", "src_copied", "activated1", "dst_copied", *two[1], "linear_copied",
                   "sums_copied"],
              dve=["root_attr", "normed", "masked", "products", "combined0", "combined1", "combined2", "combined3",
                   *factors, "factor", "self_added", "added", "measured", "merged", "widened"],
              pool=["keys", "roots"])
    part = 10.70
    order = [("load", 0.0), ("keep_attr", 0.0), ("keep_busy0", 1.41), ("turn_attr", 2.9), ("copy_keys", 3.75),
             ("roots", 3.95), ("copy_attr", 4.15), ("root_attr", 5.1), ("normalize", 5.3), ("mask", 6.4),
             ("gather_next", 6.65), ("turn_src", 7.05), ("hidden1", 7.5), ("copy_src", 7.85),
             ("activate1", 8.4), ("turn_dst", 8.7), ("hidden2", 9.15), ("copy_dst", 9.5), ("activate2", 10.05),
             ("linear", 11.25), ("copy_linear", 12.9), ("weights", 13.85), ("products", 17.85),
             ("messages", 20.3), ("combine0", 22.2), ("combine1", 23.15), ("combine2", 24.0),
             ("combine3", 24.85), ("add_up", 25.85), ("copy_sums", 28.7), ("limit_count", 29.4),
             ("invert", 29.6), ("part_attr", 29.8), ("half_factor", 30.0), ("whole_factor", 30.2),
             ("add_self", 30.4), ("add_messages", 31.1), ("measure", 31.8), ("merge", 32.5), ("widen", 32.75),
             ("scatter", 33.1)]
    fill = [(3, 1, 6)]
    gathered = [sem(f"edges{l}_rows_gathered_lane{n}") for n in range(LANES)]
    attrs_loaded = [sem(f"edges{l}_attrs_loaded_lane{n}") for n in range(LANES)]
    scattered = [sem(f"edges{l}_rows_scattered_lane{n}") for n in range(LANES)]
    index_copied = [sem(f"edges{l}_index_copied_lane{n}") for n in range(LANES)]
    ready = sem(f"edges{l}_ready")

    func, scale = [(ACT.Gelu_apprx_tanh, 8 ** -0.5), (ACT.Silu, 0.25), (ACT.Relu, 10 ** -0.5)][l]

    with nc.Block() as block:
        @block.sync
        def _(sp):
            def load(n, i):
                sp.wait_ge(t["pe"][n], count_at(t, i, "pe", "attr_turned"))
                gate(sp, t)
                sp.wait_ge(t["dve"][n], count_at(t, i, "dve", "combined3"))
                gate(sp, t)
                own = slice(J * n, J * n + J)
                sp.dma_start(e["attrs"][:, own, 0:basis], attrs[:, bass.ds(i * T + J * n, J), :]
                             ).then_inc(attrs_loaded[n], 16)
                sp.dma_start(e["y"][:, own, :], y_view[:, bass.ds(i * T + J * n, J), :]
                             ).then_inc(attrs_loaded[n], 16)
                sp.dma_start(e["dst_row"][:, n, :],
                             inp["dst"][bass.ds(i * ROWS + W * n, W)].unsqueeze(0).broadcast_to([P, W])
                             ).then_inc(attrs_loaded[n], 16)

            run_rounds(sp, rounds, order, part, dict(load=load))

        @block.gpsimd
        def _(p):
            prime(p, t, "pool")

            def gather(n, i, copies):
                own = slice(J * n, J * n + J)
                p.tensor_copy(e["ends_now"][:, :, own], index["ends"][:, :, bass.ds(i * T + J * n, J)]
                              ).then_inc(index_copied[n], 1)
                p.wait_ge(index_copied[n], copies)
                gate(p, t)
                for j in range(J):
                    for side in range(2):
                        k = J * n + j
                        p.indirect_dma_start(e["rows"][:, n, side, j, :], None, source,
                                             bass.IndirectOffsetOnAxis(ap=e["ends_now"][:, side, k:k + 1], axis=0)
                                             ).then_inc(gathered[n], 16)

            def copy_keys(n, i):
                p.wait_ge(t["dve"][n], count_at(t, i, "dve", "masked"))
                gate(p, t)
                own = slice(J * n, J * n + J)
                p.tensor_copy(e["key_now"][:, :, own], index["keys"][:, :, bass.ds(i * T + J * n, J)]
                              ).then_inc(t["pool"][n], 1)

            def roots(n, i):
                p.wait_ge(gathered[n], 64 * i + 64)
                gate(p, t)
                p.wait_ge(t["dve"][n], count_at(t, i, "dve", "normed"))
                gate(p, t)
                p.tensor_tensor(e["root"][:, n, :, :].unsqueeze(3), e["rows"][:, n, :, :, Q:Q + 1],
                                w["half"][:, 0:2 * J].rearrange("p (s j) -> p s j", j=J).unsqueeze(3), ALU.pow
                                ).then_inc(t["pool"][n], 1)

            def gather_next(n, i):
                p.wait_ge(t["dve"][n], count_at(t, i + 1, "dve", "normed"))
                gate(p, t)
                p.wait_ge(t["act"][n], count_at(t, i + 1, "act", "attr_kept"))
                gate(p, t)
                gather(n, i + 1, 2 * i + 2)

            def scatter(n, i):
                p.wait_ge(scattered[n], 16 * J * i + 16)
                gate(p, t)
                own = slice(J * n, J * n + J)
                p.tensor_copy(e["into_now"][:, own], index["into_i"][:, bass.ds(i * T + J * n, J)]
                              ).then_inc(index_copied[n], 1)
                p.wait_ge(index_copied[n], 2 * i + 3)
                gate(p, t)
                p.wait_ge(t["dve"][n], count_at(t, i + 1, "dve", "widened"))
                gate(p, t)
                for j in range(J):
                    k = J * n + j
                    p.indirect_dma_start(target, bass.IndirectOffsetOnAxis(ap=e["into_now"][:, k:k + 1], axis=0),
                                         e["new"][:, n, j, :], None, bounds_check=nodes - 1, oob_is_err=False
                                         ).then_inc(scattered[n], 16)

            for n in range(LANES):
                p.dma_start(e["first"][:, n:n + 1], inp["node_vec1"][0:P, :]).then_inc(scattered[n], 16)
                gather(n, 0, 1)
            run_rounds(p, rounds, order, part, dict(copy_keys=copy_keys, roots=roots, gather_next=gather_next,
                                                    scatter=scatter))
            for n in range(LANES):
                p.wait_ge(gathered[n], 64 * (rounds + 1))
                p.wait_ge(scattered[n], 16 * J * rounds + 16)

        @block.vector
        def _(v):
            v.memset(e["msg"][:, :, :, M - 1:M], 1.0)
            v.memset(e["new"][:, :, :, MEAN:ROW], 0.0)
            v.memset(e["sums"][:, :, :, :], 0.0).then_inc(ready, 1)
            v.wait_ge(ready, 1)
            prime(v, t, "dve")

            def one(ins, n):
                ins.then_inc(t["dve"][n], 1)

            def after(i, n, step):
                v.wait_ge(t["dve"][n], count_at(t, i + 1, "dve", step))

            def root_attr(n, i):
                v.wait_ge(t["pool"][n], count_at(t, i + 1, "pool", "roots"))
                one(v.tensor_tensor(e["root_a"][:, n, :].unsqueeze(2), e["root"][:, n, 0, :].unsqueeze(2),
                                    e["rows"][:, n, 0, :, A:A + 1], ALU.mult), n)

            def normalize(n, i):
                after(i, n, "root_attr")
                for j in range(J):
                    v.tensor_scalar(e["xs"][:, n, j, :], e["rows"][:, n, 0, j, 0:F], e["rows"][:, n, 0, j, MEAN:Q],
                                    e["root_a"][:, n, j:j + 1], ALU.subtract, ALU.mult)
                    ins = v.tensor_scalar(e["xd"][:, n, j, :], e["rows"][:, n, 1, j, 0:F], e["rows"][:, n, 1, j, MEAN:Q],
                                          e["root"][:, n, 1, j:j + 1], ALU.subtract, ALU.mult)
                one(ins, n)

            def mask(n, i):
                v.wait_ge(t["pool"][n], count_at(t, i + 1, "pool", "keys"))
                v.wait_ge(attrs_loaded[n], 48 * i + 48)
                masks(v, t, e, i + 1, n)

            def products(n, i):
                a, b = banks[2 * n], banks[2 * n + 1]
                v.wait_ge(t["pe"][n], count_at(t, i + 1, "pe", "weights"))
                v.tensor_tensor(e["p01"][:, n, :], a[:, 0:W], e["f01"][:, n, :], ALU.mult)
                v.tensor_tensor(e["p2"][:, n, :], b[0:V, 0:W], e["fv"][:, n, :], ALU.mult)
                one(v.tensor_tensor(e["p3"][:, n, :], b[0:V, W:2 * W], e["fv"][:, n, :], ALU.mult), n)

            def combine(k):
                def step(n, i):
                    if k:
                        after(i, n, f"combined{k - 1}")
                    else:
                        v.wait_ge(t["pe"][n], count_at(t, i + 1, "pe", "messages"))
                    for j in range(J):
                        bank, y = banks[2 * n + j], e["y"][:, J * n + j, k:k + 1]
                        scalars, vectors = e["msg"][:, n, j, 0:1 + S], e["msg"][:, n, j, 1 + S:1 + F]
                        if k == 0:
                            v.tensor_scalar(scalars, bank[0:P, 0:1 + S], y, None, ALU.mult)
                            ins = v.tensor_scalar(vectors, bank[0:P, 97:193], y, None, ALU.mult)
                        else:
                            o = 193 + (k - 1) * (1 + S)
                            v.scalar_tensor_tensor(scalars, bank[0:P, o:o + 1 + S], y, scalars, ALU.mult, ALU.add)
                            mv = vectors.rearrange("p (w c) -> p c w", c=3)[:, k - 1, :]
                            ins = v.scalar_tensor_tensor(mv, bank[0:P, 1 + S:97], y, mv, ALU.mult, ALU.add)
                    one(ins, n)
                return step

            def small(n):
                return (e["new"][:, n, :, A:A + 1], e["part"][:, n, :].unsqueeze(2),
                        e["factor"][:, n, :].unsqueeze(2), e["sums"][:, n, :, 0:1], e["sums"][:, n, :, M - 1:M])

            def limit_count(n, i):
                attr, part_, factor, alpha, count = small(n)
                v.wait_ge(t["act"][n], count_at(t, i + 1, "act", "sums_copied"))
                one(v.tensor_scalar(part_, count, 1.0, None, ALU.max), n)

            def invert(n, i):
                attr, part_, factor, alpha, count = small(n)
                after(i, n, "count")
                one(v.reciprocal(part_, part_), n)

            def part_attr(n, i):
                attr, part_, factor, alpha, count = small(n)
                after(i, n, "inverse")
                one(v.tensor_tensor(part_, part_, attr, ALU.mult), n)

            def half_factor(n, i):
                attr, part_, factor, alpha, count = small(n)
                if l == 1:
                    after(i, n, "part")
                    one(v.tensor_tensor(factor, alpha, part_, ALU.mult), n)
                else:
                    v.wait_ge(t["act"][n], count_at(t, i + 1, "act", "sums_copied"))
                    one(v.tensor_tensor(part_, alpha, attr, ALU.mult), n)

            def whole_factor(n, i):
                attr, part_, factor, alpha, count = small(n)
                if l == 2:
                    v.wait_ge(t["act"][n], count_at(t, i + 1, "act", "sums_copied"))
                    one(v.tensor_copy(factor, attr), n)
                else:
                    after(i, n, "half_factor")
                    one(v.tensor_tensor(factor, factor if l else part_, part_ if l else attr, ALU.mult), n)

            def add_self(n, i):
                for j in range(J):
                    ins = v.scalar_tensor_tensor(e["new"][:, n, j, 0:F], banks[2 * n + j][0:P, 192:192 + F],
                                                 e["new"][:, n, j, A:A + 1], e["xd"][:, n, j, :], ALU.mult, ALU.add)
                one(ins, n)

            def add_messages(n, i):
                after(i, n, "self_added")
                for j in range(J):
                    ins = v.scalar_tensor_tensor(e["new"][:, n, j, 0:F], e["sums"][:, n, j, 1:1 + F],
                                                 e["factor"][:, n, j:j + 1], e["new"][:, n, j, 0:F], ALU.mult, ALU.add)
                one(ins, n)

            def measure(n, i):
                after(i, n, "added")
                for j in range(J):
                    ins = v.bn_stats(e["stats"][:, n, j, :], e["new"][:, n, j, 0:F])
                one(ins, n)

            def merge(n, i):
                after(i, n, "measured")
                gate(v, t)
                for j in range(J):
                    ins = v.bn_aggr(e["new"][:, n, j, MEAN:Q + 1], e["stats"][:, n, j, :])
                one(ins, n)

            def widen(n, i):
                after(i, n, "merged")
                one(v.tensor_scalar(e["new"][:, n, :, Q:Q + 1], e["new"][:, n, :, Q:Q + 1], EPS, None, ALU.add), n)

            by_layer = [dict(half_factor=half_factor),
                        dict(limit_count=limit_count, invert=invert, part_attr=part_attr, half_factor=half_factor),
                        {}][l]
            run_rounds(v, rounds, order, part, dict(
                root_attr=root_attr, normalize=normalize, mask=mask, products=products,
                **{f"combine{k}": combine(k) for k in range(4)}, **by_layer, whole_factor=whole_factor,
                add_self=add_self, add_messages=add_messages, measure=measure, merge=merge, widen=widen))

        @block.scalar
        def _(act):
            prime(act, t, "act")
            act.wait_ge(ready, 1)

            def wait(n, i, step):
                act.wait_ge(t["pe"][n], count_at(t, i + 1, "pe", step))

            def one(ins, n):
                ins.then_inc(t["act"][n], 1)

            def keep_attr(n, i):
                act.wait_ge(gathered[n], 64 * i + 64)
                act.wait_ge(scattered[n], 16 * J * i + 16)
                one(act.activation(e["new"][:, n, :, A:A + 1], e["rows"][:, n, 1, :, A:A + 1], ACT.Copy), n)

            def copy_attr(n, i):
                wait(n, i, "attr_turned")
                one(act.activation(e["attr_t"][0:basis, n, :], banks[2 * n + 1][0:basis, 0:W], ACT.Copy), n)

            def copy_turned(side, s_t, v_t):
                def step(n, i):
                    wait(n, i, side + "_turned")
                    act.activation(s_t[:, n, :], banks[2 * n][0:S, 0:W], ACT.Copy)
                    one(act.activation(v_t[:, n, :], banks[2 * n][0:V, W:2 * W], ACT.Copy), n)
                return step

            def activate1(n, i):
                wait(n, i, "hidden1")
                width = hid if l else S
                one(act.activation(e["h"][0:width, n, :], banks[2 * n + 1][0:width, W:2 * W], func, scale=scale), n)

            def activate2(n, i):
                wait(n, i, "hidden2")
                one(act.activation(e["h2"][0:S, n, :], banks[2 * n + 1][0:S, 0:W], func, scale=S ** -0.5), n)

            def copy_linear(n, i):
                wait(n, i, "linear")
                act.activation(e["f01"][:, n, :], banks[2 * n][:, 0:W], ACT.Copy)
                one(act.activation(e["fv"][:, n, :], banks[2 * n][0:V, W:2 * W], ACT.Copy), n)

            def copy_sums(n, i):
                wait(n, i, "summed")
                for j in range(J):
                    ins = act.activation(e["sums"][:, n, j, 0:M], banks[2 * n + j][0:P, 0:M], ACT.Copy)
                one(ins, n)

            run_rounds(act, rounds, order, part, dict(
                keep_attr=keep_attr, copy_attr=copy_attr, copy_src=copy_turned("src", e["s_t"], e["v_t"]),
                activate1=activate1, copy_dst=copy_turned("dst", e["ds_t"], e["dv_t"]),
                **(dict(activate2=activate2) if l == 0 else {}), copy_linear=copy_linear, copy_sums=copy_sums))

        @block.tensor
        def _(pe):
            prime(pe, t, "pe")
            ident = w["ident"][0:P, 0:P]
            last_h = e["h2"] if l == 0 else e["h"]
            hid1 = w["fc1"].shape[1]

            def wait(engine, n, i, step):
                pe.wait_ge(t[engine][n], count_at(t, i + 1, engine, step))
                gate(pe, t)

            def one(ins, n):
                ins.then_inc(t["pe"][n], 1)

            def turn_attr(n, i):
                pe.wait_ge(attrs_loaded[n], 48 * i + 48)
                gate(pe, t)
                wait("dve", n, i - 1, "self_added")
                wait("act", n, i - 1, "sums_copied")
                for j in range(J):
                    ins = pe.transpose(banks[2 * n + 1][0:basis, j * P:(j + 1) * P],
                                       e["attrs"][:, J * n + j, 0:basis], ident)
                one(ins, n)

            def turn_rows(side, x):
                def step(n, i):
                    if side == "src":
                        wait("dve", n, i, "normed")
                    else:
                        wait("act", n, i, "src_copied")
                    bank = banks[2 * n]
                    for j in range(J):
                        pe.transpose(bank[0:S, j * P:(j + 1) * P], x[:, n, j, 0:S], ident)
                        ins = pe.transpose(bank[0:V, W + j * P:W + (j + 1) * P], x[:, n, j, S:F], ident)
                    one(ins, n)
                return step

            def hidden1(n, i):
                wait("act", n, i, "attr_copied")
                one(pe.matmul(banks[2 * n + 1][0:hid1, W:2 * W], w["fc1"][:, :], e["attr_t"][0:basis, n, :],
                              start=True, stop=True), n)

            def hidden2(n, i):
                wait("act", n, i, "activated1")
                one(pe.matmul(banks[2 * n + 1][0:S, 0:W], w["fc2"][:, :], e["h"][0:S, n, :], start=True, stop=True), n)

            def linear(n, i):
                wait("act", n, i, "activated2" if l == 0 else "dst_copied")
                pe.matmul(banks[2 * n][:, 0:W], w[f"lin_s{l}"][:, :], e["s_t"][:, n, :], start=True, stop=True)
                one(pe.matmul(banks[2 * n][0:V, W:2 * W], w[f"lin_v{l}"][:, :], e["v_t"][:, n, :],
                              start=True, stop=True), n)

            def weights(n, i):
                wait("act", n, i, "linear_copied")
                h = last_h[0:hid, n, :]
                pe.matmul(banks[2 * n][:, 0:W], w["fc_last"][:, 0:128], h, start=True, stop=True)
                pe.matmul(banks[2 * n + 1][0:V, 0:W], w["fc_last"][:, 128:128 + V], h, start=True, stop=True)
                one(pe.matmul(banks[2 * n + 1][0:V, W:2 * W], w["fc_last"][:, 128 + V:128 + 2 * V], h,
                              start=True, stop=True), n)

            def messages(n, i):
                wait("dve", n, i, "products")
                for j in range(J):
                    c, bank = slice(j * P, (j + 1) * P), banks[2 * n + j]
                    pe.matmul(bank[0:P, 0:97], e["p01"][:, n, c], w["msg_a"][:, :], start=True, stop=True)
                    pe.matmul(bank[0:P, 97:193], e["p2"][:, n, c], w["msg_c"][:, :], start=True, stop=True)
                    ins = pe.matmul(bank[0:P, 193:388], e["p3"][:, n, c], w["msg_d"][:, :], start=True, stop=True)
                one(ins, n)

            def add_up(n, i):
                wait("dve", n, i, "combined3")
                wait("act", (n - 1) % LANES, i if n else i - 1, "sums_copied")
                run_sums(pe, e, banks, n, M)
                for j in range(J):
                    c, bank = slice(j * P, (j + 1) * P), banks[2 * n + j]
                    pe.matmul(bank[0:P, 192:192 + S], e["ds_t"][:, n, c], w[f"self_s{l}"][:, :],
                              start=True, stop=True)
                    ins = pe.matmul(bank[0:P, 192 + S:192 + F], e["dv_t"][:, n, c], w[f"self_v{l}"][0:V, S:F],
                                    start=True, stop=True)
                one(ins, n)

            run_rounds(pe, rounds, order, part, dict(
                **keep_busy(pe, banks, w, fill), turn_attr=turn_attr, turn_src=turn_rows("src", e["xs"]),
                turn_dst=turn_rows("dst", e["xd"]), hidden1=hidden1, **(dict(hidden2=hidden2) if l == 0 else {}),
                linear=linear, weights=weights, messages=messages, add_up=add_up))


VALS, X3, ATTR, KEPT = 0, F, 2 * F, 2 * F + 4
HEADS = 8


def attention_weights(nc, sem, keep, sb, banks, inp, w):
    loaded = sem("att_weights_loaded")
    built = sem("att_weights_built")
    summed = sem("att_weights_summed")
    g = {k: inp["L3_gnn_" + k] for k in (
        "ln1_w0 ln1_b0 ln1_w1 msrc_ws msrc_wv mdst_ws mdst_bs mdst_wv rw1 rb1 rg1 rbe1 rw2 rb2 rg2 rbe2 rw3 roff "
        "lin_ws lin_bs lin_wv alpha_dot proj_ws proj_wv").split()}
    for name, shape in (("src_s", [S, 128]), ("dst_s", [S, 128]), ("src_v", [V, V]), ("dst_v", [V, V]),
                        ("ms_bias", [128, 1]), ("rw1", [64, 64]), ("rw2", [64, 64]), ("rw3", [64, 128 + 3 * V]),
                        ("rb1", [P, 64]), ("rb2", [P, 64]), ("rg", [64, 4]), ("rbe", [64, 4]),
                        ("roff12", [128, 1]), ("roff", [V, 3]), ("lin_a", [128, 160]), ("lin_4", [V, 128]),
                        ("lin_3", [V, V]), ("lin_5", [V, V]), ("lin_b", [P, 128]), ("alpha_dot", [P, 64]),
                        ("proj_s", [S, S]), ("proj_v", [V, V]), ("spread", [3, V])):
        w[name] = keep("att_" + name, shape)
    loads = []

    def thrice(src):
        return src.unsqueeze(1).broadcast_to([U, 3, src.shape[1]])

    def raw(name, shape, *parts):
        t = sb("att_raw_" + name, shape)
        for at, src in parts:
            loads.append((t[at, :], src))
        return t

    every = slice(None)
    src_s = raw("src_s", [S, 64], (every, g["msrc_ws"]))
    dst_s = raw("dst_s", [S, 64], (every, g["mdst_ws"]))
    src_v = raw("src_v", [V, U], (every, thrice(g["msrc_wv"])))
    dst_v = raw("dst_v", [V, U], (every, thrice(g["mdst_wv"])))
    w0 = raw("w0", [S, 1], (every, g["ln1_w0"].unsqueeze(1)))
    b0 = raw("b0", [S, 1], (every, g["ln1_b0"].unsqueeze(1)))
    w1 = raw("w1", [V, 1], (every, thrice(g["ln1_w1"].unsqueeze(1))))
    bias = raw("bias", [128, 1], (slice(0, 64), g["mdst_bs"].unsqueeze(1)), (slice(64, 128), g["mdst_bs"].unsqueeze(1)))
    rw2 = raw("rw2", [64, 64], (every, g["rw2"]))
    rw3 = raw("rw3", [64, 224], (every, g["rw3"]))
    both = sb("att_raw_both", [S, 2, 128])
    lin_v0 = raw("lin_v0", [128, U], (slice(64, 128), g["lin_wv"][0:S, :]))
    lin_3 = raw("lin_3", [V, U], (every, thrice(g["lin_wv"][S:S + U, :])))
    lin_5 = raw("lin_5", [V, U], (every, thrice(g["lin_wv"][S + U:S + 2 * U, :])))
    proj_v = raw("proj_v", [V, U], (every, thrice(g["proj_wv"])))
    lin_s = raw("lin_s", [S, 128], (every, g["lin_ws"][0:S, :]))
    for name, src in (("rw1", g["rw1"]), ("proj_s", g["proj_ws"]), ("lin_4", thrice(g["lin_ws"][S:S + U, :])),
                      ("rb1", g["rb1"].unsqueeze(0).broadcast_to([P, 64])),
                      ("rb2", g["rb2"].unsqueeze(0).broadcast_to([P, 64])),
                      ("lin_b", g["lin_bs"].unsqueeze(0).broadcast_to([P, 128])),
                      ("alpha_dot", g["alpha_dot"].rearrange("h k -> (h k)").unsqueeze(0).broadcast_to([P, 64])),
                      ("roff12", g["roff"][0:128].unsqueeze(1))):
        loads.append((w[name][:, :], src))
    for k in range(3):
        loads.append((w["roff"][:, k:k + 1], thrice(g["roff"][128 + k * U:128 + (k + 1) * U].unsqueeze(1))))
    for k in range(2):
        loads.append((w["rg"][:, k:k + 1], g[f"rg{k + 1}"].unsqueeze(1)))
        loads.append((w["rbe"][:, k:k + 1], g[f"rbe{k + 1}"].unsqueeze(1)))

    def kron(v, dst, src, factor):
        for c in range(3):
            v.tensor_scalar(dst[:, :].rearrange("p (w c) -> p c w", c=3)[:, c, :], src[:, :],
                            w["mod3"][:, c:c + 1], factor, ALU.mult, ALU.mult)

    with nc.Block() as block:
        @block.sync
        def _(sp):
            for dst, src in loads:
                sp.dma_start(dst, src).then_inc(loaded, 16)

        @block.vector
        def _(v):
            v.memset(w["lin_a"][:, :], 0.0).then_inc(built, 1)
            v.wait_ge(built, 1)
            v.wait_ge(loaded, 16 * len(loads))
            for k in range(2):
                h = slice(k * 64, (k + 1) * 64)
                v.tensor_scalar(w["src_s"][:, h], src_s[:, :], w0[:, 0:1], None, ALU.mult)
                v.tensor_scalar(w["dst_s"][:, h], dst_s[:, :], w0[:, 0:1], None, ALU.mult)
                v.tensor_copy(both[:, 0, h], src_s[:, :])
                v.tensor_copy(both[:, 1, h], dst_s[:, :])
            kron(v, w["src_v"], src_v, w1[:, 0:1])
            kron(v, w["dst_v"], dst_v, w1[:, 0:1])
            kron(v, w["lin_3"], lin_3, 1.0)
            kron(v, w["lin_5"], lin_5, 1.5 ** 0.5)
            kron(v, w["proj_v"], proj_v, 1.0)
            v.tensor_copy(w["lin_a"][0:S, 0:128], lin_s[:, :])
            v.tensor_scalar(w["lin_a"][S:128, 128:160], lin_v0[S:128, :], 3 ** 0.5, None, ALU.mult)
            v.tensor_scalar(w["rw2"][:, :], rw2[:, :], 0.5, None, ALU.mult)
            v.tensor_scalar(w["rw3"][:, 0:128], rw3[:, 0:128], 0.5, None, ALU.mult)
            for k in range(3):
                v.tensor_scalar(w["rw3"][:, 128 + k * V:128 + (k + 1) * V].rearrange("p (u c) -> p u c", c=3),
                                rw3[:, 128 + k * U:128 + (k + 1) * U].unsqueeze(2).broadcast_to([64, U, 3]),
                                0.5, None, ALU.mult)
            v.tensor_scalar(w["rg"][:, 2:4], w["rg"][:, 0:2], 0.5, None, ALU.mult)
            v.tensor_scalar(w["rbe"][:, 2:4], w["rbe"][:, 0:2], 0.5, None, ALU.mult).then_inc(built, 1)
            v.wait_ge(summed, 1)
            v.tensor_tensor(w["ms_bias"][:, :], banks[0][:, 0:1], bias[:, :], ALU.add)
            v.tensor_copy(w["spread"][:, :], banks[1][0:3, 0:V])

        @block.tensor
        def _(pe):
            pe.wait_ge(built, 2)
            pe.matmul(banks[0][:, 0:1], both[:, 0, :], b0[:, :], start=True, stop=False)
            pe.matmul(banks[0][:, 0:1], both[:, 1, :], b0[:, :], start=False, stop=True)
            pe.transpose(banks[1][0:3, 0:V], w["mod3"][:, :], w["ident"][0:V, 0:V]).then_inc(summed, 1)


def attention_edges(nc, sem, sb, banks, inp, w, e, index, table, kept, logits, edges):
    T = LANES * J
    rounds = edges // ROWS
    attrs = inp["edge_attr_64"].rearrange("(t p) f -> p t f", p=P)
    vec_view = inp["edge_attr_3"].rearrange("(t p) f -> p t f", p=P)
    kept_view = kept.rearrange("(t p) f -> p t f", p=P)
    logit_view = logits.rearrange("(t p) h -> p t h", p=P)
    radial = [["h_added" + k, "h_measured" + k, "h_merged" + k, "h_widened" + k, "h_normed" + k, "h_gated" + k]
              for k in ("1", "2")]
    t = lane_steps(sem, "att",
              pe=["attr_turned", "hidden1", "src_turned", "h_turned1", "dst_turned", "hidden2", "h_turned2",
                  "vec_turned", "vec_spread", "linear", "weights", "outputs"],
              act=["attr_copied", "src_copied", "h_activated1", "dst_copied", "attr_kept", "h_activated2",
                   "vec_copied", "spread_copied", "linear_copied", "values_copied", "tanh"],
              dve=["measured", "merged", "differences", "squares", "summed", "widened", *radial[0][:4], "x3",
                   "normed", *radial[0][4:], *radial[1], "products", "product4", "biased",
                   *[f"cross{k}" for k in range(3)], "leak", "leaked", "dotted", "logits"],
              pool=["roots", "h_roots1", "h_roots2"])
    part = 17.05
    order = [("load", 0.0), ("turn_attr", 2.7), ("measure", 2.7), ("copy_attr", 3.3), ("merge", 4.25),
             ("differences", 4.95), ("hidden1", 5.2), ("squares", 5.4), ("add_squares", 5.65), ("widen", 5.85),
             ("roots", 6.15), ("h_add1", 7.15), ("h_measure1", 7.5), ("h_merge1", 8.0), ("h_widen1", 8.25),
             ("h_roots1", 8.55), ("divide", 8.6), ("normalize", 10.1), ("h_normalize1", 12.0),
             ("turn_src", 12.25), ("turn_h1", 12.7), ("keep_busy0", 12.96), ("copy_src", 13.05),
             ("turn_dst", 13.9), ("activate1", 15.05), ("copy_dst", 15.65), ("h_gate1", 15.95),
             ("keep_attr", 16.2), ("hidden2", 16.55), ("gather_next", 16.6), ("h_add2", 18.25),
             ("h_measure2", 18.6), ("h_merge2", 19.1), ("h_widen2", 19.35), ("h_roots2", 21.3),
             ("h_normalize2", 22.6), ("keep_busy1", 22.71), ("turn_h2", 23.3), ("keep_busy2", 23.56),
             ("activate2", 23.9), ("turn_vec", 24.8), ("keep_busy3", 25.06), ("h_gate2", 25.2),
             ("copy_vec", 25.4), ("spread_vec", 26.0), ("keep_busy4", 26.46), ("copy_spread", 26.8),
             ("linear", 27.4), ("copy_linear", 29.45), ("weights", 31.4), ("products", 33.45),
             ("product4", 34.9), ("outputs", 37.05), ("bias", 40.1), ("copy_values", 41.55),
             ("take_tanh", 41.95), ("cross0", 46.55), ("cross1", 47.75), ("cross2", 48.95), ("leak", 53.0),
             ("leaked", 53.35), ("dot", 53.65), ("add_heads", 55.2), ("store", 55.65)]
    fill = [(3, 1, 3), (1, 0, 2), (0, 0, 5), (0, 0, 3), (0, 0, 3)]
    gathered = [sem(f"att_rows_gathered_lane{n}") for n in range(LANES)]
    attrs_loaded = [sem(f"att_attrs_loaded_lane{n}") for n in range(LANES)]
    kept_stored = [sem(f"att_kept_stored_lane{n}") for n in range(LANES)]
    cleared = sem("att_columns_cleared")
    index_copied = [sem(f"att_index_copied_lane{n}") for n in range(LANES)]
    stats = sb("att_stats", [P, LANES, 2, 2 * J, 6])
    mom = sb("att_moments", [P, LANES, 2, 2 * J, 2])
    diff = sb("att_diff", [P, LANES, 2 * J])
    vec_sq = sb("att_vec_sq", [P, LANES, J, 3])
    wide = sb("att_wide", [P, LANES, 12])
    root = sb("att_root", [P, LANES, 12])
    r = sb("att_r", [P, LANES, 2, J, 3])
    r_t = sb("att_r_t", [3, LANES, W])
    spread = sb("att_spread_r", [V, LANES, W])
    hx = sb("att_hx", [P, LANES, J, 64])
    hn = sb("att_hn", [P, LANES, J, 64])
    h_stats = sb("att_h_stats", [P, LANES, J, 6])
    h_mom = sb("att_h_moments", [P, LANES, J, 2])
    h_wide = sb("att_h_wide", [P, LANES, J])
    h_root = sb("att_h_root", [P, LANES, J])
    h_u = sb("att_h_u", [64, LANES, W])
    h_tanh = sb("att_h_tanh", [64, LANES, W])
    p5 = sb("att_p5", [V, LANES, W])
    keep = sb("att_keep", [P, T, KEPT])
    alpha = sb("att_alpha", [P, LANES, J, 64])
    tanh = sb("att_tanh", [P, LANES, J, 64])
    logit = sb("att_logit", [P, T, HEADS])

    with nc.Block() as block:
        @block.sync
        def _(sp):
            for n in range(LANES):
                sp.sem_inc(kept_stored[n], 32)

            def load(n, i):
                sp.wait_ge(t["pe"][n], count_at(t, i, "pe", "attr_turned"))
                gate(sp, t)
                sp.wait_ge(t["dve"][n], count_at(t, i, "dve", "x3"))
                gate(sp, t)
                own = slice(J * n, J * n + J)
                sp.dma_start(e["attrs"][:, own, :], attrs[:, bass.ds(i * T + J * n, J), :]
                             ).then_inc(attrs_loaded[n], 16)
                sp.dma_start(e["y"][:, own, 0:3], vec_view[:, bass.ds(i * T + J * n, J), :]
                             ).then_inc(attrs_loaded[n], 16)

            def store(n, i):
                sp.wait_ge(t["dve"][n], count_at(t, i + 1, "dve", "logits"))
                gate(sp, t)
                sp.wait_ge(t["act"][n], count_at(t, i + 1, "act", "attr_kept"))
                gate(sp, t)
                own = slice(J * n, J * n + J)
                sp.dma_start(kept_view[:, bass.ds(i * T + J * n, J), :], keep[:, own, :]
                             ).then_inc(kept_stored[n], 16)
                sp.dma_start(logit_view[:, bass.ds(i * T + J * n, J), :], logit[:, own, :]
                             ).then_inc(kept_stored[n], 16)

            run_rounds(sp, rounds, order, part, dict(load=load, store=store))
            for n in range(LANES):
                sp.wait_ge(kept_stored[n], 32 * rounds + 32)

        @block.gpsimd
        def _(p):
            prime(p, t, "pool")

            def gather(n, i):
                own = slice(J * n, J * n + J)
                p.tensor_copy(e["ends_now"][:, :, own], index["ends"][:, :, bass.ds(i * T + J * n, J)]
                              ).then_inc(index_copied[n], 1)
                p.wait_ge(index_copied[n], i + 1)
                gate(p, t)
                for j in range(J):
                    for side in range(2):
                        k = J * n + j
                        p.indirect_dma_start(e["rows"][:, n, side, j, :], None, table,
                                             bass.IndirectOffsetOnAxis(ap=e["ends_now"][:, side, k:k + 1], axis=0)
                                             ).then_inc(gathered[n], 16)

            def gather_next(n, i):
                p.wait_ge(gathered[n], 64 * i + 64)
                gate(p, t)
                p.wait_ge(t["dve"][n], count_at(t, i + 1, "dve", "normed"))
                gate(p, t)
                p.wait_ge(t["act"][n], count_at(t, i + 1, "act", "attr_kept"))
                gate(p, t)
                gather(n, i + 1)

            def roots(n, i):
                p.wait_ge(t["dve"][n], count_at(t, i + 1, "dve", "widened"))
                gate(p, t)
                p.tensor_tensor(root[:, n, :], wide[:, n, :], w["half"][:, 0:12], ALU.pow
                                ).then_inc(t["pool"][n], 1)

            def h_roots(k):
                def step(n, i):
                    p.wait_ge(t["dve"][n], count_at(t, i + 1, "dve", "h_widened" + k))
                    gate(p, t)
                    p.tensor_tensor(h_root[:, n, :], h_wide[:, n, :], w["half"][:, 0:J], ALU.pow
                                    ).then_inc(t["pool"][n], 1)
                return step

            for n in range(LANES):
                gather(n, 0)
            run_rounds(p, rounds, order, part, dict(gather_next=gather_next, roots=roots, h_roots1=h_roots("1"),
                                                    h_roots2=h_roots("2")))
            for n in range(LANES):
                p.wait_ge(gathered[n], 64 * (rounds + 1))

        @block.vector
        def _(v):
            v.memset(keep[:, :, ATTR:KEPT], 0.0).then_inc(cleared, 1)
            prime(v, t, "dve")

            def one(ins, n):
                ins.then_inc(t["dve"][n], 1)

            def after(i, n, step):
                v.wait_ge(t["dve"][n], count_at(t, i + 1, "dve", step))

            def rows_of(n):
                return e["rows"][:, n, :, :, :].rearrange("p s j f -> p (s j) f")

            def measure(n, i):
                v.wait_ge(attrs_loaded[n], 32 * i + 32)
                v.wait_ge(gathered[n], 64 * i + 64)
                rows = rows_of(n)
                for k in range(2 * J):
                    v.bn_stats(stats[:, n, 0, k, :], rows[:, k, 0:S])
                    v.bn_stats(stats[:, n, 1, k, :], rows[:, k, S:F])
                one(v.tensor_tensor(vec_sq[:, n, :, :], e["y"][:, J * n:J * n + J, 0:3], e["y"][:, J * n:J * n + J, 0:3],
                                    ALU.mult), n)

            def merge(n, i):
                after(i, n, "measured")
                gate(v, t)
                for k in range(2 * J):
                    v.bn_aggr(mom[:, n, 0, k, :], stats[:, n, 0, k, :])
                    ins = v.bn_aggr(mom[:, n, 1, k, :], stats[:, n, 1, k, :])
                one(ins, n)

            def differences(n, i):
                after(i, n, "merged")
                q, mean = rows_of(n)[:, :, Q:Q + 1], rows_of(n)[:, :, MEAN:Q]
                v.scalar_tensor_tensor(wide[:, n, 0:4].unsqueeze(2), q, EPS, mom[:, n, 0, :, 1:2], ALU.mult, ALU.add)
                v.tensor_copy(wide[:, n, 8:10].unsqueeze(2), e["rows"][:, n, 1, :, Q:Q + 1])
                v.tensor_reduce(wide[:, n, 10:12], vec_sq[:, n, :, :], AX.X, ALU.add)
                one(v.tensor_tensor(diff[:, n, :].unsqueeze(2), mom[:, n, 1, :, 0:1], mean, ALU.subtract), n)

            def squares(n, i):
                after(i, n, "differences")
                d = diff[:, n, :]
                v.tensor_scalar(wide[:, n, 10:12], wide[:, n, 10:12], 1e-12, None, ALU.add)
                one(v.tensor_tensor(d, d, d, ALU.mult), n)

            def add_squares(n, i):
                after(i, n, "squares")
                d = diff[:, n, :].unsqueeze(2)
                one(v.tensor_tensor(d, d, mom[:, n, 1, :, 1:2], ALU.add), n)

            def widen(n, i):
                after(i, n, "summed")
                one(v.scalar_tensor_tensor(wide[:, n, 4:8].unsqueeze(2), rows_of(n)[:, :, Q:Q + 1], EPS,
                                           diff[:, n, :].unsqueeze(2), ALU.mult, ALU.add), n)

            def divide(n, i):
                v.wait_ge(t["pool"][n], count_at(t, i + 1, "pool", "roots"))
                v.wait_ge(kept_stored[n], 32 * i + 32)
                for j in range(J):
                    v.tensor_scalar(keep[:, J * n + j, X3:X3 + F], e["rows"][:, n, 1, j, 0:F],
                                    e["rows"][:, n, 1, j, MEAN:Q], root[:, n, 8 + j:9 + j], ALU.subtract, ALU.mult)
                    v.tensor_scalar(r[:, n, 0, j, :], e["y"][:, J * n + j, 0:3], root[:, n, 10 + j:11 + j], None,
                                    ALU.mult)
                    ins = v.tensor_scalar(r[:, n, 1, j, :], e["y"][:, J * n + j, 0:3], root[:, n, 10 + j:11 + j],
                                          -1.0, ALU.mult, ALU.mult)
                one(ins, n)

            def normalize(n, i):
                for j in range(J):
                    for side, x in enumerate((e["xs"], e["xd"])):
                        k = side * J + j
                        v.tensor_scalar(x[:, n, j, 0:S], e["rows"][:, n, side, j, 0:S], mom[:, n, 0, k, 0:1],
                                        root[:, n, k:k + 1], ALU.subtract, ALU.mult)
                        ins = v.tensor_scalar(x[:, n, j, S:F], e["rows"][:, n, side, j, S:F],
                                              e["rows"][:, n, side, j, MEAN:Q], root[:, n, 4 + k:5 + k],
                                              ALU.subtract, ALU.mult)
                one(ins, n)

            def radial_steps(k):
                def h_add(n, i):
                    v.wait_ge(t["pe"][n], count_at(t, i + 1, "pe", "hidden" + k))
                    one(v.tensor_tensor(hx[:, n, :, :],
                                        banks[2 * n + 1][0:P, 256:384].rearrange("p (j f) -> p j f", j=J),
                                        w["rb" + k][:, :].unsqueeze(1).broadcast_to([P, J, 64]), ALU.add), n)

                def h_measure(n, i):
                    after(i, n, "h_added" + k)
                    for j in range(J):
                        ins = v.bn_stats(h_stats[:, n, j, :], hx[:, n, j, :])
                    one(ins, n)

                def h_merge(n, i):
                    after(i, n, "h_measured" + k)
                    gate(v, t)
                    for j in range(J):
                        ins = v.bn_aggr(h_mom[:, n, j, :], h_stats[:, n, j, :])
                    one(ins, n)

                def h_widen(n, i):
                    after(i, n, "h_merged" + k)
                    one(v.tensor_scalar(h_wide[:, n, :].unsqueeze(2), h_mom[:, n, :, 1:2], EPS, None, ALU.add), n)

                def h_normalize(n, i):
                    v.wait_ge(t["pool"][n], count_at(t, i + 1, "pool", "h_roots" + k))
                    for j in range(J):
                        ins = v.tensor_scalar(hn[:, n, j, :], hx[:, n, j, :], h_mom[:, n, j, 0:1],
                                              h_root[:, n, j:j + 1], ALU.subtract, ALU.mult)
                    one(ins, n)

                def h_gate(n, i):
                    v.wait_ge(t["act"][n], count_at(t, i + 1, "act", "h_activated" + k))
                    one(v.scalar_tensor_tensor(e[{"1": "h", "2": "h2"}[k]][0:64, n, :], h_tanh[:, n, :], 1.0,
                                               h_u[:, n, :], ALU.add, ALU.mult), n)

                return {"h_add" + k: h_add, "h_measure" + k: h_measure, "h_merge" + k: h_merge,
                        "h_widen" + k: h_widen, "h_normalize" + k: h_normalize, "h_gate" + k: h_gate}

            def products(n, i):
                a, b = banks[2 * n], banks[2 * n + 1]
                v.wait_ge(t["pe"][n], count_at(t, i + 1, "pe", "weights"))
                v.scalar_tensor_tensor(e["p01"][:, n, :], a[:, 0:W], w["roff12"][:, 0:1], e["f01"][:, n, :],
                                       ALU.add, ALU.mult)
                v.scalar_tensor_tensor(e["p2"][:, n, :], a[0:V, W:2 * W], w["roff"][:, 0:1], e["fv"][:, n, :],
                                       ALU.add, ALU.mult)
                v.scalar_tensor_tensor(e["p3"][:, n, :], b[0:V, 0:W], w["roff"][:, 1:2], e["fv"][:, n, :],
                                       ALU.add, ALU.mult)
                one(v.scalar_tensor_tensor(p5[:, n, :], b[0:V, W:2 * W], w["roff"][:, 2:3], e["fv"][:, n, :],
                                           ALU.add, ALU.mult), n)

            def product4(n, i):
                after(i, n, "products")
                one(v.tensor_tensor(e["p3"][:, n, :], e["p3"][:, n, :], spread[:, n, :], ALU.mult), n)

            def bias(n, i):
                v.wait_ge(t["pe"][n], count_at(t, i + 1, "pe", "outputs"))
                for j in range(J):
                    k, bank = J * n + j, banks[2 * n + j]
                    v.tensor_tensor(alpha[:, n, j, :], bank[0:P, 0:64], w["lin_b"][:, 0:64], ALU.add)
                    ins = v.tensor_tensor(keep[:, k, 0:S], bank[0:P, 64:128], w["lin_b"][:, 64:128], ALU.add)
                one(ins, n)

            def cross(k):
                def step(n, i):
                    if k:
                        after(i, n, f"cross{k - 1}")
                    else:
                        v.wait_ge(t["act"][n], count_at(t, i + 1, "act", "values_copied"))
                    for j in range(J):
                        bank = banks[2 * n + j]
                        out = keep[:, J * n + j, S:F].rearrange("p (w c) -> p c w", c=3)
                        x = bank[0:P, 256:352].rearrange("p (w c) -> p c w", c=3)
                        for d in range(3):
                            src, sign, comp = ((bank[0:P, 128:160], 0, d), (x[:, (d + 1) % 3, :], 0, (d + 2) % 3),
                                               (x[:, (d + 2) % 3, :], 1, (d + 1) % 3))[k]
                            ins = v.scalar_tensor_tensor(out[:, d, :], src, r[:, n, sign, j, comp:comp + 1],
                                                         out[:, d, :], ALU.mult, ALU.add)
                    one(ins, n)
                return step

            def leak(n, i):
                v.wait_ge(t["act"][n], count_at(t, i + 1, "act", "tanh"))
                one(v.tensor_scalar(tanh[:, n, :, :], tanh[:, n, :, :], 0.4, 0.6, ALU.mult, ALU.add), n)

            def leaked(n, i):
                after(i, n, "leak")
                one(v.tensor_tensor(alpha[:, n, :, :], alpha[:, n, :, :], tanh[:, n, :, :], ALU.mult), n)

            def dot(n, i):
                after(i, n, "leaked")
                one(v.tensor_tensor(alpha[:, n, :, :], alpha[:, n, :, :],
                                    w["alpha_dot"][:, :].unsqueeze(1).broadcast_to([P, J, 64]), ALU.mult), n)

            def add_heads(n, i):
                after(i, n, "dotted")
                one(v.tensor_reduce(logit[:, J * n:J * n + J, :],
                                    alpha[:, n, :, :].rearrange("p j (h k) -> p j h k", h=HEADS), AX.X, ALU.add), n)

            run_rounds(v, rounds, order, part, dict(
                measure=measure, merge=merge, differences=differences, squares=squares, add_squares=add_squares,
                widen=widen, divide=divide, normalize=normalize, **radial_steps("1"), **radial_steps("2"),
                products=products, product4=product4, bias=bias, cross0=cross(0), cross1=cross(1), cross2=cross(2),
                leak=leak, leaked=leaked, dot=dot, add_heads=add_heads))

        @block.scalar
        def _(act):
            prime(act, t, "act")
            act.wait_ge(cleared, 1)

            def wait(engine, n, i, step):
                act.wait_ge(t[engine][n], count_at(t, i + 1, engine, step))

            def one(ins, n):
                ins.then_inc(t["act"][n], 1)

            def copy_attr(n, i):
                wait("pe", n, i, "attr_turned")
                one(act.activation(e["attr_t"][:, n, :], banks[2 * n + 1][0:64, 0:W], ACT.Copy), n)

            def activate(k):
                def step(n, i):
                    wait("pe", n, i, f"h_turned{k + 1}")
                    x = banks[2 * n + 1][0:64, 0:W]
                    act.activation(h_u[:, n, :], x, ACT.Identity, bias=w["rbe"][:, k:k + 1],
                                   scale=w["rg"][:, k:k + 1])
                    one(act.activation(h_tanh[:, n, :], x, ACT.Tanh, bias=w["rbe"][:, 2 + k:3 + k],
                                       scale=w["rg"][:, 2 + k:3 + k]), n)
                return step

            def copy_turned(side, s_t, v_t):
                def step(n, i):
                    wait("pe", n, i, side + "_turned")
                    act.activation(s_t[:, n, :], banks[2 * n][0:S, 0:W], ACT.Copy)
                    one(act.activation(v_t[:, n, :], banks[2 * n][0:V, W:2 * W], ACT.Copy), n)
                return step

            def keep_attr(n, i):
                wait("dve", n, i, "x3")
                one(act.activation(keep[:, J * n:J * n + J, ATTR:ATTR + 1], e["rows"][:, n, 1, :, A:A + 1],
                                   ACT.Copy), n)

            def copy_vec(n, i):
                wait("pe", n, i, "vec_turned")
                one(act.activation(r_t[:, n, :], banks[2 * n + 1][0:3, 0:W], ACT.Copy), n)

            def copy_spread(n, i):
                wait("pe", n, i, "vec_spread")
                one(act.activation(spread[:, n, :], banks[2 * n + 1][0:V, W:2 * W], ACT.Copy), n)

            def copy_linear(n, i):
                wait("pe", n, i, "linear")
                act.activation(e["f01"][:, n, :], banks[2 * n][:, 0:W], ACT.Identity, bias=w["ms_bias"][:, 0:1])
                one(act.activation(e["fv"][:, n, :], banks[2 * n][0:V, W:2 * W], ACT.Copy), n)

            def copy_values(n, i):
                wait("dve", n, i, "biased")
                for j in range(J):
                    ins = act.activation(keep[:, J * n + j, S:F], banks[2 * n + j][0:P, 160:256], ACT.Copy)
                one(ins, n)

            def take_tanh(n, i):
                wait("dve", n, i, "biased")
                one(act.activation(tanh[:, n, :, :], alpha[:, n, :, :], ACT.Tanh, scale=0.5), n)

            run_rounds(act, rounds, order, part, dict(
                copy_attr=copy_attr, activate1=activate(0), activate2=activate(1),
                copy_src=copy_turned("src", e["s_t"], e["v_t"]), copy_dst=copy_turned("dst", e["ds_t"], e["dv_t"]),
                keep_attr=keep_attr, copy_vec=copy_vec, copy_spread=copy_spread, copy_linear=copy_linear,
                copy_values=copy_values, take_tanh=take_tanh))

        @block.tensor
        def _(pe):
            prime(pe, t, "pe")
            ident = w["ident"][0:P, 0:P]

            def wait(engine, n, i, step):
                pe.wait_ge(t[engine][n], count_at(t, i + 1, engine, step))
                gate(pe, t)

            def one(ins, n):
                ins.then_inc(t["pe"][n], 1)

            def turn_attr(n, i):
                pe.wait_ge(attrs_loaded[n], 32 * i + 32)
                gate(pe, t)
                pe.wait_ge(t["dve"][n], count_at(t, i, "dve", "cross2"))
                gate(pe, t)
                for j in range(J):
                    ins = pe.transpose(banks[2 * n + 1][0:64, j * P:(j + 1) * P], e["attrs"][:, J * n + j, :], ident)
                one(ins, n)

            def hidden(k):
                def step(n, i):
                    if k == "1":
                        wait("act", n, i, "attr_copied")
                    else:
                        wait("dve", n, i, "h_gated1")
                    x = e["attr_t"] if k == "1" else e["h"]
                    for j in range(J):
                        ins = pe.matmul(banks[2 * n + 1][0:P, 256 + j * 64:320 + j * 64],
                                        x[0:64, n, j * P:(j + 1) * P], w["rw" + k][:, :], start=True, stop=True)
                    one(ins, n)
                return step

            def turn_h(k):
                def step(n, i):
                    wait("dve", n, i, "h_normed" + k)
                    if k == "2":
                        wait("act", n, i, "dst_copied")
                    for j in range(J):
                        ins = pe.transpose(banks[2 * n + 1][0:64, j * P:(j + 1) * P], hn[:, n, j, :], ident)
                    one(ins, n)
                return step

            def turn_rows(side, x):
                def step(n, i):
                    if side == "dst":
                        wait("act", n, i, "src_copied")
                    else:
                        wait("dve", n, i, "normed")
                    for j in range(J):
                        pe.transpose(banks[2 * n][0:S, j * P:(j + 1) * P], x[:, n, j, 0:S], ident)
                        ins = pe.transpose(banks[2 * n][0:V, W + j * P:W + (j + 1) * P], x[:, n, j, S:F], ident)
                    one(ins, n)
                return step

            def turn_vec(n, i):
                wait("act", n, i, "h_activated2")
                for j in range(J):
                    ins = pe.transpose(banks[2 * n + 1][0:3, j * P:(j + 1) * P], r[:, n, 0, j, :], ident)
                one(ins, n)

            def spread_vec(n, i):
                wait("act", n, i, "vec_copied")
                one(pe.matmul(banks[2 * n + 1][0:V, W:2 * W], w["spread"][:, :], r_t[:, n, :],
                              start=True, stop=True), n)

            def linear(n, i):
                wait("act", n, i, "spread_copied")
                a = banks[2 * n]
                pe.matmul(a[:, 0:W], w["src_s"][:, :], e["s_t"][:, n, :], start=True, stop=False)
                pe.matmul(a[:, 0:W], w["dst_s"][:, :], e["ds_t"][:, n, :], start=False, stop=True)
                pe.matmul(a[0:V, W:2 * W], w["src_v"][:, :], e["v_t"][:, n, :], start=True, stop=False)
                one(pe.matmul(a[0:V, W:2 * W], w["dst_v"][:, :], e["dv_t"][:, n, :], start=False, stop=True), n)

            def weights(n, i):
                wait("act", n, i, "linear_copied")
                wait("dve", n, i, "h_gated2")
                a, b, h = banks[2 * n], banks[2 * n + 1], e["h2"][0:64, n, :]
                pe.matmul(a[:, 0:W], w["rw3"][:, 0:128], h, start=True, stop=True)
                pe.matmul(a[0:V, W:2 * W], w["rw3"][:, 128:128 + V], h, start=True, stop=True)
                pe.matmul(b[0:V, 0:W], w["rw3"][:, 128 + V:128 + 2 * V], h, start=True, stop=True)
                one(pe.matmul(b[0:V, W:2 * W], w["rw3"][:, 128 + 2 * V:128 + 3 * V], h, start=True, stop=True), n)

            def outputs(n, i):
                wait("dve", n, i, "product4")
                for j in range(J):
                    c, bank = slice(j * P, (j + 1) * P), banks[2 * n + j]
                    pe.matmul(bank[0:P, 0:160], e["p01"][:, n, c], w["lin_a"][:, :], start=True, stop=True)
                    pe.matmul(bank[0:P, 0:128], e["p3"][:, n, c], w["lin_4"][:, :], start=False, stop=True,
                              skip_group_check=True)
                    pe.matmul(bank[0:P, 160:256], e["p2"][:, n, c], w["lin_3"][:, :], start=True, stop=True)
                    ins = pe.matmul(bank[0:P, 256:352], p5[:, n, c], w["lin_5"][:, :], start=True, stop=True)
                one(ins, n)

            run_rounds(pe, rounds, order, part, dict(
                **keep_busy(pe, banks, w, fill),
                turn_attr=turn_attr, hidden1=hidden("1"), hidden2=hidden("2"), turn_h1=turn_h("1"),
                turn_h2=turn_h("2"), turn_src=turn_rows("src", e["xs"]), turn_dst=turn_rows("dst", e["xd"]),
                turn_vec=turn_vec, spread_vec=spread_vec, linear=linear, weights=weights, outputs=outputs))


def attention_softmax(nc, sem, sb, banks, inp, w, logits, probs, edges):
    C = edges // P
    BIG = 1e30
    loaded = sem("softmax_loaded")
    vec = sem("softmax_vector_steps")
    tri_made = sem("softmax_triangles_made")
    turned = sem("softmax_ends_turned")
    exped = sem("softmax_exp_done")
    stored = sem("softmax_stored")
    spread_made = sem("softmax_ends_spread")
    lg = sb("sm_logits", [P, C, HEADS])
    m = [[sb(f"sm_max{k}{x}", [P, C, HEADS]) for x in range(2)] for k in range(2)]
    cand = sb("sm_candidates", [P, C, HEADS])
    d_i = sb("sm_dst_i", [P, C], I32)
    d = sb("sm_dst", [P, C])
    off = sb("sm_off", [P, C])
    tri = sb("sm_triangles", [P, 2, P])
    ends = sb("sm_ends", [P, 2, 1 + HEADS, P])
    ends_t = sb("sm_ends_t", [P, 2, 1 + HEADS, P])
    far = sb("sm_far", [P, 2, P])
    cross = sb("sm_cross", [P, 2, HEADS])

    with nc.Block() as block:
        @block.sync
        def _(sp):
            sp.dma_start(lg[:, :, :], logits.rearrange("(p c) h -> p c h", p=P)).then_inc(loaded, 16)
            sp.dma_start(d_i[:, :], inp["dst"].rearrange("(p c) -> p c", p=P)).then_inc(loaded, 16)
            sp.wait_ge(exped, 1)
            sp.dma_start(probs.rearrange("(p c) h -> p c h", p=P), lg[:, :, :]).then_inc(stored, 16)
            sp.wait_ge(stored, 16)

        @block.gpsimd
        def _(p):
            p.memset(tri[:, :, :], 1.0).then_inc(tri_made, 1)
            p.wait_ge(tri_made, 1)
            p.affine_select(out=tri[:, 0, :], in_=tri[:, 0, :], compare_op=ALU.is_gt, fill=0.0, base=0,
                            pattern=[[-1, P]], channel_multiplier=1)
            p.affine_select(out=tri[:, 1, :], in_=tri[:, 1, :], compare_op=ALU.is_gt, fill=0.0, base=0,
                            pattern=[[1, P]], channel_multiplier=-1).then_inc(tri_made, 1)

        @block.vector
        def _(v):
            count = 0

            def then(ins):
                nonlocal count
                count += 1
                ins.then_inc(vec, 1)
                v.wait_ge(vec, count)

            v.wait_ge(loaded, 32)
            v.tensor_copy(d[:, :], d_i[:, :])
            v.tensor_copy(m[0][0][:, :, :], lg[:, :, :])
            then(v.tensor_copy(m[1][0][:, :, :], lg[:, :, :]))
            step, at = 1, 0
            while step < C:
                n = C - step
                then(v.tensor_tensor(off[:, 0:n], d[:, step:C], d[:, 0:n], ALU.is_equal))
                then(v.tensor_scalar(off[:, 0:n], off[:, 0:n], BIG, -BIG, ALU.mult, ALU.add))
                away = off[:, 0:n].unsqueeze(2).broadcast_to([P, n, HEADS])
                f, b = m[0][at], m[1][at]
                f2, b2 = m[0][1 - at], m[1][1 - at]
                then(v.tensor_tensor(cand[:, 0:n, :], f[:, 0:n, :], away, ALU.add))
                v.tensor_tensor(f2[:, step:C, :], f[:, step:C, :], cand[:, 0:n, :], ALU.max)
                then(v.tensor_copy(f2[:, 0:step, :], f[:, 0:step, :]))
                then(v.tensor_tensor(cand[:, 0:n, :], b[:, step:C, :], away, ALU.add))
                v.tensor_tensor(b2[:, 0:n, :], b[:, 0:n, :], cand[:, 0:n, :], ALU.max)
                then(v.tensor_copy(b2[:, n:C, :], b[:, n:C, :]))
                step, at = 2 * step, 1 - at
            fwd, bwd = m[0][at], m[1][at]
            for k, (x, c) in enumerate(((fwd, C - 1), (bwd, 0))):
                v.tensor_copy(ends[:, k, 0, :], d[:, c:c + 1].broadcast_to([P, P]))
                ins = v.tensor_copy(ends[:, k, 1:1 + HEADS, :], x[:, c, :].unsqueeze(2).broadcast_to([P, HEADS, P]))
            ins.then_inc(spread_made, 1)
            v.wait_ge(turned, 1)
            for k in range(2):
                for q in range(3):
                    ins = v.tensor_copy(ends_t[:, k, 3 * q:3 * q + 3, :].rearrange("p h c -> p (h c)"),
                                        banks[3 * k + q][0:P, 0:3 * P])
            then(ins)
            v.wait_ge(tri_made, 2)
            for k, c in enumerate((0, C - 1)):
                then(v.scalar_tensor_tensor(far[:, k, :], ends_t[:, k, 0, :], d[:, c:c + 1], tri[:, k, :],
                                            ALU.is_equal, ALU.mult))
                then(v.tensor_scalar(far[:, k, :], far[:, k, :], BIG, -BIG, ALU.mult, ALU.add))
                then(v.tensor_tensor(ends_t[:, k, 1:1 + HEADS, :], ends_t[:, k, 1:1 + HEADS, :],
                                     far[:, k, :].unsqueeze(1).broadcast_to([P, HEADS, P]), ALU.add))
                then(v.tensor_reduce(cross[:, k, :], ends_t[:, k, 1:1 + HEADS, :], AX.X, ALU.max))
            then(v.tensor_tensor(fwd[:, :, :], fwd[:, :, :], bwd[:, :, :], ALU.max))
            for k, c in enumerate((0, C - 1)):
                then(v.tensor_scalar(off[:, :], d[:, :], d[:, c:c + 1], BIG, ALU.is_equal, ALU.mult))
                then(v.tensor_scalar(off[:, :], off[:, :], -BIG, None, ALU.add))
                then(v.tensor_tensor(cand[:, :, :], off[:, :].unsqueeze(2).broadcast_to([P, C, HEADS]),
                                     cross[:, k, :].unsqueeze(1).broadcast_to([P, C, HEADS]), ALU.add))
                then(v.tensor_tensor(fwd[:, :, :], fwd[:, :, :], cand[:, :, :], ALU.max))
            then(v.tensor_tensor(lg[:, :, :], lg[:, :, :], fwd[:, :, :], ALU.subtract))
            v.tensor_copy(off[:, 0:1], d[:, 0:1]).then_inc(spread_made, 1)

        @block.tensor
        def _(pe):
            pe.wait_ge(spread_made, 1)
            for k in range(2):
                for h in range(1 + HEADS):
                    ins = pe.transpose(banks[3 * k + h // 3][0:P, (h % 3) * P:(h % 3 + 1) * P], ends[:, k, h, :],
                                       w["ident"][0:P, 0:P])
            ins.then_inc(turned, 1)

        @block.scalar
        def _(act):
            act.wait_ge(spread_made, 2)
            act.activation(lg[:, :, :], lg[:, :, :], ACT.Exp).then_inc(exped, 1)


def attention_nodes(nc, sem, sb, banks, inp, w, e, ffn, index, kept, probs, out, nodes, edges):
    T = LANES * J
    rounds = edges // ROWS
    M = F + HEADS
    kept_view = kept.rearrange("(t p) f -> p t f", p=P)
    probs_view = probs.rearrange("(t p) h -> p t h", p=P)
    t = lane_steps(sem, "dest",
              pe=["summed", "turned", "projected"] + FFN_PE,
              act=["sums_copied", "turned_copied"] + FFN_ACT,
              dve=["masked", "weighted", "denominator", "inverse", "divided", "with_bias", "x", "doubled"] + FFN_DVE,
              pool=FFN_POOL)
    rows_loaded, scattered = sem("dest_rows_loaded"), sem("dest_rows_scattered")
    index_copied, ready = sem("dest_index_copied"), sem("dest_sums_cleared")
    rows = sb("dest_rows", [P, T, KEPT])
    p_row = sb("dest_probs", [P, T, HEADS])
    inverse = sb("dest_inverse", [P, LANES, J, HEADS])
    mean = sb("dest_mean", [P, LANES, J, F])
    base = sb("dest_base", [P, LANES, J, F])
    xp = sb("dest_xp", [P, LANES, J, F])
    u = sb("dest_u", [P, LANES, J, F])
    res = sb("dest_res", [P, LANES, J, F])

    with nc.Block() as block:
        @block.sync
        def _(sp):
            with sp.Fori(0, rounds) as i:
                for n in range(LANES):
                    sp.wait_ge(t["dve"][n], count_at(t, i, "dve", "ffn_added"))
                    gate(sp, t)
                sp.dma_start(rows[:, :, :], kept_view[:, bass.ds(i * T, T), :]).then_inc(rows_loaded, 16)
                sp.dma_start(p_row[:, :, :], probs_view[:, bass.ds(i * T, T), :]).then_inc(rows_loaded, 16)
                sp.dma_start(e["dst_row"][:, :, :].rearrange("p n c -> p (n c)"),
                             inp["dst"][bass.ds(i * ROWS, ROWS)].unsqueeze(0).broadcast_to([P, ROWS])
                             ).then_inc(rows_loaded, 16)

        @block.gpsimd
        def _(p):
            prime(p, t, "pool")
            p.dma_start(e["first"][:, 0:1], inp["node_vec1"][0:P, :]).then_inc(scattered, 16)
            with p.Fori(0, rounds) as i:
                for n in range(LANES):
                    p.wait_ge(t["dve"][n], count_at(t, i, "dve", "masked"))
                    gate(p, t)
                p.wait_ge(scattered, 16 * T * i + 16)
                gate(p, t)
                p.tensor_copy(e["into_now"][:, :], index["into_i"][:, bass.ds(i * T, T)])
                p.tensor_copy(e["key_now"][:, 0, :], index["dst_f"][:, bass.ds(i * T, T)])
                p.tensor_copy(e["key_now"][:, 1, :], index["before"][:, bass.ds(i * T, T)]).then_inc(index_copied, 1)
                p.wait_ge(index_copied, i + 1)
                gate(p, t)
                for n in range(LANES):
                    ffn_roots(p, ffn, t, i + 1, n)
                for n in range(LANES):
                    ffn_out_roots(p, ffn, t, i + 1, n)
                for n in range(LANES):
                    p.wait_ge(t["dve"][n], count_at(t, i + 1, "dve", "out_normed"))
                    gate(p, t)
                    for j in range(J):
                        k = J * n + j
                        p.indirect_dma_start(out, bass.IndirectOffsetOnAxis(ap=e["into_now"][:, k:k + 1], axis=0),
                                             res[:, n, j, :], None, bounds_check=nodes - 1, oob_is_err=False
                                             ).then_inc(scattered, 16)
            p.wait_ge(scattered, 16 * T * rounds + 16)

        @block.vector
        def _(v):
            v.memset(ffn["hid_v2"][S:S + 1, :, :], 1.0)
            v.memset(e["sums"][:, :, :, :], 0.0).then_inc(ready, 1)
            prime(v, t, "dve")

            def one(ins, n):
                ins.then_inc(t["dve"][n], 1)

            def after(i, n, step):
                v.wait_ge(t["dve"][n], count_at(t, i + 1, "dve", step))

            with v.Fori(0, rounds) as i:
                v.wait_ge(index_copied, i + 1)
                v.wait_ge(rows_loaded, 48 * i + 48)
                for n in range(LANES):
                    masks(v, t, e, i + 1, n)
                    for j in range(J):
                        k = J * n + j
                        p = p_row[:, k, :].unsqueeze(2)
                        v.tensor_tensor(e["msg"][:, n, j, 0:S].rearrange("p (h k) -> p h k", h=HEADS),
                                        rows[:, k, VALS:VALS + S].rearrange("p (h k) -> p h k", h=HEADS),
                                        p.broadcast_to([P, HEADS, 8]), ALU.mult)
                        v.tensor_tensor(e["msg"][:, n, j, S:F].rearrange("p (h k) -> p h k", h=HEADS),
                                        rows[:, k, VALS + S:VALS + F].rearrange("p (h k) -> p h k", h=HEADS),
                                        p.broadcast_to([P, HEADS, 12]), ALU.mult)
                        ins = v.tensor_copy(e["msg"][:, n, j, F:M], p_row[:, k, :])
                    one(ins, n)
                for n in range(LANES):
                    v.wait_ge(t["act"][n], count_at(t, i + 1, "act", "sums_copied"))
                    one(v.tensor_scalar(inverse[:, n, :, :], e["sums"][:, n, :, F:M], 1e-12, None, ALU.add), n)
                    after(i, n, "denominator")
                    one(v.reciprocal(inverse[:, n, :, :], inverse[:, n, :, :]), n)
                    after(i, n, "inverse")
                    for j in range(J):
                        q = inverse[:, n, j, :].unsqueeze(2)
                        for at, width in ((0, 8), (S, 12)):
                            o = slice(at, at + HEADS * width)
                            ins = v.tensor_tensor(mean[:, n, j, o].rearrange("p (h k) -> p h k", h=HEADS),
                                                  e["sums"][:, n, j, o].rearrange("p (h k) -> p h k", h=HEADS),
                                                  q.broadcast_to([P, HEADS, width]), ALU.mult)
                    one(ins, n)
                for n in range(LANES):
                    x3 = rows[:, J * n:J * n + J, X3:X3 + F]
                    v.tensor_copy(base[:, n, :, S:F], x3[:, :, S:F])
                    one(v.tensor_tensor(base[:, n, :, 0:S], x3[:, :, 0:S],
                                        w["proj_b"][:, :].unsqueeze(1).broadcast_to([P, J, S]), ALU.add), n)
                    after(i, n, "with_bias")
                    v.wait_ge(t["pe"][n], count_at(t, i + 1, "pe", "projected"))
                    one(v.tensor_tensor(xp[:, n, :, :],
                                        banks[2 * n + 1][0:P, 0:J * F].rearrange("p (j f) -> p j f", j=J),
                                        base[:, n, :, :], ALU.add), n)
                    after(i, n, "x")
                    one(v.tensor_tensor(u[:, n, :, :], xp[:, n, :, :], x3, ALU.add), n)
                    ffn_measure(v, ffn, t, i + 1, n, [xp[:, n, j, 0:S] for j in range(J)],
                                [xp[:, n, j, S:F] for j in range(J)])
                    ffn_merge(v, ffn, t, i + 1, n)
                    ffn_square(v, ffn, t, i + 1, n)
                    ffn_widen(v, ffn, t, i + 1, n)
                for n in range(LANES):
                    ffn_root_attr(v, ffn, t, i + 1, n,
                                  rows[:, J * n:J * n + J, ATTR:ATTR + 1].rearrange("p j o -> p (j o)"))
                    ffn_normalize(v, ffn, t, i + 1, n, [xp[:, n, j, 0:S] for j in range(J)])
                for n in range(LANES):
                    ffn_gates(v, ffn, t, i + 1, n)
                for n in range(LANES):
                    ffn_add(v, ffn, t, i + 1, n, lambda j: rows[:, J * n + j, ATTR:ATTR + 1],
                            [u[:, n, j, :] for j in range(J)])
                    out_measure(v, ffn, t, i + 1, n)
                    out_merge(v, ffn, t, i + 1, n)
                    out_widen(v, ffn, t, i + 1, n)
                for n in range(LANES):
                    v.wait_ge(scattered, 16 * T * i + 16)
                    ffn_finish(v, ffn, t, i + 1, n, [res[:, n, j, :] for j in range(J)])

        @block.scalar
        def _(act):
            prime(act, t, "act")
            with act.Fori(0, rounds) as i:
                for n in range(LANES):
                    act.wait_ge(t["pe"][n], count_at(t, i + 1, "pe", "summed"))
                    for j in range(J):
                        ins = act.activation(e["sums"][:, n, j, 0:M], banks[2 * n + j][0:P, 0:M], ACT.Copy)
                    ins.then_inc(t["act"][n], 1)
                for n in range(LANES):
                    act.wait_ge(t["pe"][n], count_at(t, i + 1, "pe", "turned"))
                    act.activation(e["s_t"][:, n, :], banks[2 * n][0:S, 0:W], ACT.Copy)
                    act.activation(e["v_t"][:, n, :], banks[2 * n][0:V, W:2 * W], ACT.Copy
                                   ).then_inc(t["act"][n], 1)
                for n in range(LANES):
                    ffn_scale(act, ffn, t, i + 1, n, [xp[:, n, j, S:F] for j in range(J)],
                              rows[:, J * n:J * n + J, ATTR:ATTR + 1].rearrange("p j o -> p (j o)"))
                for n in range(LANES):
                    ffn_copy_turned(act, ffn, t, i + 1, n)
                for n in range(LANES):
                    ffn_sigmoid(act, ffn, t, i + 1, n)

        @block.tensor
        def _(pe):
            prime(pe, t, "pe")
            ident = w["ident"][0:P, 0:P]
            pe.wait_ge(ready, 1)
            with pe.Fori(0, rounds) as i:
                for n in range(LANES):
                    pe.wait_ge(t["dve"][n], count_at(t, i, "dve", "ffn_added"))
                    gate(pe, t)
                    pe.wait_ge(t["dve"][n], count_at(t, i + 1, "dve", "weighted"))
                    gate(pe, t)
                    pe.wait_ge(t["act"][n - 1], count_at(t, i + 1 if n else i, "act", "sums_copied"))
                    gate(pe, t)
                    run_sums(pe, e, banks, n, M).then_inc(t["pe"][n], 1)
                for n in range(LANES):
                    pe.wait_ge(t["dve"][n], count_at(t, i + 1, "dve", "divided"))
                    gate(pe, t)
                    for j in range(J):
                        pe.transpose(banks[2 * n][0:S, j * P:(j + 1) * P], mean[:, n, j, 0:S], ident)
                        ins = pe.transpose(banks[2 * n][0:V, W + j * P:W + (j + 1) * P], mean[:, n, j, S:F], ident)
                    ins.then_inc(t["pe"][n], 1)
                for n in range(LANES):
                    pe.wait_ge(t["act"][n], count_at(t, i + 1, "act", "turned_copied"))
                    gate(pe, t)
                    for j in range(J):
                        c, o = slice(j * P, (j + 1) * P), j * F
                        pe.matmul(banks[2 * n + 1][0:P, o:o + S], e["s_t"][:, n, c], w["proj_s"][:, :],
                                  start=True, stop=True)
                        ins = pe.matmul(banks[2 * n + 1][0:P, o + S:o + F], e["v_t"][:, n, c], w["proj_v"][:, :],
                                        start=True, stop=True)
                    ins.then_inc(t["pe"][n], 1)
                for n in range(LANES):
                    ffn_turn(pe, ffn, t, i + 1, n)
                for n in range(LANES):
                    ffn_hidden(pe, ffn, t, i + 1, n)
                for n in range(LANES):
                    ffn_out(pe, ffn, t, i + 1, n)


def semaphores(nc):
    taken = []

    def sem(name):
        taken.append(nc.alloc_semaphore(name=name))
        return taken[-1]

    def free():
        nc.clear_and_free_semaphores(taken)
        nc.all_engine_barrier()

    return sem, free


def program(nc, inp, out, nodes, edges, layers=4):
    tables = [nc.dram_tensor(f"table{l}", (nodes, ROW), F32).ap() for l in range(4)]
    kept = nc.dram_tensor("kept", (edges, KEPT), F32).ap()
    logits = nc.dram_tensor("logits", (edges, HEADS), F32).ap()
    probs = nc.dram_tensor("probs", (edges, HEADS), F32).ap()
    with ExitStack() as ctx:
        def place(scope, prefix=""):
            return lambda name, shape, dtype=F32: scope.enter_context(nc.sbuf_tensor(prefix + name, shape, dtype))

        banks = [ctx.enter_context(nc.psum_tensor(f"bank{n}", [128, 512], F32)) for n in range(8)]
        w = {}
        keep = place(ctx)
        with ExitStack() as phase:
            sem, free = semaphores(nc)
            prepare_weights(nc, sem, keep, place(phase), banks, inp, w)
            free()
        with ExitStack() as phase:
            sem, free = semaphores(nc)
            all_nodes(nc, sem, place(phase), banks, inp, w, ffn_buffers(place(phase), w, banks), tables, out, nodes)
            free()
        with ExitStack() as phase:
            sem, free = semaphores(nc)
            index = edge_index(nc, sem, keep, place(phase), banks, inp, w, nodes, edges)
            free()
        with ExitStack() as phase:
            e = edge_buffers(place(phase))
            for l in range(min(layers, 3)):
                with ExitStack() as layer:
                    sem, free = semaphores(nc)
                    edges_layer(nc, sem, place(layer), banks, inp, w, e, index, tables, l, nodes, edges)
                    free()
        if layers < 4:
            return
        with ExitStack() as phase:
            sem, free = semaphores(nc)
            attention_weights(nc, sem, keep, place(phase), banks, inp, w)
            free()
        with ExitStack() as phase:
            sem, free = semaphores(nc)
            attention_edges(nc, sem, place(phase), banks, inp, w, edge_buffers(place(phase, "att_")), index,
                            tables[3], kept, logits, edges)
            free()
        with ExitStack() as phase:
            sem, free = semaphores(nc)
            attention_softmax(nc, sem, place(phase), banks, inp, w, logits, probs, edges)
            free()
        with ExitStack() as phase:
            sem, free = semaphores(nc)
            attention_nodes(nc, sem, place(phase), banks, inp, w, edge_buffers(place(phase, "dest_")),
                            ffn_buffers(place(phase, "dest_"), w, banks), index, kept, probs, out, nodes, edges)
            free()


def kernel(**inputs):
    import concourse.bacc as bacc
    from concourse.bass_utils import run_bass_kernel_spmd

    nc = bacc.Bacc("TRN2", target_bir_lowering=False, num_devices=1)
    arrays = {name: np.ascontiguousarray(a) for name, a in inputs.items()}
    inp = {name: nc.dram_tensor(name, a.shape, mybir.dt.from_np(a.dtype), kind="ExternalInput").ap()
           for name, a in arrays.items()}
    nodes, edges = arrays["x"].shape[0], arrays["src"].shape[0]
    out = nc.dram_tensor("out", (nodes, F), F32, kind="ExternalOutput").ap()
    program(nc, inp, out, nodes, edges)
    return run_bass_kernel_spmd(nc, [arrays], core_ids=[0]).results[0]["out"]
```
